# Optimizing a Trainium2 kernel written in Bass

```python
import numpy as np
import jax
import jax.numpy as jnp

def _softmax(x, axis=-1):
    return jax.nn.softmax(x, axis=axis)

def _gelu(x):
    return jax.nn.gelu(x, approximate=True)

def _silu(x):
    return jax.nn.silu(x)

def _sigmoid(x):
    return jax.nn.sigmoid(x)

def _layernorm(x, axis=-1, eps=1e-05):
    m = jnp.mean(x, axis=axis, keepdims=True)
    v = jnp.var(x, axis=axis, keepdims=True)
    return (x - m) / jnp.sqrt(v + eps)

def _scatter_add(tgt, idx, src, axis=0):
    return tgt.at[idx].add(src)

def _segment_sum(src, seg, n):
    return jax.ops.segment_sum(src, seg, n)
kernel_name = 'mk_gnn_resnorm_d4_gnn_r32_5fd1a9'

def setup_inputs(seed: int=0):
    np.random.seed(seed)
    _w = jnp.asarray

    def _rec_inputs():
        import jax
        import jax.numpy as jnp
        _gk = jax.random.key(seed)
        x = -0.0005121 + 1.001 * jax.random.normal(jax.random.fold_in(_gk, 1), (3125, 64), jnp.float32)
        _s = jax.random.randint(jax.random.fold_in(_gk, 2), (25000,), 0, 3125, jnp.int32)
        _d = jax.random.randint(jax.random.fold_in(_gk, 3), (25000,), 0, 3125, jnp.int32)
        _loop = jnp.arange(3125, dtype=jnp.int32)
        src = jnp.concatenate([_s, _d, _loop])
        dst = jnp.concatenate([_d, _s, _loop])
        _o = jnp.argsort(dst, stable=True)
        src = src[_o]
        dst = dst[_o]
        edge_attr_8 = 0.000398945 + 1.00003 * jax.random.normal(jax.random.fold_in(_gk, 12), (53125, 8), jnp.float32)
        edge_type_16 = jax.random.randint(jax.random.fold_in(_gk, 14), (53125,), 0, 16, jnp.int32)
        edge_type_9 = jax.random.randint(jax.random.fold_in(_gk, 15), (53125,), 0, 9, jnp.int32)
        return (x, src, dst, edge_attr_8, edge_type_16, edge_type_9)
    x, src, dst, edge_attr_8, edge_type_16, edge_type_9 = _rec_inputs()

    def _L0_gnn_setup():
        import jax, jax.numpy as jnp
        import numpy as np
        N_NODES = 50000
        E_EDGES = 25000
        IN_F = 64
        OUT_F = 64
        EDGE_F = 8
        key = jax.random.key(seed)
        ks = jax.random.split(key, 6)
        x = jax.random.normal(ks[0], (N_NODES, IN_F), dtype=jnp.float32)
        edge_index = jax.random.randint(ks[1], (2, E_EDGES), 0, N_NODES, dtype=jnp.int64)
        edge_attr = jax.random.normal(ks[2], (E_EDGES, EDGE_F), dtype=jnp.float32)
        fan_in1 = 2 * IN_F + EDGE_F
        W1 = jax.random.normal(ks[3], (fan_in1, OUT_F), dtype=jnp.float32) / np.sqrt(fan_in1)
        b1 = jnp.zeros((OUT_F,), dtype=jnp.float32)
        W2 = jax.random.normal(ks[4], (OUT_F, OUT_F), dtype=jnp.float32) / np.sqrt(OUT_F)
        b2 = jnp.zeros((OUT_F,), dtype=jnp.float32)
        return {'x': x, 'edge_index': edge_index, 'edge_attr': edge_attr, 'W1': W1, 'b1': b1, 'W2': W2, 'b2': b2}
    _L0_gnn_all = _L0_gnn_setup()
    _L0_gnn_in = {k: v for k, v in _L0_gnn_all.items() if k in ('W1', 'b1', 'W2', 'b2')}
    del _L0_gnn_all

    def _L1_gnn_setup():
        import jax, jax.numpy as jnp
        import numpy as np
        N_NODES = 3125
        HIDDEN = 64
        N_REL = 9
        N_LAYERS = 3
        N_EDGES = 31250
        key = jax.random.key(seed)
        k1, k2, k3, k4, k5 = jax.random.split(key, 5)
        edge_index = jax.random.randint(k1, (2, N_EDGES), 0, N_NODES, dtype=jnp.int64)
        edge_type = jax.random.randint(k2, (N_EDGES,), 0, N_REL, dtype=jnp.int64)
        embeddings = jax.random.uniform(k3, (N_NODES, HIDDEN), dtype=jnp.float32)
        weights = jax.random.uniform(k4, (N_LAYERS, 2 * N_REL, HIDDEN, HIDDEN), dtype=jnp.float32)
        biases = jax.random.uniform(k5, (N_LAYERS, 2 * N_REL, HIDDEN), dtype=jnp.float32)
        return {'edge_index': edge_index, 'edge_type': edge_type, 'embeddings': embeddings, 'weights': weights, 'biases': biases}
    _L1_gnn_all = _L1_gnn_setup()
    _L1_gnn_in = {k: v for k, v in _L1_gnn_all.items() if k in ('weights', 'biases')}
    del _L1_gnn_all

    def _L2_gnn_setup():
        import jax, jax.numpy as jnp
        import numpy as np
        N_NODES = 3125
        N_EDGES = 50000
        IN_FEAT = 64
        OUT_FEAT = 64
        NUM_RELS = 16
        key = jax.random.key(seed)
        k1, k2, k3, k4, k5 = jax.random.split(key, 5)
        feat = jax.random.normal(k1, (N_NODES, IN_FEAT), dtype=jnp.float32)
        weight = jax.random.normal(k2, (NUM_RELS, IN_FEAT, OUT_FEAT), dtype=jnp.float32)
        src = jax.random.randint(k3, (N_EDGES,), 0, N_NODES, dtype=jnp.int32)
        dst = jax.random.randint(k4, (N_EDGES,), 0, N_NODES, dtype=jnp.int32)
        etypes = jax.random.randint(k5, (N_EDGES,), 0, NUM_RELS, dtype=jnp.int32)
        return {'feat': feat, 'weight': weight, 'src': src, 'dst': dst, 'etypes': etypes}
    _L2_gnn_all = _L2_gnn_setup()
    _L2_gnn_in = {k: v for k, v in _L2_gnn_all.items() if k in ('weight',)}
    del _L2_gnn_all

    def _L3_gnn_setup():
        import jax, jax.numpy as jnp
        import numpy as np
        N_NODES = 50000
        N_EDGES = 25000
        D = 64
        NEG_SLOPE = 0.2

        def _gat_conv(x, src, dst, W, a_src, a_dst, b, n_nodes):
            h = x @ W
            alpha_s = h @ a_src
            alpha_d = h @ a_dst
            e = alpha_s[src] + alpha_d[dst]
            e = jnp.where(e > 0, e, NEG_SLOPE * e)
            m = jax.ops.segment_max(e, dst, num_segments=n_nodes)
            m = jnp.where(jnp.isfinite(m), m, 0.0)
            ex = jnp.exp(e - m[dst])
            s = jax.ops.segment_sum(ex, dst, num_segments=n_nodes)
            alpha = ex / (s[dst] + 1e-16)
            out = jax.ops.segment_sum(alpha[:, None] * h[src], dst, num_segments=n_nodes)
            return out + b

        def _add_self_loops(edge_index, n_nodes):
            loop = jnp.arange(n_nodes, dtype=edge_index.dtype)
            src = jnp.concatenate([edge_index[0], loop])
            dst = jnp.concatenate([edge_index[1], loop])
            return (src, dst)
        key = jax.random.key(seed)
        ks = jax.random.split(key, 16)
        x = jax.random.normal(ks[0], (N_NODES, D), dtype=jnp.float32)
        edge_index = jax.random.randint(ks[1], (2, N_EDGES), 0, N_NODES, dtype=jnp.int32)
        sc = 1.0 / np.sqrt(D)

        def lin(k):
            return jax.random.uniform(k, (D, D), jnp.float32, -sc, sc)

        def att(k):
            return jax.random.uniform(k, (D,), jnp.float32, -sc, sc)
        return {'x': x, 'edge_index': edge_index, 'W1': lin(ks[2]), 'a1s': att(ks[3]), 'a1d': att(ks[4]), 'b1': jnp.zeros((D,), jnp.float32), 'W2': lin(ks[5]), 'a2s': att(ks[6]), 'a2d': att(ks[7]), 'b2': jnp.zeros((D,), jnp.float32), 'W3': lin(ks[8]), 'a3s': att(ks[9]), 'a3d': att(ks[10]), 'b3': jnp.zeros((D,), jnp.float32)}
    _L3_gnn_all = _L3_gnn_setup()
    _L3_gnn_in = {k: v for k, v in _L3_gnn_all.items() if k in ('W1', 'a1s', 'a1d', 'b1', 'W2', 'a2s', 'a2d', 'b2', 'W3', 'a3s', 'a3d', 'b3')}
    del _L3_gnn_all
    return {'x': x, 'src': src, 'dst': dst, 'edge_attr_8': edge_attr_8, 'edge_type_16': edge_type_16, 'edge_type_9': edge_type_9, 'L0_gnn_W1': _L0_gnn_in['W1'], 'L0_gnn_b1': _L0_gnn_in['b1'], 'L0_gnn_W2': _L0_gnn_in['W2'], 'L0_gnn_b2': _L0_gnn_in['b2'], 'L1_gnn_weights': _L1_gnn_in['weights'], 'L1_gnn_biases': _L1_gnn_in['biases'], 'L2_gnn_weight': _L2_gnn_in['weight'], 'L3_gnn_W1': _L3_gnn_in['W1'], 'L3_gnn_a1s': _L3_gnn_in['a1s'], 'L3_gnn_a1d': _L3_gnn_in['a1d'], 'L3_gnn_b1': _L3_gnn_in['b1'], 'L3_gnn_W2': _L3_gnn_in['W2'], 'L3_gnn_a2s': _L3_gnn_in['a2s'], 'L3_gnn_a2d': _L3_gnn_in['a2d'], 'L3_gnn_b2': _L3_gnn_in['b2'], 'L3_gnn_W3': _L3_gnn_in['W3'], 'L3_gnn_a3s': _L3_gnn_in['a3s'], 'L3_gnn_a3d': _L3_gnn_in['a3d'], 'L3_gnn_b3': _L3_gnn_in['b3']}

def reference(x, src, dst, edge_attr_8, edge_type_16, edge_type_9, L0_gnn_W1, L0_gnn_b1, L0_gnn_W2, L0_gnn_b2, L1_gnn_weights, L1_gnn_biases, L2_gnn_weight, L3_gnn_W1, L3_gnn_a1s, L3_gnn_a1d, L3_gnn_b1, L3_gnn_W2, L3_gnn_a2s, L3_gnn_a2d, L3_gnn_b2, L3_gnn_W3, L3_gnn_a3s, L3_gnn_a3d, L3_gnn_b3):
    import jax
    import jax.numpy as jnp

    def _L0_gnn_ref(x, edge_index, edge_attr, W1, b1, W2, b2):
        import jax, jax.numpy as jnp
        import numpy as np
        N_NODES = 50000
        E_EDGES = 25000
        IN_F = 64
        OUT_F = 64
        EDGE_F = 8
        src, dst = (edge_index[0], edge_index[1])
        msg_input = jnp.concatenate([x[src], x[dst], edge_attr], axis=1)
        h = jax.nn.relu(msg_input @ W1 + b1)
        msg = h @ W2 + b2
        out = jax.ops.segment_sum(msg, dst, num_segments=x.shape[0])
        return out

    def _L1_gnn_ref(edge_index, edge_type, embeddings, weights, biases):
        import jax, jax.numpy as jnp
        import numpy as np
        N_NODES = 3125
        HIDDEN = 64
        N_REL = 9
        N_LAYERS = 3
        N_EDGES = 31250
        N, E = embeddings.shape
        L = weights.shape[0]
        R = weights.shape[1] // 2
        idx0 = edge_index[0]
        idx1 = edge_index[1]
        rel0 = edge_type
        rel1 = edge_type + R
        output = embeddings
        for l in range(L):
            T = jnp.einsum('ne,reo->rno', embeddings, weights[l])
            m0 = T[rel0, idx0] + biases[l][rel0]
            m1 = T[rel1, idx1] + biases[l][rel1]
            m = jnp.concatenate([m0, m1], axis=0)
            d = jnp.concatenate([idx0, idx1], axis=0)
            s = jax.ops.segment_sum(m, d, num_segments=N)
            cnt = jax.ops.segment_sum(jnp.ones((d.shape[0],), m.dtype), d, num_segments=N)
            hidden = jnp.where(cnt[:, None] > 0, s / jnp.maximum(cnt, 1.0)[:, None], 0.0)
            if l + 1 < L:
                hidden = jax.nn.relu(hidden)
            output = hidden
        return output

    def _L2_gnn_ref(feat, weight, src, dst, etypes):
        import jax, jax.numpy as jnp
        import numpy as np
        N_NODES = 3125
        N_EDGES = 50000
        IN_FEAT = 64
        OUT_FEAT = 64
        NUM_RELS = 16
        n_nodes = feat.shape[0]
        h_rel = jnp.einsum('nf,rfo->rno', feat, weight)
        msg = h_rel[etypes, src]
        out = jax.ops.segment_sum(msg, dst, num_segments=n_nodes)
        return out

    def _L3_gnn_ref(x, edge_index, W1, a1s, a1d, b1, W2, a2s, a2d, b2, W3, a3s, a3d, b3):
        import jax, jax.numpy as jnp
        import numpy as np
        N_NODES = 50000
        N_EDGES = 25000
        D = 64
        NEG_SLOPE = 0.2

        def _gat_conv(x, src, dst, W, a_src, a_dst, b, n_nodes):
            h = x @ W
            alpha_s = h @ a_src
            alpha_d = h @ a_dst
            e = alpha_s[src] + alpha_d[dst]
            e = jnp.where(e > 0, e, NEG_SLOPE * e)
            m = jax.ops.segment_max(e, dst, num_segments=n_nodes)
            m = jnp.where(jnp.isfinite(m), m, 0.0)
            ex = jnp.exp(e - m[dst])
            s = jax.ops.segment_sum(ex, dst, num_segments=n_nodes)
            alpha = ex / (s[dst] + 1e-16)
            out = jax.ops.segment_sum(alpha[:, None] * h[src], dst, num_segments=n_nodes)
            return out + b

        def _add_self_loops(edge_index, n_nodes):
            loop = jnp.arange(n_nodes, dtype=edge_index.dtype)
            src = jnp.concatenate([edge_index[0], loop])
            dst = jnp.concatenate([edge_index[1], loop])
            return (src, dst)
        n = x.shape[0]
        src, dst = _add_self_loops(edge_index, n)
        h = _gat_conv(x, src, dst, W1, a1s, a1d, b1, n)
        h = jax.nn.relu(h)
        h = _gat_conv(h, src, dst, W2, a2s, a2d, b2, n)
        h = jax.nn.relu(h)
        return _gat_conv(h, src, dst, W3, a3s, a3d, b3, n)
    edge_index = jnp.stack([src, dst])
    x = _layernorm(x + _L0_gnn_ref(x, edge_index, edge_attr_8, L0_gnn_W1, L0_gnn_b1, L0_gnn_W2, L0_gnn_b2), axis=-1)
    x = _layernorm(x + _L1_gnn_ref(edge_index, edge_type_9, x, L1_gnn_weights, L1_gnn_biases), axis=-1)
    x = _layernorm(x + _L2_gnn_ref(x, L2_gnn_weight, src, dst, edge_type_16), axis=-1)
    x = _layernorm(x + _L3_gnn_ref(x, edge_index, L3_gnn_W1, L3_gnn_a1s, L3_gnn_a1d, L3_gnn_b1, L3_gnn_W2, L3_gnn_a2s, L3_gnn_a2d, L3_gnn_b2, L3_gnn_W3, L3_gnn_a3s, L3_gnn_a3d, L3_gnn_b3), axis=-1)
    return x

_drawn_inputs = setup_inputs


def setup_inputs(seed=0):
    import zlib

    import numpy as np

    out = dict(_drawn_inputs(seed))
    spreads = {'L0_gnn_b1': (0.0, 0.1),
     'L0_gnn_b2': (0.0, 0.1),
     'L3_gnn_b1': (0.0, 0.53),
     'L3_gnn_b2': (0.0, 0.267),
     'L3_gnn_b3': (0.0, 0.1)}
    factors = {'L3_gnn_a1s': 31.091,
     'L3_gnn_a1d': 200.0,
     'L3_gnn_a2s': 64.0,
     'L3_gnn_a2d': 200.0,
     'L3_gnn_a3s': 171.417,
     'L3_gnn_a3d': 200.0}
    for name, (base, spread) in spreads.items():
        noise = np.random.default_rng([zlib.crc32(name.encode()), seed]).standard_normal(out[name].shape)
        drawn = base * np.exp(spread * noise) if base else spread * noise
        out[name] = jnp.asarray(drawn.astype(out[name].dtype))
    for name, factor in factors.items():
        out[name] = (out[name] * factor).astype(out[name].dtype)
    return out
```

```python
import concourse.bass as bass
from concourse import mybir
from contextlib import ExitStack

N, F, E, NREL, NTYPE = 3125, 64, 53125, 9, 16
P = 128
BLOCKS = -(-N // P)
NP_ = BLOCKS * P
TILES = -(-E // P)
EP = TILES * P
STEPS = TILES + BLOCKS - 1
TROW = TILES // 4
SROW = STEPS // 4
GS = 4
GROUPS = STEPS // GS
RING = 10
OUTER = GROUPS // RING
ACC0 = F + 1 + NREL
GW = F + 1
BIG = 1e30
EPS = 1e-5


def gnn_kernel(nc, x, ints, attr_t, w0_pq, w0_attr, w0_out, w1, w2, w3, w3_t, a3, b3, out):
    fp32, bf16, i32 = mybir.dt.float32, mybir.dt.bfloat16, mybir.dt.int32
    ALU, ACT, AX = mybir.AluOpType, mybir.ActivationFunctionType, mybir.AxisListType
    ds = bass.ds

    src_rows = nc.dram_tensor("src_rows", [NP_, F], fp32).ap()
    rel_rows = nc.dram_tensor("rel_rows", [NP_ * NTYPE, F], fp32).ap()
    gat_rows = [nc.dram_tensor(f"gat_rows{n}", [NP_, F], fp32).ap() for n in range(3)]
    keys = nc.dram_tensor("keys", [STEPS * P + 1, 1], fp32).ap()
    seg_max = nc.dram_tensor("seg_max", [STEPS * P + 1, 1], fp32).ap()

    ctx = ExitStack()
    with ctx:
        def sb(name, shape, dt=fp32):
            return ctx.enter_context(nc.sbuf_tensor(name, shape, dt))

        sems = {}

        def S(name):
            if name not in sems:
                sems[name] = ctx.enter_context(nc.semaphore(name))
            return sems[name]

        arena = sb("arena", [P, STEPS * P // 2])
        src_hot_T = arena[:, :].bitcast(bf16)
        at = [0]

        def carve(cols):
            a = arena[:, at[0]:at[0] + cols]
            at[0] += cols
            assert at[0] <= STEPS * P // 2
            return a

        ints_sb = carve(4 * 512).bitcast(i32)
        edge_f = carve(4 * 512)
        step_of_tile = carve(4 * STEPS)
        itmp = carve(4 * 512).bitcast(i32)
        q_parts = carve(BLOCKS * 3 * F // 2).bitcast(bf16)
        attr_ring = carve(5 * GS * P)
        w1_sb = carve(2 * NREL * F)
        w2_sb = carve(NTYPE * F)
        relprod = carve(2 * 2 * NREL * F)
        rel_stage = carve(2 * NTYPE * F)
        src_hot = carve(2 * GS * P // 2).bitcast(bf16)
        bucket_hot = carve(2 * GS * 226 // 2).bitcast(bf16)
        w0_pq_sb = carve(2 * F)
        w0_attr_sb = carve(F)
        w0_out_sb = carve(F)
        sf = carve(4 * STEPS)
        type9 = carve(STEPS)
        bucket = carve(STEPS // 2).bitcast(bf16)
        tile_row = carve(STEPS)[0:1, :].bitcast(i32)
        counts = carve(BLOCKS * 2 * NREL)
        pre = carve(2 * GS * F)
        upper = carve(P)
        zero_bf = carve(113).bitcast(bf16)

        iota = sb("iota", [P, STEPS])
        iota_bf = sb("iota_bf", [P, 226], bf16)
        ident = sb("ident", [P, P])
        ident_bf = sb("ident_bf", [P, P], bf16)
        next_row = sb("next_row", [TROW, TROW])
        ones = sb("ones", [P, P])
        tile_no = sb("tile_no", [TROW, 4])
        node_base = sb("node_base", [P, BLOCKS])
        small = sb("small", [P, 64])
        node_loc = sb("node_loc", [P, STEPS])
        src_lo = sb("src_lo", [P, STEPS], bf16)
        src_hi = sb("src_hi", [P, STEPS])
        src_idx = sb("src_idx", [P, STEPS + RING * GS], i32)
        rel_idx = sb("rel_idx", [P, STEPS + RING * GS], i32)
        block_row = sb("block_row", [1, STEPS], i32)
        seg_start = sb("seg_start", [SROW, 512])
        row_start = sb("row_start", [1, SROW])
        end_idx = sb("end_idx", [P, BLOCKS], i32)
        X = sb("X", [P, BLOCKS * F])
        XT = sb("XT", [F + 1, NP_])
        acc = sb("acc", [P, BLOCKS * ACC0])
        node_h = sb("node_h", [P, BLOCKS * (F + 2)])
        nA = sb("nA", [P, BLOCKS * F])
        nB = sb("nB", [P, BLOCKS * F])
        c25 = sb("c25", [P, 16 * BLOCKS])
        idx_ring = sb("idx_ring", [P, RING * GS], i32)
        rows_ring = sb("rows_ring", [P, RING * GS * GW])
        hot_ring = sb("hot_ring", [P, 5 * GS * P])
        hot_T = sb("hot_T", [P, 2 * GS * P], bf16)
        msg_ring = sb("msg_ring", [P, 5 * GS * ACC0])
        as_edge = sb("as_edge", [P, STEPS])
        picked = sb("picked", [P, 2 * GS * BLOCKS])
        wtmp = sb("wtmp", [P, 4 * 2 * GS])
        scan = sb("scan", [SROW, 512])
        carry = sb("carry", [1, SROW + 1])
        carry_col = sb("carry_col", [SROW, 1])
        tail = sb("tail", [SROW, 2])
        seg_node = sb("seg_node", [P, BLOCKS])
        as_parts = sb("as_parts", [P, 3 * BLOCKS], bf16)
        adm_parts = sb("adm_parts", [P, BLOCKS * 6], bf16)
        w3_sb = sb("w3_sb", [F, F + 2])
        w3T_sb = sb("w3T_sb", [F, F])
        a3_sb = sb("a3_sb", [F, 2])
        b3_sb = sb("b3_sb", [P, F])

        PS = ctx.enter_context(nc.psum_tensor("PS", [P, 8 * 512], fp32))

        def bank(n, a=0, b=512, p=P):
            return PS[0:p, n * 512 + a:n * 512 + b]

        def xv(t, w=F):
            return t.rearrange("p (b f) -> p b f", f=w)

        def col(n, k=1):
            return c25[:, n * BLOCKS:(n + k) * BLOCKS]

        LAYERS = ["l0", "l2", "g0", "g1", "g2"]
        XG = [min(4, BLOCKS - 4 * q) for q in range(-(-BLOCKS // 4))]

        def pipeline(eng, iteration, lag):
            for k in range(RING):
                iteration(0, k)
            with eng.Fori(1, OUTER) as o:
                for k in range(RING):
                    iteration(o, k)
            for k in range(lag):
                iteration(OUTER, k)

        def live(o, k, lag):
            return not isinstance(o, int) or 0 <= o * RING + k - lag < GROUPS

        def reached(eng, sem, value):
            if not isinstance(value, int) or value > 0:
                eng.wait_ge(sem, value)

        block = ctx.enter_context(nc.Block())

        @block.sync
        def _(sp):
            sp.dma_start(ints_sb[0:TROW, :].rearrange("q (a f) -> q a f", a=4),
                         ints.rearrange("a (q f) -> q a f", q=TROW)).then_inc(S("ints_in"), 16)
            sp.dma_start(xv(X[:, :]), x.rearrange("(b p) f -> p b f", p=P)).then_inc(S("x_in"), 16)
            for dst, s in ((w0_pq_sb[0:F + 1, :], w0_pq), (w0_attr_sb[0:8, :], w0_attr),
                           (w0_out_sb[0:F + 1, :], w0_out), (w1_sb[0:F + 1, :], w1[2]),
                           (w2_sb[0:F, :], w2)):
                sp.dma_start(dst, s).then_inc(S("w_in"), 16)
            sp.wait_ge(S("p_staged"), len(XG))
            sp.dma_start(src_rows.rearrange("(b p) f -> p b f", p=P),
                         xv(node_h[:, 0:BLOCKS * F])).then_inc(S("l0_table"), 16)
            sp.wait_ge(S("keys_staged"), 1)
            sp.dma_start(keys[0:1, :], small[0:1, 0:1]).then_inc(S("keys_out"), 16)
            sp.dma_start(keys[1:STEPS * P + 1, :].rearrange("(q f) o -> q (f o)", q=SROW),
                         scan[:, :]).then_inc(S("keys_out"), 16)
            sp.dma_start(seg_max[STEPS * P:STEPS * P + 1, :], small[0:1, 1:2]).then_inc(S("keys_out"), 16)
            sp.wait_ge(S("keys_out"), 48)
            sp.dma_start(seg_start[:, :], keys[0:STEPS * P, :].rearrange("(q f) o -> q (f o)", q=SROW))\
              .then_inc(S("prev_key"), 16)

            def attrs(o, k):
                if o is OUTER:
                    return
                reached(sp, S("l0_expanded"), o * RING + k - 4)
                _, ts_ = nc.values_load_multi_w_load_instructions(
                    tile_row[0:1, ds((o * RING + k) * GS, GS)], engines=[mybir.EngineType.SP],
                    min_val=0, max_val=TILES - 1,
                    skip_runtime_bounds_check_because="a tile number by construction")
                for s in range(GS):
                    sp.dma_start(attr_ring[0:8, (k % 5 * GS + s) * P:(k % 5 * GS + s + 1) * P],
                                 attr_t[:, ds(ts_[s] * P, P)]).then_inc(S(f"attr_in{k % 5}"), 16)

            sp.wait_ge(S("steps_ready"), 1)
            pipeline(sp, attrs, 0)

            for b in range(BLOCKS):
                sp.wait_ge(S("rel_staged_v"), b + 1)
                sp.wait_ge(S("rel_staged_a"), b + 1)
                sp.dma_start(rel_rows.rearrange("(n r) f -> n (r f)", r=NTYPE)[b * P:(b + 1) * P, :],
                             rel_stage[:, (b % 2) * 1024:(b % 2 + 1) * 1024])\
                  .then_inc(S(f"l2_table{b % 2}"), 16)

            for n in range(3):
                if n:
                    sp.wait_ge(S("weights_free"), n)
                sp.dma_start(w3_sb[:, 0:F], w3[n]).then_inc(S("w3_in"), 16)
                sp.dma_start(w3T_sb[:, :], w3_t[n]).then_inc(S("w3_in"), 16)
                sp.dma_start(a3_sb[:, :], a3[n]).then_inc(S("w3_in"), 16)
                if n:
                    sp.wait_ge(S("gat_done"), n)
                sp.dma_start(b3_sb[:, :], b3[n].to_broadcast([P, F]))\
                  .then_inc(S("b3_in"), 16)
                sp.wait_ge(S("gat_h"), (n + 1) * len(XG))
                sp.dma_start(gat_rows[n].rearrange("(b p) f -> p b f", p=P),
                             xv(node_h[:, :], F + 2)[:, :, 0:F]).then_inc(S("gat_table"), 16)
                sp.wait_ge(S("gat_scanned"), n + 1)
                sp.dma_start(seg_max[0:STEPS * P, :].rearrange("(q f) o -> q (f o)", q=SROW),
                             scan[:, :]).then_inc(S("seg_max_out"), 16)
            sp.wait_ge(S("ln_done"), 4)
            full = N // P
            sp.dma_start(out[0:full * P, :].rearrange("(b p) f -> p b f", p=P),
                         xv(X[:, 0:full * F])).then_inc(S("out_done"), 16)
            sp.dma_start(out[full * P:N, :], X[0:N - full * P, full * F:BLOCKS * F]).then_inc(S("out_done"), 16)
            sp.wait_ge(S("out_done"), 32)

        @block.gpsimd
        def _(pool):
            pool.iota(iota[:, :], [[1, STEPS]], base=0, channel_multiplier=0,
                      allow_small_or_imprecise_dtypes=True)
            pool.iota(iota_bf[:, :], [[1, 226]], base=0, channel_multiplier=0,
                      allow_small_or_imprecise_dtypes=True)
            pool.iota(tile_no[:, :], [[1, 4]], base=0, channel_multiplier=4,
                      allow_small_or_imprecise_dtypes=True)
            pool.iota(node_base[:, :], [[P, BLOCKS]], base=-1, channel_multiplier=0,
                      allow_small_or_imprecise_dtypes=True)
            pool.memset(ident[:, :], 0.0)
            pool.memset(ident_bf[:, :], 0.0)
            pool.memset(next_row[:, :], 0.0)
            pool.memset(ones[:, :], 1.0)
            pool.memset(upper[:, :], 1.0).then_inc(S("filled"), 1)
            pool.wait_ge(S("filled"), 1)
            for m in (ident, ident_bf):
                pool.affine_select(out=m[:, :], in_=m[:, :], compare_op=ALU.not_equal, fill=1.0,
                                   base=0, pattern=[[-1, P]], channel_multiplier=1)
            pool.affine_select(out=next_row[:, :], in_=next_row[:, :], compare_op=ALU.not_equal,
                               fill=1.0, base=1, pattern=[[-1, TROW]], channel_multiplier=1)
            pool.affine_select(out=upper[:, :], in_=upper[:, :], compare_op=ALU.is_ge, fill=0.0,
                               base=0, pattern=[[1, P]], channel_multiplier=-1).then_inc(S("consts"), 1)
            pool.wait_ge(S("consts"), 1)
            pool.memset(XT[F:F + 1, :], 1.0).then_inc(S("row_of_ones"), 1)
            pool.wait_ge(S("row_of_ones"), 1)
            pool.memset(msg_ring[:, :], 1.0)
            pool.memset(rows_ring[:, :], 1.0)
            pool.memset(zero_bf[:, :], 0.0)
            pool.memset(src_idx[:, STEPS:], 0)
            pool.memset(rel_idx[:, STEPS:], 0)
            pool.memset(small[:, 0:1], -1.0)
            pool.memset(small[:, 1:2], -BIG)
            pool.memset(small[:, 2:3], EPS)
            pool.memset(carry[:, :], -BIG).then_inc(S("presets"), 1)

            def gathers(li, table, freed, before=0):

                def group(o, k):
                    reached(pool, S(freed), before + (o - 1) * RING + k + 1)
                    if not isinstance(o, int):
                        pool.sem_inc(S("slot_free"), 1)
                        pool.wait_ge(S("idx_staged"), li * (GROUPS + 1) + 2 + (o - 1) * RING + k)
                        pool.sem_inc(S("slot_free"), 1)
                    for s in range(GS):
                        c = k * GS + s
                        pool.indirect_dma_start(
                            rows_ring[:, c * GW:c * GW + F], None, table,
                            bass.IndirectOffsetOnAxis(ap=idx_ring[:, c:c + 1], axis=0))\
                            .then_inc(S(f"rows_in{k}"), 16)

                pool.wait_ge(S("idx_staged"), li * (GROUPS + 1) + 1)
                for k in range(RING):
                    group(0, k)
                return group

            def rest(group):
                with pool.Fori(1, OUTER) as o:
                    for k in range(RING):
                        group(o, k)

            pool.wait_ge(S("presets"), 1)
            pool.wait_ge(S("steps_ready"), 1)
            pool.wait_ge(S("l0_table"), 16)
            rest(gathers(0, src_rows, "l0_pre"))
            pool.wait_ge(S("out0_psum"), 4)
            pool.memset(XT[F:F + 1, :], 1.0).then_inc(S("row_of_ones"), 1)
            pool.wait_ge(S("l2_table0"), 16 * (BLOCKS - BLOCKS // 2))
            pool.wait_ge(S("l2_table1"), 16 * (BLOCKS // 2))
            rest(gathers(1, rel_rows, "l2_summed"))
            for n in range(3):
                pool.wait_ge(S("gat_table"), 16 * (n + 1))
                parts = gathers(2 + n, gat_rows[n], "gat_scaled", n * GROUPS)
                pool.wait_ge(S("seg_max_out"), 16 * (n + 1))
                for b in range(BLOCKS):
                    pool.indirect_dma_start(
                        seg_node[:, b:b + 1], None, seg_max,
                        bass.IndirectOffsetOnAxis(ap=end_idx[:, b:b + 1], axis=0))\
                        .then_inc(S("seg_node_in"), 16)
                rest(parts)

        @block.scalar
        def _(act):
            A = nc.scalar

            def copy_XT(time):
                for q, nb in enumerate(XG):
                    act.wait_ge(S("xT_psum"), time * len(XG) + q + 1)
                    A.activation(XT[0:F, q * 512:q * 512 + nb * P], bank(q % 2, 0, nb * P, F), ACT.Copy)\
                        .then_inc(S("xT"), 1)

            def ln_sqrt(n):
                act.wait_ge(S("ln_var"), n + 1)
                A.activation(col(2), col(1), ACT.Sqrt, bias=small[:, 2:3], scale=1.0 / F)\
                    .then_inc(S("ln_std"), 1)

            def first_indices(idx):
                A.activation(idx_ring[:, :], idx[:, 0:RING * GS], ACT.Copy).then_inc(S("idx_staged"), 1)

            def next_indices(idx, o, k, li):
                g, kk = o * RING + k - 1, (k - 1) % RING
                act.wait_ge(S(f"rows_in{kk}"), 64 * (li * OUTER + o + (k - 1) // RING + 1))
                A.activation(idx_ring[:, kk * GS:(kk + 1) * GS], idx[:, ds((g + RING) * GS, GS)], ACT.Copy)\
                    .then_inc(S("idx_staged"), 1)

            act.wait_ge(S("presets"), 1)
            copy_XT(0)
            for q, nb in enumerate(XG):
                act.wait_ge(S("q_read"), q + 1)
                A.activation(xv(node_h[:, q * 4 * F:(q * 4 + nb) * F]),
                             xv(bank(2 + q % 2, 0, nb * P), P)[:, :, 0:F], ACT.Copy)\
                    .then_inc(S("p_staged"), 1)

            act.wait_ge(S("steps_ready"), 1)
            first_indices(src_idx)

            def l0(o, k):
                if live(o, k, 0):
                    g = o * RING + k
                    act.wait_ge(S("l0_hotT_psum"), g + 1)
                    reached(act, S("l0_expanded"), g - 1)
                    A.activation(hot_T[:, k % 2 * 512:k % 2 * 512 + 512], bank(k % 2), ACT.Copy)\
                        .then_inc(S("l0_hotT"), 1)
                if live(o, k, 1):
                    g, kk = o * RING + k - 1, k - 1
                    act.wait_ge(S("l0_pre"), g + 1)
                    reached(act, S("l0_summed"), g - 4)
                    A.activation(xv(msg_ring[:, kk % 5 * GS * ACC0:(kk % 5 + 1) * GS * ACC0], ACC0)[:, :, 0:F],
                                 xv(pre[:, kk % 2 * 256:kk % 2 * 256 + 256]), ACT.Relu)\
                        .then_inc(S("l0_msg"), 1)
                    next_indices(src_idx, o, k, 0)

            pipeline(act, l0, 1)
            for q, nb in enumerate(XG):
                act.wait_ge(S("sum_T_psum"), q + 1)
                A.activation(XT[0:F + 1, q * 512:q * 512 + nb * P], bank(q % 2, 0, nb * P, F + 1), ACT.Copy)\
                    .then_inc(S("sum_T"), 1)
            ln_sqrt(0)
            copy_XT(1)
            ln_sqrt(1)
            copy_XT(2)
            for b in range(BLOCKS):
                act.wait_ge(S("rel_psum"), b + 1)
                if b >= 2:
                    act.wait_ge(S(f"l2_table{b % 2}"), 16 * (b // 2))
                A.activation(rel_stage[:, (b % 2) * 1024 + 512:(b % 2 + 1) * 1024],
                             bank(2 + (b % 2) * 2 + 1), ACT.Copy).then_inc(S("rel_staged_a"), 1)

            first_indices(rel_idx)

            def l2(o, k):
                if live(o, k, 0):
                    g = o * RING + k
                    if isinstance(o, int) and o == 0 and k == 0:
                        act.wait_ge(S("l2_table0"), 16 * (BLOCKS - BLOCKS // 2))
                        act.wait_ge(S("l2_table1"), 16 * (BLOCKS // 2))
                        act.wait_ge(S("arena_free"), 1)
                    act.wait_ge(S("l2_srcT_psum"), g + 1)
                    A.activation(src_hot_T[:, ds(g * GS * P, GS * P)],
                                 bank(k % 2).bitcast(bf16)[:, 0:GS * P], ACT.Copy)\
                        .then_inc(S("l2_srcT"), 1)
                if live(o, k, 1):
                    next_indices(rel_idx, o, k, 1)

            pipeline(act, l2, 1)
            ln_sqrt(2)

            for n in range(3):
                copy_XT(3 + n)
                act.wait_ge(S("gat_wa_psum"), n + 1)
                A.activation(w3_sb[:, F:F + 2], bank(7, 0, 2, F), ACT.Copy).then_inc(S("gat_wa"), 1)
                for q, nb in enumerate(XG):
                    act.wait_ge(S("gat_h_psum"), n * len(XG) + q + 1)
                    A.activation(xv(node_h[:, q * 4 * (F + 2):(q * 4 + nb) * (F + 2)], F + 2),
                                 xv(bank(2 + q % 2, 0, nb * (F + 2)), F + 2), ACT.Copy)\
                        .then_inc(S("gat_h"), 1)
                first_indices(src_idx)
                act.wait_ge(S("gat_self_e"), n + 1)
                A.activation(col(8), col(7), ACT.Exp).then_inc(S("gat_self_w"), 1)

                def gat(o, k, n=n, before=n * GROUPS):
                    if live(o, k, 0):
                        g = o * RING + k
                        act.wait_ge(S("gat_hotT_psum"), before + g + 1)
                        reached(act, S("gat_expanded"), before + g - 1)
                        A.activation(hot_T[:, k % 2 * 512:k % 2 * 512 + 512], bank(k % 2), ACT.Copy)\
                            .then_inc(S("gat_hotT"), 1)
                    if live(o, k, 1):
                        g, kk = o * RING + k - 1, k - 1
                        act.wait_ge(S("gat_logit"), before + g + 1)
                        w = wtmp[:, 24 + kk % 2 * GS:24 + kk % 2 * GS + GS]
                        reached(act, S("gat_scaled"), before + g - 1)
                        A.activation(w, wtmp[:, 16 + kk % 2 * GS:16 + kk % 2 * GS + GS], ACT.Exp)\
                            .then_inc(S("gat_weight"), 1)
                        act.wait_ge(S("gat_weight"), before + g + 1)
                        act.wait_ge(S(f"rows_in{kk % RING}"), 64 * ((2 + n) * OUTER + o + kk // RING + 1))
                        reached(act, S("gat_summed"), before + g - 4)
                        for s in range(GS):
                            c, m = kk % RING * GS + s, kk % 5 * GS + s
                            i = A.activation(msg_ring[:, m * ACC0:m * ACC0 + GW],
                                             rows_ring[:, c * GW:(c + 1) * GW], ACT.Copy,
                                             scale=w[:, s:s + 1])
                        i.then_inc(S("gat_scaled"), 1)
                        next_indices(src_idx, o, k, 2 + n)

                pipeline(act, gat, 1)
            ln_sqrt(3)

        @block.vector
        def _(dve):
            V = nc.vector
            n_linked = [0]

            def link(ins):
                n_linked[0] += 1
                ins.then_inc(S("dve_chain"), 1)
                dve.wait_ge(S("dve_chain"), n_linked[0])

            dve.wait_ge(S("ints_in"), 16)
            dve.wait_ge(S("presets"), 1)
            src_i, dst_i, t16_i, t9_i = (ints_sb[0:TROW, a * 512:(a + 1) * 512] for a in range(4))
            dst_f, src_f, rel_f, t9_f = (edge_f[0:TROW, a * 512:(a + 1) * 512] for a in range(4))
            lb_i = itmp[0:TROW, 0:4]
            V.tensor_scalar(lb_i, dst_i.rearrange("q (j f) -> q j f", j=4)[:, :, P - 1], 7, None,
                            ALU.arith_shift_right)
            V.tensor_copy(dst_f, dst_i)
            V.tensor_copy(src_f, src_i)
            V.tensor_copy(t9_f, t9_i)
            link(V.tensor_copy(rel_f, t16_i))
            link(V.scalar_tensor_tensor(out=rel_f, in0=src_f, scalar=float(NTYPE), in1=rel_f,
                                        op0=ALU.mult, op1=ALU.add))
            last_block = small[0:TROW, 8:12]
            V.tensor_copy(last_block, lb_i).then_inc(S("last_block"), 1)
            dve.wait_ge(S("prev_block"), 1)
            first, end = small[0:TROW, 12:16], small[0:TROW, 16:20]
            V.tensor_tensor(first[:, 1:4], tile_no[:, 1:4], last_block[:, 0:3], ALU.add)
            V.tensor_tensor(first[:, 0:1], tile_no[:, 0:1], bank(4, 0, 1, TROW), ALU.add)
            link(V.scalar_tensor_tensor(out=end, in0=tile_no[:, :], scalar=1.0, in1=last_block,
                                        op0=ALU.add, op1=ALU.add))
            for j in range(4):
                m = step_of_tile[0:TROW, j * STEPS:(j + 1) * STEPS]
                link(V.tensor_scalar(m, iota[0:TROW, :], first[:, j:j + 1], None, ALU.is_ge))
                i = V.scalar_tensor_tensor(out=m, in0=iota[0:TROW, :], scalar=end[:, j:j + 1], in1=m,
                                           op0=ALU.is_lt, op1=ALU.mult)
            i.then_inc(S("step_of_tile"), 1)
            dve.wait_ge(S("step_psum"), 5)
            blk, tmp, vld = sf[:, 0:STEPS], sf[:, STEPS:2 * STEPS], sf[:, 2 * STEPS:3 * STEPS]
            V.tensor_copy(tile_row[:, :], bank(2, 0, STEPS, 1))
            V.tensor_copy(src_idx[:, 0:STEPS], bank(4, 0, STEPS))
            V.tensor_copy(rel_idx[:, 0:STEPS], bank(5, 0, STEPS))
            V.tensor_copy(type9[:, :], bank(6, 0, STEPS))
            link(V.tensor_tensor(blk, iota[:, :], bank(2, 0, STEPS), ALU.subtract))
            V.tensor_copy(block_row[:, :], blk[0:1, :]).then_inc(S("steps_ready"), 1)
            link(V.scalar_tensor_tensor(out=node_loc[:, :], in0=blk, scalar=-float(P),
                                        in1=bank(3, 0, STEPS), op0=ALU.mult, op1=ALU.add))
            hi_i, lo_i = itmp[:, 0:STEPS], itmp[:, STEPS:2 * STEPS]
            V.tensor_scalar(hi_i, src_idx[:, 0:STEPS], 7, None, ALU.arith_shift_right)
            V.tensor_scalar(lo_i, src_idx[:, 0:STEPS], P - 1, None, ALU.bitwise_and)
            link(V.tensor_scalar(tmp, node_loc[:, :], 0.0, None, ALU.is_ge))
            link(V.scalar_tensor_tensor(out=vld, in0=node_loc[:, :], scalar=float(P), in1=tmp,
                                        op0=ALU.is_lt, op1=ALU.mult))
            V.tensor_copy(src_hi[:, :], hi_i)
            link(V.tensor_copy(tmp, lo_i))
            V.scalar_tensor_tensor(out=bucket[:, :], in0=src_hi[:, :], scalar=float(NREL),
                                   in1=type9[:, :], op0=ALU.mult, op1=ALU.add)
            link(V.scalar_tensor_tensor(out=tmp, in0=tmp, scalar=1.0, in1=vld, op0=ALU.add, op1=ALU.mult))
            V.tensor_scalar(src_lo[:, :], tmp, -1.0, None, ALU.add)
            V.tensor_copy(sf[:, 3 * STEPS:4 * STEPS], bank(3, 0, STEPS)).then_inc(S("dst_step"), 1)

            for q, nb in enumerate(XG):
                dve.wait_ge(S("pq_psum"), q + 1)
                V.tensor_copy(xv(nA[:, q * 4 * F:(q * 4 + nb) * F]),
                              xv(bank(2 + q % 2, 0, nb * P), P)[:, :, F:2 * F]).then_inc(S("q_read"), 1)
            dve.wait_ge(S("q_read"), len(XG))
            qv = q_parts.rearrange("p (b a f) -> p b a f", a=3, f=F)
            link(V.tensor_copy(qv[:, :, 0, :], xv(nA[:, :])))
            link(V.tensor_tensor(xv(nB[:, :]), xv(nA[:, :]), qv[:, :, 0, :], ALU.subtract))
            link(V.tensor_copy(qv[:, :, 1, :], xv(nB[:, :])))
            link(V.tensor_tensor(xv(nA[:, :]), xv(nB[:, :]), qv[:, :, 1, :], ALU.subtract))
            V.tensor_copy(qv[:, :, 2, :], xv(nA[:, :])).then_inc(S("q_parts"), 1)
            dve.wait_ge(S("keys_psum"), 1)
            V.tensor_copy(scan[:, :], bank(6, 0, 512, SROW)).then_inc(S("keys_staged"), 1)
            link(V.memset(acc[:, :], 0.0))

            def hots(g, k, sumw, before=0):
                reached(dve, S(sumw), before + g - 4)
                return V.tensor_tensor(
                    hot_ring[:, k % 5 * 512:k % 5 * 512 + 512].rearrange("p (s c) -> p s c", s=GS),
                    iota[:, 0:P].unsqueeze(1).to_broadcast([P, GS, P]),
                    node_loc[:, ds(g * GS, GS)].unsqueeze(2).to_broadcast([P, GS, P]), ALU.is_equal)

            def add_sums(layer, g, kk, w, before=0):
                _, bs = nc.values_load_multi_w_load_instructions(
                    block_row[0:1, ds(g * GS, GS)], engines=[mybir.EngineType.DVE], min_val=0,
                    max_val=BLOCKS - 1, skip_runtime_bounds_check_because="a block number by construction")
                dve.wait_ge(S(f"{layer}_summed"), before + g + 1)
                for s in range(GS):
                    reached(dve, S(f"{layer}_added"), (before + g) * GS + s)
                    a = acc[:, ds(bs[s] * w, w)]
                    V.tensor_tensor(a, a, bank(4 + kk % 2, s * w, (s + 1) * w), ALU.add)\
                        .then_inc(S(f"{layer}_added"), 1)

            def l0(o, k):
                if live(o, k, 0):
                    g = o * RING + k
                    hots(g, k, "l0_summed")
                    V.tensor_tensor(
                        xv(msg_ring[:, k % 5 * GS * ACC0:(k % 5 + 1) * GS * ACC0], ACC0)[:, :, F + 1:ACC0],
                        iota[:, 0:NREL].unsqueeze(1).to_broadcast([P, GS, NREL]),
                        type9[:, ds(g * GS, GS)].unsqueeze(2).to_broadcast([P, GS, NREL]), ALU.is_equal)
                    reached(dve, S("l0_counted"), g - 1)
                    V.tensor_tensor(
                        src_hot[:, k % 2 * 512:k % 2 * 512 + 512].rearrange("p (s c) -> p s c", s=GS),
                        iota_bf[:, 0:P].unsqueeze(1).to_broadcast([P, GS, P]),
                        src_lo[:, ds(g * GS, GS)].unsqueeze(2).to_broadcast([P, GS, P]), ALU.is_equal)
                    V.tensor_tensor(
                        bucket_hot[:, k % 2 * GS * 226:(k % 2 + 1) * GS * 226].rearrange("p (s c) -> p s c", s=GS),
                        iota_bf[:, :].unsqueeze(1).to_broadcast([P, GS, 226]),
                        bucket[:, ds(g * GS, GS)].unsqueeze(2).to_broadcast([P, GS, 226]), ALU.is_equal)\
                        .then_inc(S("l0_hots"), 1)
                if live(o, k, 1):
                    g, kk = o * RING + k - 1, k - 1
                    dve.wait_ge(S(f"rows_in{kk % RING}"), 64 * (o + kk // RING + 1))
                    dve.wait_ge(S("l0_expanded"), g + 1)
                    reached(dve, S("l0_msg"), g - 1)
                    r = kk % RING * GS * GW
                    V.tensor_tensor(xv(pre[:, kk % 2 * 256:kk % 2 * 256 + 256]),
                                    xv(rows_ring[:, r:r + GS * GW], GW)[:, :, 0:F],
                                    xv(bank(2 + kk % 2, 0, 256)), ALU.add).then_inc(S("l0_pre"), 1)
                if live(o, k, 3):
                    add_sums("l0", o * RING + k - 3, k - 3, ACC0)

            pipeline(dve, l0, 3)
            dve.wait_ge(S("l0_added"), STEPS)
            dve.wait_ge(S("src_counts"), 1)
            cv = xv(counts[:, :], 2 * NREL)
            av = xv(acc[:, :], ACC0)
            V.tensor_copy(cv[:, :, 0:NREL], xv(bank(6, 0, BLOCKS * NREL), NREL))
            link(V.tensor_copy(cv[:, :, NREL:], av[:, :, F + 1:]))
            link(V.tensor_reduce(col(10), cv, axis=AX.X, op=ALU.add))
            link(V.tensor_scalar(col(10), col(10), 1.0, None, ALU.max))
            V.reciprocal(col(11), col(10))
            link(V.tensor_copy(col(12), av[:, :, F]))
            V.tensor_scalar(col(13), col(12), 0.0, None, ALU.is_gt).then_inc(S("degree"), 1)
            dve.wait_ge(S("degree_psum"), 1)
            link(V.tensor_copy(col(14), bank(7, 32, 32 + BLOCKS)))
            link(V.tensor_tensor_scan(col(15), ones[:, 0:BLOCKS],
                                      col(14), 0.0, ALU.mult, ALU.add))
            link(V.tensor_tensor(col(15), col(15), col(14), ALU.subtract))
            link(V.tensor_tensor(col(15), col(15), node_base[:, :], ALU.add))
            link(V.tensor_tensor(col(15), col(15), bank(7, 0, BLOCKS), ALU.add))
            link(V.tensor_scalar(col(15), col(15), -float(STEPS * P), None, ALU.add))
            link(V.tensor_tensor(col(15), col(15), col(13), ALU.mult))
            V.tensor_scalar(end_idx[:, :], col(15), float(STEPS * P), None, ALU.add)

            dve.wait_ge(S("prev_key"), 16)
            link(V.tensor_tensor(seg_start[:, :], scan[:, :], seg_start[:, :], ALU.not_equal))
            link(V.tensor_reduce(tail[:, 0:1], seg_start[:, :], axis=AX.X, op=ALU.max))
            link(V.tensor_scalar(tail[:, 1:2], tail[:, 0:1], -BIG, None, ALU.mult))
            V.tensor_scalar(seg_start[:, :], seg_start[:, :], -BIG, None, ALU.mult)\
                .then_inc(S("row_start_in"), 1)
            dve.wait_ge(S("row_start_psum"), 1)
            link(V.tensor_copy(row_start[:, :], bank(7, 64, 64 + SROW, 1)))

            def layer_norm(n):
                link(V.tensor_reduce(col(0), xv(nA[:, :]), axis=AX.X, op=ALU.add))
                link(V.tensor_scalar(col(0), col(0), 1.0 / F, None, ALU.mult))
                link(V.tensor_tensor(xv(nA[:, :]), xv(nA[:, :]),
                                     col(0).unsqueeze(2).to_broadcast([P, BLOCKS, F]), ALU.subtract))
                link(V.tensor_tensor(nB[:, :], nA[:, :], nA[:, :], ALU.mult))
                V.tensor_reduce(col(1), xv(nB[:, :]), axis=AX.X, op=ALU.add).then_inc(S("ln_var"), 1)
                dve.wait_ge(S("ln_std"), n + 1)
                link(V.reciprocal(col(3), col(2)))
                V.tensor_tensor(xv(X[:, :]), xv(nA[:, :]),
                                col(3).unsqueeze(2).to_broadcast([P, BLOCKS, F]), ALU.mult)\
                    .then_inc(S("ln_done"), 1)

            for q in range(4):
                nb = min(8, BLOCKS - 8 * q)
                dve.wait_ge(S("out0_psum"), q + 1)
                i = V.tensor_tensor(nA[:, q * 512:q * 512 + nb * F], X[:, q * 512:q * 512 + nb * F],
                                    bank(2 + q % 2, 0, nb * F), ALU.add)
                i.then_inc(S("out0_added"), 1)
            dve.wait_ge(S("out0_added"), 4)
            layer_norm(0)

            for b in range(BLOCKS):
                dve.wait_ge(S("rel1_psum"), b + 1)
                z = relprod[:, b % 2 * 1152:(b % 2 + 1) * 1152].rearrange("p (r f) -> p r f", f=F)
                lo = (b % 2) * 3
                V.tensor_tensor(z, PS[:, lo * 512:lo * 512 + 1152].rearrange("p (r f) -> p r f", f=F),
                                cv[:, b, :].unsqueeze(2).to_broadcast([P, 2 * NREL, F]), ALU.mult)\
                    .then_inc(S("rel1_read"), 1)
                dve.wait_ge(S("rel1_read"), b + 1)
                V.tensor_reduce(nA[:, b * F:(b + 1) * F], z.rearrange("p r f -> p f r"),
                                axis=AX.X, op=ALU.add).then_inc(S("rel1_sum"), 1)
            dve.wait_ge(S("rel1_sum"), BLOCKS)
            link(V.tensor_tensor(xv(nA[:, :]), xv(nA[:, :]),
                                 col(11).unsqueeze(2).to_broadcast([P, BLOCKS, F]), ALU.mult))
            link(V.tensor_tensor(nA[:, :], nA[:, :], X[:, :], ALU.add))
            layer_norm(1)

            for b in range(BLOCKS):
                dve.wait_ge(S("rel_psum"), b + 1)
                if b >= 2:
                    dve.wait_ge(S(f"l2_table{b % 2}"), 16 * (b // 2))
                V.tensor_copy(rel_stage[:, (b % 2) * 1024:(b % 2) * 1024 + 512],
                              bank(2 + (b % 2) * 2)).then_inc(S("rel_staged_v"), 1)
            dve.wait_ge(S("rel_staged_v"), BLOCKS)
            V.memset(acc[:, :], 0.0).then_inc(S("arena_free"), 1)
            dve.wait_ge(S("arena_free"), 1)

            def l2(o, k):
                if live(o, k, 0):
                    g = o * RING + k
                    hots(g, k, "l2_summed")
                    reached(dve, S("l2_srcT_psum"), g - 1)
                    V.tensor_tensor(
                        hot_T[:, k % 2 * 512:k % 2 * 512 + 512].rearrange("p (s c) -> p s c", s=GS),
                        iota_bf[:, 0:P].unsqueeze(1).to_broadcast([P, GS, P]),
                        src_lo[:, ds(g * GS, GS)].unsqueeze(2).to_broadcast([P, GS, P]), ALU.is_equal)\
                        .then_inc(S("l2_hots"), 1)
                if live(o, k, 3):
                    add_sums("l2", o * RING + k - 3, k - 3, F)

            pipeline(dve, l2, 3)
            dve.wait_ge(S("l2_added"), STEPS)
            link(V.tensor_tensor(nA[:, :], X[:, :], acc[:, 0:BLOCKS * F], ALU.add))
            layer_norm(2)

            def split3(dst, value, rest):
                link(V.tensor_copy(dst(0), value))
                link(V.tensor_tensor(rest, value, dst(0), ALU.subtract))
                link(V.tensor_copy(dst(1), rest))
                link(V.tensor_tensor(rest, rest, dst(1), ALU.subtract))
                return V.tensor_copy(dst(2), rest)

            for n in range(3):
                dve.wait_ge(S("gat_h"), (n + 1) * len(XG))
                hv = xv(node_h[:, :], F + 2)
                V.tensor_copy(col(4), hv[:, :, F])
                link(V.tensor_copy(col(5), hv[:, :, F + 1]))
                split3(lambda a: as_parts[:, a * BLOCKS:(a + 1) * BLOCKS], col(4), col(6))\
                    .then_inc(S("gat_as_parts"), 1)
                link(V.memset(acc[:, :], 0.0))

                def pick(o, k, before=n * GROUPS):
                    if live(o, k, 0):
                        g = o * RING + k
                        dve.wait_ge(S("gat_as_psum"), before + g + 1)
                        reached(dve, S("gat_picked"), before + g - 1)
                        pv = picked[:, k % 2 * 100:k % 2 * 100 + 100].rearrange("p (s c) -> p s c", s=GS)
                        V.tensor_tensor(pv, iota[:, 0:BLOCKS].unsqueeze(1).to_broadcast([P, GS, BLOCKS]),
                                        src_hi[:, ds(g * GS, GS)].unsqueeze(2).to_broadcast([P, GS, BLOCKS]),
                                        ALU.is_equal).then_inc(S("gat_p1"), 1)
                        dve.wait_ge(S("gat_p1"), 2 * (before + g) + 1)
                        V.tensor_tensor(pv, pv, bank(4 + k % 2, 0, 100).rearrange("p (s c) -> p s c", s=GS),
                                        ALU.mult).then_inc(S("gat_p1"), 1)
                        dve.wait_ge(S("gat_p1"), 2 * (before + g) + 2)
                        V.tensor_reduce(as_edge[:, ds(g * GS, GS)], pv, axis=AX.X, op=ALU.add)\
                            .then_inc(S("gat_picked"), 1)

                pipeline(dve, pick, 0)
                dve.wait_ge(S("gat_asT_psum"), n + 1)
                V.tensor_tensor_scan(scan[:, :], seg_start[:, :], bank(6, 0, 512, SROW), -BIG,
                                     ALU.add, ALU.max).then_inc(S("gat_scan1"), 1)
                dve.wait_ge(S("gat_tail_psum"), n + 1)
                V.tensor_tensor_scan(carry[:, 1:SROW + 1], row_start[:, :], bank(7, 0, SROW, 1), -BIG,
                                     ALU.add, ALU.max).then_inc(S("gat_carry"), 1)
                dve.wait_ge(S("gat_carry_psum"), n + 1)
                link(V.tensor_copy(carry_col[:, :], bank(7, 128, 129, SROW)))
                V.tensor_tensor_scan(scan[:, :], seg_start[:, :], bank(6, 0, 512, SROW), carry_col[:, 0:1],
                                     ALU.add, ALU.max).then_inc(S("gat_scanned"), 1)
                dve.wait_ge(S("seg_node_in"), 16 * BLOCKS * (n + 1))
                link(V.tensor_tensor(col(6), seg_node[:, :], col(4), ALU.max))
                link(V.tensor_tensor(col(6), col(6), col(5), ALU.add))
                link(V.scalar_tensor_tensor(out=col(6), in0=col(6), scalar=0.2, in1=col(6),
                                            op0=ALU.mult, op1=ALU.max))
                link(V.tensor_tensor(col(7), col(4), col(5), ALU.add))
                link(V.scalar_tensor_tensor(out=col(7), in0=col(7), scalar=0.2, in1=col(7),
                                            op0=ALU.mult, op1=ALU.max))
                V.tensor_tensor(col(7), col(7), col(6), ALU.subtract).then_inc(S("gat_self_e"), 1)
                mv = adm_parts[:, :].rearrange("p (b a c) -> p b a c", a=3, c=2)
                link(split3(lambda a: mv[:, :, a, 0], col(5), col(9)))
                split3(lambda a: mv[:, :, a, 1], col(6), col(9)).then_inc(S("gat_adm_parts"), 1)

                def gat(o, k, before=n * GROUPS):
                    if live(o, k, 0):
                        g = o * RING + k
                        hots(g, k, "gat_summed", before).then_inc(S("gat_hots"), 1)
                    if live(o, k, 1):
                        g, kk = o * RING + k - 1, k - 1
                        dve.wait_ge(S("gat_expanded"), before + g + 1)
                        reached(dve, S("gat_weight"), before + g - 1)
                        z = wtmp[:, kk % 2 * GS:kk % 2 * GS + GS]
                        ev = bank(2 + kk % 2, 0, 2 * GS).rearrange("p (s c) -> p s c", c=2)
                        V.tensor_tensor(z, as_edge[:, ds(g * GS, GS)], ev[:, :, 0], ALU.add)\
                            .then_inc(S("gat_z"), 1)
                        dve.wait_ge(S("gat_z"), 2 * (before + g) + 1)
                        V.scalar_tensor_tensor(out=z, in0=z, scalar=0.2, in1=z, op0=ALU.mult, op1=ALU.max)\
                            .then_inc(S("gat_z"), 1)
                        dve.wait_ge(S("gat_z"), 2 * (before + g) + 2)
                        V.tensor_tensor(wtmp[:, 16 + kk % 2 * GS:16 + kk % 2 * GS + GS], z, ev[:, :, 1],
                                        ALU.subtract).then_inc(S("gat_logit"), 1)
                    if live(o, k, 3):
                        add_sums("gat", o * RING + k - 3, k - 3, GW, before)

                pipeline(dve, gat, 3)
                dve.wait_ge(S("gat_added"), (n + 1) * STEPS)
                dve.wait_ge(S("gat_self_w"), n + 1)
                sv = acc[:, 0:BLOCKS * GW].rearrange("p (b f) -> p b f", f=GW)
                wide = lambda c: col(c).unsqueeze(2).to_broadcast([P, BLOCKS, F])
                link(V.tensor_tensor(xv(nB[:, :]), hv[:, :, 0:F], wide(8), ALU.mult))
                link(V.tensor_tensor(xv(nB[:, :]), xv(nB[:, :]), sv[:, :, 0:F], ALU.add))
                link(V.tensor_tensor(col(9), sv[:, :, F], col(8), ALU.add))
                link(V.tensor_scalar(col(9), col(9), 1e-16, None, ALU.add))
                link(V.reciprocal(col(7), col(9)))
                link(V.tensor_tensor(xv(nB[:, :]), xv(nB[:, :]), wide(7), ALU.mult))
                dve.wait_ge(S("b3_in"), 16 * (n + 1))
                i = V.tensor_tensor(xv(nB[:, :]), xv(nB[:, :]),
                                    b3_sb[:, :].unsqueeze(1).to_broadcast([P, BLOCKS, F]), ALU.add)
                link(i)
                if n < 2:
                    V.tensor_scalar(nA[:, :], nB[:, :], 0.0, None, ALU.max).then_inc(S("gat_done"), 1)
                else:
                    link(V.tensor_tensor(nA[:, :], X[:, :], nB[:, :], ALU.add))
            layer_norm(3)

        @block.tensor
        def _(pe):
            T = nc.tensor

            def transpose_X(time, src_tile):
                for q, nb in enumerate(XG):
                    if q >= 2:
                        pe.wait_ge(S("xT"), time * len(XG) + q - 1)
                    for s in range(nb):
                        b = 4 * q + s
                        i = T.transpose(bank(q % 2, s * P, (s + 1) * P, F), src_tile[:, b * F:(b + 1) * F],
                                        ident[:, :])
                    i.then_inc(S("xT_psum"), 1)

            pe.wait_ge(S("consts"), 1)
            pe.wait_ge(S("last_block"), 1)
            T.matmul(bank(4, 0, 1, TROW), next_row[:, :], small[0:TROW, 11:12], start=True, stop=True)\
                .then_inc(S("prev_block"), 1)
            pe.wait_ge(S("x_in"), 16)
            transpose_X(0, X)
            pe.wait_ge(S("step_of_tile"), 1)
            for j in range(4):
                i = T.matmul(bank(2, 0, STEPS), tile_no[:, j:j + 1].to_broadcast([TROW, P]),
                             step_of_tile[0:TROW, j * STEPS:(j + 1) * STEPS], start=j == 0, stop=j == 3)
            i.then_inc(S("step_psum"), 1)
            for a in range(4):
                for j in range(4):
                    i = T.matmul(bank(3 + a, 0, STEPS), edge_f[0:TROW, a * 512 + j * P:a * 512 + (j + 1) * P],
                                 step_of_tile[0:TROW, j * STEPS:(j + 1) * STEPS], start=j == 0, stop=j == 3)
                i.then_inc(S("step_psum"), 1)
            pe.wait_ge(S("w_in"), 80)
            pe.wait_ge(S("dst_step"), 1)
            for j in range(4):
                i = T.transpose(bank(6, j * P, (j + 1) * P, SROW),
                                sf[:, 3 * STEPS:4 * STEPS].rearrange("p (q j) -> p j q", j=4)[:, j, :],
                                ident[:, :])
            i.then_inc(S("keys_psum"), 1)
            for q, nb in enumerate(XG):
                pe.wait_ge(S("xT"), q + 1)
                if q >= 2:
                    pe.wait_ge(S("p_staged"), q - 1)
                    pe.wait_ge(S("q_read"), q - 1)
                for s in range(nb):
                    b = 4 * q + s
                    i = T.matmul(bank(2 + q % 2, s * P, (s + 1) * P), XT[:, b * P:(b + 1) * P],
                                 w0_pq_sb[0:F + 1, :], start=True, stop=True)
                i.then_inc(S("pq_psum"), 1)

            def sums(layer, o, k, w, rows, before=0):
                g, kk = o * RING + k - 2, k - 2
                reached(pe, S(f"{layer}_added"), (before + g - 1) * GS)
                for s in range(GS):
                    h = (kk % 5 * GS + s) * P
                    i = T.matmul(bank(4 + kk % 2, s * w, (s + 1) * w), hot_ring[:, h:h + P],
                                 rows(kk, s), start=True, stop=True)
                i.then_inc(S(f"{layer}_summed"), 1)

            def transpose_hots(layer, k, g, before=0):
                reached(pe, S(f"{layer}_hotT"), before + g - 1)
                for s in range(GS):
                    h = (k % 5 * GS + s) * P
                    i = T.transpose(bank(k % 2, s * P, (s + 1) * P), hot_ring[:, h:h + P], ident[:, :])
                i.then_inc(S(f"{layer}_hotT_psum"), 1)

            def blocks_of(g):
                return nc.values_load_multi_w_load_instructions(
                    block_row[0:1, ds(g * GS, GS)], engines=[mybir.EngineType.PE], min_val=0,
                    max_val=BLOCKS - 1,
                    skip_runtime_bounds_check_because="a block number by construction")[1]

            pe.wait_ge(S("q_parts"), 1)
            pe.wait_ge(S("steps_ready"), 1)
            pe.wait_ge(S("keys_staged"), 1)
            T.matmul(bank(6, 0, 226), ident_bf[:, :], zero_bf[:, :], start=True, stop=False,
                     skip_group_check=True)

            def l0(o, k):
                if live(o, k, 2):
                    pe.wait_ge(S("l0_msg"), o * RING + k - 1)
                    sums("l0", o, k, ACC0, lambda kk, s: msg_ring[:, (kk % 5 * GS + s) * ACC0:(kk % 5 * GS + s + 1) * ACC0])
                if live(o, k, 1):
                    g, kk = o * RING + k - 1, k - 1
                    bs = blocks_of(g)
                    pe.wait_ge(S("l0_hotT"), g + 1)
                    reached(pe, S("l0_pre"), g - 1)
                    pe.wait_ge(S(f"attr_in{kk % 5}"), 64 * (2 * o + kk // 5 + 1))
                    for s in range(GS):
                        ps = bank(2 + kk % 2, s * F, (s + 1) * F)
                        e = (kk % 5 * GS + s) * P
                        T.matmul(ps, attr_ring[0:8, e:e + P], w0_attr_sb[0:8, :], start=True, stop=False)
                        for a in range(3):
                            i = T.matmul(ps, hot_T[:, (kk % 2 * GS + s) * P:(kk % 2 * GS + s + 1) * P],
                                         q_parts[:, ds(bs[s] * (3 * F) + a * F, F)], start=False, stop=a == 2)
                    i.then_inc(S("l0_expanded"), 1)
                if live(o, k, 0):
                    g = o * RING + k
                    pe.wait_ge(S("l0_hots"), g + 1)
                    transpose_hots("l0", k, g)
                    for s in range(GS):
                        i = T.matmul(bank(6, 0, 226), src_hot[:, (k % 2 * GS + s) * P:(k % 2 * GS + s + 1) * P],
                                     bucket_hot[:, (k % 2 * GS + s) * 226:(k % 2 * GS + s + 1) * 226],
                                     start=False, stop=False, skip_group_check=True)
                    i.then_inc(S("l0_counted"), 1)

            pipeline(pe, l0, 2)
            T.matmul(bank(6, 0, 226), ident_bf[:, :], zero_bf[:, :], start=False, stop=True,
                     skip_group_check=True).then_inc(S("src_counts"), 1)
            pe.wait_ge(S("degree"), 1)
            T.matmul(bank(7, 0, BLOCKS), upper[:, :], col(12), start=True, stop=True)
            T.matmul(bank(7, 32, 32 + BLOCKS), ones[:, :], col(12), start=True, stop=True)\
                .then_inc(S("degree_psum"), 1)
            pe.wait_ge(S("row_start_in"), 1)
            T.transpose(bank(7, 64, 64 + SROW, 1), tail[:, 1:2], ident[0:SROW, 0:SROW])\
                .then_inc(S("row_start_psum"), 1)
            for q, nb in enumerate(XG):
                if q >= 2:
                    pe.wait_ge(S("sum_T"), q - 1)
                for s in range(nb):
                    b = 4 * q + s
                    i = T.transpose(bank(q % 2, s * P, (s + 1) * P, F + 1),
                                    acc[:, b * ACC0:b * ACC0 + F + 1], ident[:, :])
                i.then_inc(S("sum_T_psum"), 1)
            for q in range(4):
                nb = min(8, BLOCKS - 8 * q)
                pe.wait_ge(S("sum_T"), min(len(XG), 2 * q + 2))
                if q >= 2:
                    pe.wait_ge(S("out0_added"), q - 1)
                for s in range(nb):
                    b = 8 * q + s
                    i = T.matmul(bank(2 + q % 2, s * F, (s + 1) * F), XT[:, b * P:(b + 1) * P],
                                 w0_out_sb[0:F + 1, :], start=True, stop=True)
                i.then_inc(S("out0_psum"), 1)

            pe.wait_ge(S("ln_done"), 1)
            transpose_X(1, X)
            pe.wait_ge(S("xT"), 2 * len(XG))
            pe.wait_ge(S("row_of_ones"), 2)
            for b in range(BLOCKS):
                if b >= 2:
                    pe.wait_ge(S("rel1_read"), b - 1)
                lo = (b % 2) * 3
                for a in range(0, 2 * NREL * F, 512):
                    w = min(512, 2 * NREL * F - a)
                    i = T.matmul(PS[:, lo * 512 + a:lo * 512 + a + w], XT[:, b * P:(b + 1) * P],
                                 w1_sb[0:F + 1, a:a + w], start=True, stop=True)
                i.then_inc(S("rel1_psum"), 1)

            pe.wait_ge(S("ln_done"), 2)
            transpose_X(2, X)
            pe.wait_ge(S("xT"), 3 * len(XG))
            for b in range(BLOCKS):
                if b >= 2:
                    pe.wait_ge(S("rel_staged_v"), b - 1)
                    pe.wait_ge(S("rel_staged_a"), b - 1)
                for a in range(2):
                    i = T.matmul(bank(2 + (b % 2) * 2 + a), XT[0:F, b * P:(b + 1) * P],
                                 w2_sb[0:F, a * 512:(a + 1) * 512], start=True, stop=True)
                i.then_inc(S("rel_psum"), 1)
            pe.wait_ge(S("arena_free"), 1)

            def l2(o, k):
                if live(o, k, 2):
                    kk = k - 2
                    pe.wait_ge(S(f"rows_in{kk % RING}"), 64 * (OUTER + o + kk // RING + 1))
                    sums("l2", o, k, F, lambda kk, s: rows_ring[:, (kk % RING * GS + s) * GW:(kk % RING * GS + s) * GW + F])
                if live(o, k, 0):
                    g = o * RING + k
                    pe.wait_ge(S("l2_hots"), g + 1)
                    reached(pe, S("l2_srcT"), g - 1)
                    for s in range(GS):
                        i = T.transpose(bank(k % 2).bitcast(bf16)[:, s * P:(s + 1) * P],
                                        hot_T[:, (k % 2 * GS + s) * P:(k % 2 * GS + s + 1) * P], ident_bf[:, :])
                    i.then_inc(S("l2_srcT_psum"), 1)

            pipeline(pe, l2, 2)
            pe.wait_ge(S("l2_srcT"), GROUPS)

            for n in range(3):
                pe.wait_ge(S("w3_in"), 48 * (n + 1))
                pe.wait_ge(S("ln_done") if n == 0 else S("gat_done"), 3 if n == 0 else n)
                T.matmul(bank(7, 0, 2, F), w3T_sb[:, :], a3_sb[:, :], start=True, stop=True)\
                    .then_inc(S("gat_wa_psum"), 1)
                transpose_X(3 + n, X if n == 0 else nA)
                pe.wait_ge(S("gat_wa"), n + 1)
                for q, nb in enumerate(XG):
                    pe.wait_ge(S("xT"), (3 + n) * len(XG) + q + 1)
                    if q >= 2:
                        pe.wait_ge(S("gat_h"), n * len(XG) + q - 1)
                    for s in range(nb):
                        b = 4 * q + s
                        i = T.matmul(bank(2 + q % 2, s * (F + 2), (s + 1) * (F + 2)),
                                     XT[0:F, b * P:(b + 1) * P], w3_sb[:, :], start=True, stop=True)
                    i.then_inc(S("gat_h_psum"), 1)
                pe.wait_ge(S("gat_h_psum"), (n + 1) * len(XG))
                pe.sem_inc(S("weights_free"), 1)
                pe.wait_ge(S("gat_as_parts"), n + 1)

                def look_up(o, k, before=n * GROUPS):
                    if live(o, k, 0):
                        g = o * RING + k
                        reached(pe, S("gat_picked"), before + g - 1)
                        for s in range(GS):
                            for a in range(3):
                                i = T.matmul(bank(4 + k % 2, s * BLOCKS, (s + 1) * BLOCKS),
                                             src_hot_T[:, ds((g * GS + s) * P, P)],
                                             as_parts[:, a * BLOCKS:(a + 1) * BLOCKS], start=a == 0, stop=a == 2)
                        i.then_inc(S("gat_as_psum"), 1)

                pipeline(pe, look_up, 0)
                pe.wait_ge(S("gat_picked"), (n + 1) * GROUPS)
                for j in range(4):
                    i = T.transpose(bank(6, j * P, (j + 1) * P, SROW),
                                    as_edge[:, :].rearrange("p (q j) -> p j q", j=4)[:, j, :], ident[:, :])
                i.then_inc(S("gat_asT_psum"), 1)
                pe.wait_ge(S("gat_scan1"), n + 1)
                T.transpose(bank(7, 0, SROW, 1), scan[:, 511:512], ident[0:SROW, 0:SROW])\
                    .then_inc(S("gat_tail_psum"), 1)
                pe.wait_ge(S("gat_carry"), n + 1)
                T.matmul(bank(7, 128, 129, SROW), carry[0:1, 0:SROW], ones[0:1, 0:1], start=True, stop=True)\
                    .then_inc(S("gat_carry_psum"), 1)
                pe.wait_ge(S("gat_adm_parts"), n + 1)

                def gat(o, k, before=n * GROUPS):
                    if live(o, k, 2):
                        pe.wait_ge(S("gat_scaled"), before + o * RING + k - 1)
                        sums("gat", o, k, GW, lambda kk, s: msg_ring[:, (kk % 5 * GS + s) * ACC0:(kk % 5 * GS + s) * ACC0 + GW], before)
                    if live(o, k, 1):
                        g, kk = o * RING + k - 1, k - 1
                        bs = blocks_of(g)
                        pe.wait_ge(S("gat_hotT"), before + g + 1)
                        reached(pe, S("gat_logit"), before + g - 1)
                        for s in range(GS):
                            for a in range(3):
                                i = T.matmul(bank(2 + kk % 2, 2 * s, 2 * s + 2),
                                             hot_T[:, (kk % 2 * GS + s) * P:(kk % 2 * GS + s + 1) * P],
                                             adm_parts[:, ds(bs[s] * 6 + 2 * a, 2)], start=a == 0, stop=a == 2)
                        i.then_inc(S("gat_expanded"), 1)
                    if live(o, k, 0):
                        g = o * RING + k
                        pe.wait_ge(S("gat_hots"), before + g + 1)
                        transpose_hots("gat", k, g, before)

                pipeline(pe, gat, 2)


_INS = ["x", "ints", "attr_t", "w0_pq", "w0_attr", "w0_out", "w1", "w2", "w3", "w3_t", "a3", "b3"]


def laid_out(inputs):
    import numpy as np
    f = lambda n: np.asarray(inputs[n])
    f32, i32 = np.float32, np.int32
    padded = lambda a, v: np.concatenate([a, np.full(EP - E, v, i32)])
    return {
        "x": np.concatenate([f("x"), np.zeros((NP_ - N, F), f32)]),
        "ints": np.stack([padded(f("src"), NP_ - 1), padded(f("dst"), NP_ - 1),
                          padded(f("edge_type_16"), 0), padded(f("edge_type_9"), 0)]),
        "attr_t": np.ascontiguousarray(np.concatenate([f("edge_attr_8"), np.zeros((EP - E, 8), f32)]).T),
        "w0_pq": np.concatenate([
            np.concatenate([f("L0_gnn_W1")[0:F], f("L0_gnn_W1")[F:2 * F]], axis=1),
            np.concatenate([np.zeros(F, f32), f("L0_gnn_b1")])[None]]),
        "w0_attr": np.ascontiguousarray(f("L0_gnn_W1")[2 * F:]),
        "w0_out": np.concatenate([f("L0_gnn_W2"), f("L0_gnn_b2")[None]]),
        "w1": np.concatenate([f("L1_gnn_weights").transpose(0, 2, 1, 3).reshape(3, F, 2 * NREL * F),
                              f("L1_gnn_biases").reshape(3, 1, 2 * NREL * F)], axis=1),
        "w2": np.ascontiguousarray(f("L2_gnn_weight").transpose(1, 0, 2).reshape(F, NTYPE * F)),
        "w3": np.stack([f(f"L3_gnn_W{n}") for n in (1, 2, 3)]),
        "w3_t": np.ascontiguousarray(np.stack([f(f"L3_gnn_W{n}").T for n in (1, 2, 3)])),
        "a3": np.ascontiguousarray(np.stack([np.stack([f(f"L3_gnn_a{n}s"), f(f"L3_gnn_a{n}d")], axis=1)
                                             for n in (1, 2, 3)])),
        "b3": np.stack([f(f"L3_gnn_b{n}")[None] for n in (1, 2, 3)]),
    }


def kernel(**inputs):
    import concourse.bacc as bacc
    from concourse.bass_utils import run_bass_kernel_spmd

    nc = bacc.Bacc("TRN2", target_bir_lowering=False, num_devices=1)
    arrays = laid_out(inputs)
    args = [nc.dram_tensor(f"in_{n}", arrays[n].shape, mybir.dt.from_np(arrays[n].dtype),
                           kind="ExternalInput").ap() for n in _INS]
    out = nc.dram_tensor("out", (N, F), mybir.dt.float32, kind="ExternalOutput").ap()
    gnn_kernel(nc, *args, out)
    r = run_bass_kernel_spmd(nc, [{f"in_{n}": arrays[n] for n in _INS}], core_ids=[0])
    return r.results[0]["out"]
```

```python
import concourse.bass as bass
from concourse import mybir
from contextlib import ExitStack

N, F, E, NREL, NTYPE = 3125, 64, 53125, 9, 16
P = 128
BLOCKS = -(-N // P)
NP_ = BLOCKS * P
TILES = -(-E // P)
EP = TILES * P
STEPS = TILES + BLOCKS - 1
TROW = TILES // 4
SROW = STEPS // 4
GS = 4
GROUPS = STEPS // GS
RING = 20
START = RING - GROUPS % RING
OUTER = (START + GROUPS) // RING
HOTS = 10
OWN_ROWS = 11
BATCH = 5 * GS
BATCHES = STEPS // BATCH
SPAN = 5 * GS
FRONT = 8 * GS
ACC0 = F + 1 + NREL
GW = F + 1
BIG = 1e30
EPS = 1e-5


def gnn_kernel(nc, x, ints, attr_t, w0_pq, w0_attr, w0_out, w1, w2, w3, w3_t, a3, b3, out):
    fp32, bf16, i32 = mybir.dt.float32, mybir.dt.bfloat16, mybir.dt.int32
    ALU, ACT, AX = mybir.AluOpType, mybir.ActivationFunctionType, mybir.AxisListType
    ds = bass.ds

    src_rows = nc.dram_tensor("src_rows", [NP_, F], fp32).ap()
    rel_rows = nc.dram_tensor("rel_rows", [NP_ * NTYPE, F], fp32).ap()
    gat_rows = [nc.dram_tensor(f"gat_rows{n}", [NP_, F], fp32).ap() for n in range(3)]
    keys = nc.dram_tensor("keys", [STEPS * P + 1, 1], fp32).ap()
    attr_parts = nc.dram_tensor("attr_parts", [3 * 8, EP], bf16).ap()
    seg_max = nc.dram_tensor("seg_max", [STEPS * P + 1, 1], fp32).ap()

    ctx = ExitStack()
    with ctx:
        def sb(name, shape, dt=fp32):
            return ctx.enter_context(nc.sbuf_tensor(name, shape, dt))

        sems = {}

        def S(name):
            if name not in sems:
                sems[name] = ctx.enter_context(nc.semaphore(name))
            return sems[name]

        arena = sb("arena", [P, STEPS * P // 2])
        src_hot_T = arena[:, :].bitcast(bf16)
        at = [0]

        def carve(cols):
            a = arena[:, at[0]:at[0] + cols]
            at[0] += cols
            assert at[0] <= STEPS * P // 2
            return a

        ints_sb = carve(4 * 512).bitcast(i32)
        edge_f = carve(4 * 512)
        step_of_tile = carve(4 * STEPS)
        itmp = carve(4 * 512).bitcast(i32)
        q_parts = carve(BLOCKS * 3 * F // 2).bitcast(bf16)
        attr_ring = carve(5 * GS * P // 2).bitcast(bf16)
        w1_sb = carve(2 * NREL * F)
        w2_sb = carve(NTYPE * F)
        work = carve(2 * 2 * NREL * F + 2 * NTYPE * F)
        relprod = work[:, 0:4 * NREL * F]
        rel_stage = work[:, 4 * NREL * F:]
        attr_half = work[:, 0:EP // 32]
        attr_split = work[:, EP // 32:EP // 32 * 5 // 2].bitcast(bf16)
        src_hot = carve(2 * GS * P // 2).bitcast(bf16)
        bucket_hot = carve(2 * GS * 226 // 2).bitcast(bf16)
        w0_pq_sb = carve(2 * F)
        w0_attr_sb = carve(F)
        w0_attr_parts = carve(3 * F // 2).bitcast(bf16)
        w0_out_sb = carve(F)
        sf = carve(4 * STEPS)
        type9 = carve(STEPS)
        bucket = carve(STEPS // 2).bitcast(bf16)
        tile_row = carve(FRONT + STEPS + SPAN)[0:1, :].bitcast(i32)
        counts = carve(BLOCKS * 2 * NREL)
        upper = carve(P)
        next_row = carve(TROW)[0:TROW, :]
        iota = carve(STEPS)

        lane = sb("lane", [P, P])
        zero_bf = sb("zero_bf", [P, GS * ACC0], bf16)
        iota_bf = sb("iota_bf", [P, 226], bf16)
        ident = sb("ident", [P, P])
        ident_bf = sb("ident_bf", [P, P], bf16)
        ones = sb("ones", [P, P])
        tile_no = sb("tile_no", [TROW, 4])
        node_base = sb("node_base", [P, BLOCKS])
        small = sb("small", [P, 64])
        node_loc = sb("node_loc", [P, STEPS])
        src_lo = sb("src_lo", [P, STEPS], bf16)
        src_hi = sb("src_hi", [P, STEPS])
        src_idx = sb("src_idx", [P, STEPS + RING * GS], i32)
        rel_idx = sb("rel_idx", [P, STEPS + RING * GS], i32)
        slot_row = sb("slot_row", [1, FRONT + STEPS + SPAN], i32)
        first_row = sb("first_row", [1, 8 + GROUPS + 8], i32)
        block_row = sb("block_row", [1, FRONT + STEPS + SPAN], i32)
        seg_start = sb("seg_start", [SROW, 512])
        row_start = sb("row_start", [1, SROW])
        end_idx = sb("end_idx", [P, BLOCKS], i32)
        X = sb("X", [P, BLOCKS * F])
        xt_area = sb("xt_area", [P, NP_])
        XT = xt_area[0:F + 1, :]
        parts = xt_area[:, :].bitcast(bf16)
        acc = sb("acc", [P, (BLOCKS + GS - 1) * ACC0])
        node_h = sb("node_h", [P, BLOCKS * (F + 2)])
        nA = sb("nA", [P, BLOCKS * F])
        nB = sb("nB", [P, BLOCKS * F])
        picked = nB[:, 0:2 * BATCH * BLOCKS]
        c25 = sb("c25", [P, 16 * BLOCKS])
        idx_ring = sb("idx_ring", [P, RING * GS], i32)
        rows_ring = sb("rows_ring", [P, OWN_ROWS * GS * F])
        hot_ring = sb("hot_ring", [P, HOTS * GS * P], bf16)
        hot_T = sb("hot_T", [P, 2 * GS * P], bf16)
        as_edge = sb("as_edge", [P, STEPS])
        wtmp = sb("wtmp", [P, 4 * 2 * GS])
        scan = sb("scan", [SROW, 512])
        carry = sb("carry", [1, SROW + 1])
        carry_col = sb("carry_col", [SROW, 1])
        tail = sb("tail", [SROW, 2])
        seg_node = sb("seg_node", [P, BLOCKS])
        as_parts = sb("as_parts", [P, 3 * BLOCKS], bf16)
        adm_parts = sb("adm_parts", [P, BLOCKS * 6], bf16)
        w3_sb = sb("w3_sb", [F, F + 2])
        w3T_sb = sb("w3T_sb", [F, F])
        a3_sb = sb("a3_sb", [F, 2])
        b3_sb = sb("b3_sb", [P, F])

        node_loc_bf = sb("node_loc_bf", [P, STEPS], bf16)
        PS = ctx.enter_context(nc.psum_tensor("PS", [P, 8 * 512], fp32))

        def bank(n, a=0, b=512, p=P):
            return PS[0:p, n * 512 + a:n * 512 + b]

        def part(k, a, w=ACC0):
            v = parts[:, k % 5 * GS * 3 * ACC0:(k % 5 + 1) * GS * 3 * ACC0]
            return v.rearrange("p (s a f) -> p s a f", s=GS, a=3)[:, :, a, 0:w]

        PARTS = 5 * GS * 3 * ACC0 // 2

        def row_slot(k):
            n = (k - START) % RING
            for area, first, count in ((rows_ring[:, :], 0, OWN_ROWS), (nA[:, :], OWN_ROWS, 6),
                                       (xt_area[:, PARTS:], OWN_ROWS + 6, 3)):
                if n < first + count:
                    return area[:, (n - first) * GS * F:(n - first + 1) * GS * F]

        def rows_in_slot(k):
            return row_slot(k).rearrange("p (s f) -> p s f", f=F)

        def group_no(o, k):
            return o * RING + k - START

        def rows_in_count(layer, o, k):
            late = k % RING >= START
            return 64 * (layer * (OUTER if late else OUTER - 1) + o + k // RING + late)

        def scaled_rows(k):
            v = nB[:, k % 5 * GS * GW:(k % 5 + 1) * GS * GW]
            return v.rearrange("p (s f) -> p s f", f=GW)

        def xv(t, w=F):
            return t.rearrange("p (b f) -> p b f", f=w)

        def col(n, k=1):
            return c25[:, n * BLOCKS:(n + k) * BLOCKS]

        LAYERS = ["l0", "l2", "g0", "g1", "g2"]
        XG = [min(4, BLOCKS - 4 * q) for q in range(-(-BLOCKS // 4))]

        def pipeline(eng, iteration, lag):
            for k in range(START, RING):
                iteration(0, k)
            with eng.Fori(1, OUTER) as o:
                for k in range(RING):
                    iteration(o, k)
            for k in range(lag):
                iteration(OUTER, k)

        def live(o, k, lag):
            return not isinstance(o, int) or 0 <= group_no(o, k) - lag < GROUPS

        def row_values(row, engine, most, per=GS, front=FRONT):
            held = {}

            def values(o, k, lag):
                if k % 5 == 0:
                    held["now"] = nc.values_load_multi_w_load_instructions(
                        row[0:1, ds((group_no(o, k) - lag) * per + front, 5 * per)], engines=[engine],
                        min_val=0, max_val=most,
                        skip_runtime_bounds_check_because="tile and block numbers by construction")[1]
                return held["now"][k % 5 * per:(k % 5 + 1) * per]
            return values

        def reached(eng, sem, value):
            if not isinstance(value, int) or value > 0:
                eng.wait_ge(sem, value)

        block = ctx.enter_context(nc.Block())

        @block.sync
        def _(sp):
            sp.dma_start(ints_sb[0:TROW, :].rearrange("q (a f) -> q a f", a=4),
                         ints.rearrange("a (q f) -> q a f", q=TROW)).then_inc(S("ints_in"), 16)
            halves = attr_t.rearrange("a (q f) -> (a q) f", q=16).rearrange("p (h f) -> p h f", h=2)
            scratch = attr_parts.rearrange("(a r) (q f) -> (r q) a f", a=3, q=16)
            sp.dma_start(attr_half, halves[:, 0, :]).then_inc(S("attr_half_in"), 16)
            sp.dma_start(xv(X[:, :]), x.rearrange("(b p) f -> p b f", p=P)).then_inc(S("x_in"), 16)
            for dst, s in ((w0_pq_sb[0:F + 1, :], w0_pq), (w0_attr_sb[0:8, :], w0_attr),
                           (w0_attr_sb[8:16, :], w0_attr), (w0_attr_sb[16:24, :], w0_attr),
                           (w0_out_sb[0:F + 1, :], w0_out), (w1_sb[0:F + 1, :], w1[2]),
                           (w2_sb[0:F, :], w2)):
                sp.dma_start(dst, s).then_inc(S("w_in"), 16)
            sp.wait_ge(S("p_staged"), len(XG))
            sp.dma_start(src_rows.rearrange("(b p) f -> p b f", p=P),
                         xv(node_h[:, 0:BLOCKS * F])).then_inc(S("l0_table"), 16)
            sp.wait_ge(S("keys_staged"), 1)
            sp.dma_start(keys[0:1, :], small[0:1, 0:1]).then_inc(S("keys_out"), 16)
            sp.dma_start(keys[1:STEPS * P + 1, :].rearrange("(q f) o -> q (f o)", q=SROW),
                         scan[:, :]).then_inc(S("keys_out"), 16)
            sp.dma_start(seg_max[STEPS * P:STEPS * P + 1, :], small[0:1, 1:2]).then_inc(S("keys_out"), 16)
            sp.wait_ge(S("keys_out"), 48)
            sp.dma_start(seg_start[:, :], keys[0:STEPS * P, :].rearrange("(q f) o -> q (f o)", q=SROW))\
              .then_inc(S("prev_key"), 16)

            for h in range(2):
                sp.wait_ge(S("attr_split"), h + 1)
                w = EP // 32
                sp.dma_start(scratch[:, :, h * w:(h + 1) * w],
                             attr_split.rearrange("p (a f) -> p a f", a=3)).then_inc(S("attr_out"), 16)
                if h == 0:
                    sp.wait_ge(S("attr_out"), 16)
                    sp.dma_start(attr_half, halves[:, 1, :]).then_inc(S("attr_half_in"), 16)
            sp.wait_ge(S("attr_out"), 32)
            tile_of = row_values(tile_row, mybir.EngineType.SP, TILES - 1)

            def attrs(o, k):
                tiles = tile_of(o, k, 0)
                reached(sp, S("l0_expanded"), group_no(o, k) - 4)
                for s in range(GS):
                    sp.dma_start(attr_ring[0:24, (k % 5 * GS + s) * P:(k % 5 * GS + s + 1) * P],
                                 attr_parts[:, ds(tiles[s] * P, P)]).then_inc(S(f"attr_in{k % 5}"), 16)

            sp.wait_ge(S("steps_ready"), 1)
            pipeline(sp, attrs, 0)

            for b in range(BLOCKS):
                sp.wait_ge(S("rel_staged_v"), b + 1)
                sp.wait_ge(S("rel_staged_a"), b + 1)
                sp.dma_start(rel_rows.rearrange("(n r) f -> n (r f)", r=NTYPE)[b * P:(b + 1) * P, :],
                             rel_stage[:, (b % 2) * 1024:(b % 2 + 1) * 1024])\
                  .then_inc(S(f"l2_table{b % 2}"), 16)

            for n in range(3):
                if n:
                    sp.wait_ge(S("weights_free"), n)
                sp.dma_start(w3_sb[:, 0:F], w3[n]).then_inc(S("w3_in"), 16)
                sp.dma_start(w3T_sb[:, :], w3_t[n]).then_inc(S("w3_in"), 16)
                sp.dma_start(a3_sb[:, :], a3[n]).then_inc(S("w3_in"), 16)
                if n:
                    sp.wait_ge(S("gat_done"), n)
                sp.dma_start(b3_sb[:, :], b3[n].to_broadcast([P, F]))\
                  .then_inc(S("b3_in"), 16)
                sp.wait_ge(S("gat_h"), (n + 1) * len(XG))
                sp.dma_start(gat_rows[n].rearrange("(b p) f -> p b f", p=P),
                             xv(node_h[:, :], F + 2)[:, :, 0:F]).then_inc(S("gat_table"), 16)
                sp.wait_ge(S("gat_scanned"), n + 1)
                sp.dma_start(seg_max[0:STEPS * P, :].rearrange("(q f) o -> q (f o)", q=SROW),
                             scan[:, :]).then_inc(S("seg_max_out"), 16)
            sp.wait_ge(S("ln_done"), 4)
            full = N // P
            sp.dma_start(out[0:full * P, :].rearrange("(b p) f -> p b f", p=P),
                         xv(X[:, 0:full * F])).then_inc(S("out_done"), 16)
            sp.dma_start(out[full * P:N, :], X[0:N - full * P, full * F:BLOCKS * F]).then_inc(S("out_done"), 16)
            sp.wait_ge(S("out_done"), 32)

        @block.gpsimd
        def _(pool):
            pool.iota(iota, [[1, STEPS]], base=0, channel_multiplier=0,
                      allow_small_or_imprecise_dtypes=True)
            pool.iota(lane[:, :], [[1, P]], base=0, channel_multiplier=0,
                      allow_small_or_imprecise_dtypes=True)
            pool.iota(iota_bf[:, :], [[1, 226]], base=0, channel_multiplier=0,
                      allow_small_or_imprecise_dtypes=True)
            pool.iota(tile_no[:, :], [[1, 4]], base=0, channel_multiplier=4,
                      allow_small_or_imprecise_dtypes=True)
            pool.iota(node_base[:, :], [[P, BLOCKS]], base=-1, channel_multiplier=0,
                      allow_small_or_imprecise_dtypes=True)
            pool.memset(ident[:, :], 0.0)
            pool.memset(ident_bf[:, :], 0.0)
            pool.memset(next_row, 0.0)
            pool.memset(ones[:, :], 1.0)
            pool.memset(upper[:, :], 1.0).then_inc(S("filled"), 1)
            pool.wait_ge(S("filled"), 1)
            for m in (ident, ident_bf):
                pool.affine_select(out=m[:, :], in_=m[:, :], compare_op=ALU.not_equal, fill=1.0,
                                   base=0, pattern=[[-1, P]], channel_multiplier=1)
            pool.affine_select(out=next_row, in_=next_row, compare_op=ALU.not_equal,
                               fill=1.0, base=1, pattern=[[-1, TROW]], channel_multiplier=1)
            pool.affine_select(out=upper[:, :], in_=upper[:, :], compare_op=ALU.is_ge, fill=0.0,
                               base=0, pattern=[[1, P]], channel_multiplier=-1).then_inc(S("consts"), 1)
            pool.wait_ge(S("consts"), 1)
            pool.memset(xt_area[F:F + 1, :], 1.0).then_inc(S("row_of_ones"), 1)
            pool.wait_ge(S("row_of_ones"), 1)
            pool.memset(zero_bf[:, :], 0.0)
            pool.memset(src_idx[:, STEPS:], 0)
            pool.memset(rel_idx[:, STEPS:], 0)
            for row in (block_row, tile_row, slot_row):
                pool.memset(row[:, 0:FRONT], 0)
                pool.memset(row[:, FRONT + STEPS:], 0)
            pool.memset(first_row[:, 0:8], 0)
            pool.memset(first_row[:, 8 + GROUPS:], 0)
            pool.memset(small[:, 0:1], -1.0)
            pool.memset(small[:, 1:2], -BIG)
            pool.memset(small[:, 2:3], EPS)
            pool.memset(carry[:, :], -BIG).then_inc(S("presets"), 1)

            def gathers(li, table, freed, before=0):

                def group(o, k):
                    if not isinstance(o, int) or group_no(o, k) >= RING:
                        reached(pool, S(freed), before + group_no(o, k) - RING + 1)
                        pool.sem_inc(S("slot_free"), 1)
                        pool.wait_ge(S("idx_staged"), li * (GROUPS + 1) + 2 + group_no(o, k) - RING)
                        pool.sem_inc(S("slot_free"), 1)
                    for s in range(GS):
                        c = k * GS + s
                        pool.indirect_dma_start(
                            row_slot(k)[:, s * F:(s + 1) * F], None, table,
                            bass.IndirectOffsetOnAxis(ap=idx_ring[:, c:c + 1], axis=0))\
                            .then_inc(S(f"rows_in{k}"), 16)

                pool.wait_ge(S("idx_staged"), li * (GROUPS + 1) + 1)
                for n in range(RING):
                    if li == 0 and n == OWN_ROWS:
                        pool.wait_ge(S("q_parts"), 1)
                    group((n + START) // RING, (n + START) % RING)
                return group

            def rest(group):
                for k in range(START, RING):
                    group(1, k)
                with pool.Fori(2, OUTER) as o:
                    for k in range(RING):
                        group(o, k)

            pool.wait_ge(S("presets"), 1)
            pool.wait_ge(S("steps_ready"), 1)
            pool.wait_ge(S("l0_table"), 16)
            pool.wait_ge(S("pq_psum"), len(XG))
            for k in range(5):
                pool.memset(part(k, 0)[:, :, F:F + 1], 1.0)
            pool.memset(small[:, 3:4], 0.0).then_inc(S("count_column"), 1)
            rest(gathers(0, src_rows, "l0_pre"))
            pool.wait_ge(S("out0_psum"), 4)
            pool.memset(xt_area[F:F + 1, :], 1.0).then_inc(S("row_of_ones"), 1)
            pool.wait_ge(S("l2_table0"), 16 * (BLOCKS - BLOCKS // 2))
            pool.wait_ge(S("l2_table1"), 16 * (BLOCKS // 2))
            rest(gathers(1, rel_rows, "l2_parts"))
            for n in range(3):
                pool.wait_ge(S("gat_table"), 16 * (n + 1))
                parts = gathers(2 + n, gat_rows[n], "gat_scaled", n * GROUPS)
                pool.wait_ge(S("seg_max_out"), 16 * (n + 1))
                for b in range(BLOCKS):
                    pool.indirect_dma_start(
                        seg_node[:, b:b + 1], None, seg_max,
                        bass.IndirectOffsetOnAxis(ap=end_idx[:, b:b + 1], axis=0))\
                        .then_inc(S("seg_node_in"), 16)
                rest(parts)

        @block.scalar
        def _(act):
            A = nc.scalar

            def copy_XT(time):
                for q, nb in enumerate(XG):
                    act.wait_ge(S("xT_psum"), time * len(XG) + q + 1)
                    A.activation(XT[0:F, q * 512:q * 512 + nb * P], bank(q % 2, 0, nb * P, F), ACT.Copy)\
                        .then_inc(S("xT"), 1)

            def ln_sqrt(n):
                act.wait_ge(S("ln_var"), n + 1)
                A.activation(col(2), col(1), ACT.Sqrt, bias=small[:, 2:3], scale=1.0 / F)\
                    .then_inc(S("ln_std"), 1)

            def first_indices(idx):
                A.activation(idx_ring[:, START * GS:], idx[:, 0:(RING - START) * GS], ACT.Copy)
                A.activation(idx_ring[:, 0:START * GS], idx[:, (RING - START) * GS:RING * GS], ACT.Copy)\
                    .then_inc(S("idx_staged"), 1)

            def next_indices(idx, o, k, lag, li):
                g, kk = group_no(o, k) - lag, (k - lag) % RING
                act.wait_ge(S(f"rows_in{kk}"), rows_in_count(li, o, k - lag))
                A.activation(idx_ring[:, kk * GS:(kk + 1) * GS], idx[:, ds((g + RING) * GS, GS)], ACT.Copy)\
                    .then_inc(S("idx_staged"), 1)

            act.wait_ge(S("presets"), 1)
            copy_XT(0)
            for q, nb in enumerate(XG):
                act.wait_ge(S("q_read"), q + 1)
                A.activation(xv(node_h[:, q * 4 * F:(q * 4 + nb) * F]),
                             xv(bank(2 + q % 2, 0, nb * P), P)[:, :, 0:F], ACT.Copy)\
                    .then_inc(S("p_staged"), 1)

            def first_part(layer, k, lag, value, before, g, func=ACT.Copy, w=F):
                reached(act, S(f"{layer}_summed"), before + g - 4)
                A.activation(part(k - lag, 0, w), value, func).then_inc(S(f"{layer}_part0"), 1)

            def second_part(layer, k, lag, rest, before, g, w=F):
                act.wait_ge(S(f"{layer}_rest"), before + g + 1)
                A.activation(part(k - lag, 1, w), rest, ACT.Copy).then_inc(S(f"{layer}_part1"), 1)

            w = EP // 32
            for h in range(2):
                act.wait_ge(S("attr_half_in"), 16 * (h + 1))
                A.activation(attr_split[:, 0:w], attr_half, ACT.Copy).then_inc(S("attr_part0"), 1)
                act.wait_ge(S("attr_rest"), h + 1)
                A.activation(attr_split[:, w:2 * w], attr_half, ACT.Copy).then_inc(S("attr_part1"), 1)

            act.wait_ge(S("steps_ready"), 1)
            first_indices(src_idx)

            def l0(o, k):
                if live(o, k, 0):
                    g = group_no(o, k)
                    act.wait_ge(S("l0_hotT_psum"), g + 1)
                    reached(act, S("l0_expanded"), g - 1)
                    A.activation(hot_T[:, k % 2 * 512:k % 2 * 512 + 512],
                                 bank(k % 2).bitcast(bf16)[:, 0:512], ACT.Copy).then_inc(S("l0_hotT"), 1)
                if live(o, k, 2):
                    g = group_no(o, k) - 2
                    act.wait_ge(S("l0_pre"), g + 1)
                    first_part("l0", k, 2, xv(nB[:, (k - 2) % 5 * 256:(k - 2) % 5 * 256 + 256]), 0, g, ACT.Relu)
                    next_indices(src_idx, o, k, 2, 0)
                if live(o, k, 3):
                    second_part("l0", k, 3, xv(nB[:, (k - 3) % 5 * 256:(k - 3) % 5 * 256 + 256]), 0, group_no(o, k) - 3)

            pipeline(act, l0, 3)
            for q, nb in enumerate(XG):
                act.wait_ge(S("sum_T_psum"), q + 1)
                A.activation(XT[0:F + 1, q * 512:q * 512 + nb * P], bank(q % 2, 0, nb * P, F + 1), ACT.Copy)\
                    .then_inc(S("sum_T"), 1)
            ln_sqrt(0)
            copy_XT(1)
            ln_sqrt(1)
            copy_XT(2)
            for b in range(BLOCKS):
                act.wait_ge(S("rel_psum"), b + 1)
                if b >= 2:
                    act.wait_ge(S(f"l2_table{b % 2}"), 16 * (b // 2))
                A.activation(rel_stage[:, (b % 2) * 1024 + 512:(b % 2 + 1) * 1024],
                             bank(2 + (b % 2) * 2 + 1), ACT.Copy).then_inc(S("rel_staged_a"), 1)

            first_indices(rel_idx)

            def l2(o, k):
                if live(o, k, 0):
                    g = group_no(o, k)
                    if isinstance(o, int) and o == 0 and k == 0:
                        act.wait_ge(S("l2_table0"), 16 * (BLOCKS - BLOCKS // 2))
                        act.wait_ge(S("l2_table1"), 16 * (BLOCKS // 2))
                        act.wait_ge(S("arena_free"), 1)
                    act.wait_ge(S("l2_srcT_psum"), g + 1)
                    A.activation(src_hot_T[:, ds(g * GS * P, GS * P)],
                                 bank(k % 2).bitcast(bf16)[:, 0:GS * P], ACT.Copy)\
                        .then_inc(S("l2_srcT"), 1)
                if live(o, k, 2):
                    next_indices(rel_idx, o, k, 2, 1)
                    first_part("l2", k, 2, rows_in_slot(k - 2), 0, group_no(o, k) - 2)
                if live(o, k, 3):
                    second_part("l2", k, 3, rows_in_slot(k - 3), 0, group_no(o, k) - 3)

            pipeline(act, l2, 3)
            ln_sqrt(2)

            for n in range(3):
                copy_XT(3 + n)
                act.wait_ge(S("gat_wa_psum"), n + 1)
                A.activation(w3_sb[:, F:F + 2], bank(7, 0, 2, F), ACT.Copy).then_inc(S("gat_wa"), 1)
                for q, nb in enumerate(XG):
                    act.wait_ge(S("gat_h_psum"), n * len(XG) + q + 1)
                    A.activation(xv(node_h[:, q * 4 * (F + 2):(q * 4 + nb) * (F + 2)], F + 2),
                                 xv(bank(2 + q % 2, 0, nb * (F + 2)), F + 2), ACT.Copy)\
                        .then_inc(S("gat_h"), 1)
                first_indices(src_idx)
                act.wait_ge(S("gat_self_e"), n + 1)
                A.activation(col(8), col(7), ACT.Exp).then_inc(S("gat_self_w"), 1)

                def gat(o, k, n=n, before=n * GROUPS):
                    if live(o, k, 0):
                        g = group_no(o, k)
                        act.wait_ge(S("gat_hotT_psum"), before + g + 1)
                        reached(act, S("gat_expanded"), before + g - 1)
                        A.activation(hot_T[:, k % 2 * 512:k % 2 * 512 + 512],
                                     bank(k % 2).bitcast(bf16)[:, 0:512], ACT.Copy).then_inc(S("gat_hotT"), 1)
                    if live(o, k, 2):
                        g, kk = group_no(o, k) - 2, k - 2
                        act.wait_ge(S("gat_logit"), before + g + 1)
                        reached(act, S("gat_parts"), before + g - 4)
                        w = scaled_rows(kk)[:, :, F]
                        A.activation(w, wtmp[:, 16 + kk % 2 * GS:16 + kk % 2 * GS + GS], ACT.Exp)\
                            .then_inc(S("gat_weight"), 1)
                        act.wait_ge(S("gat_weight"), before + g + 1)
                        act.wait_ge(S(f"rows_in{kk % RING}"), rows_in_count(2 + n, o, kk))
                        for s in range(GS):
                            i = A.activation(scaled_rows(kk)[:, s, 0:F], rows_in_slot(kk)[:, s, :],
                                             ACT.Copy, scale=w[:, s:s + 1])
                        i.then_inc(S("gat_scaled"), 1)
                        next_indices(src_idx, o, k, 2, 2 + n)
                        act.wait_ge(S("gat_scaled"), before + g + 1)
                        first_part("gat", k, 2, scaled_rows(kk), before, g, w=GW)
                    if live(o, k, 3):
                        second_part("gat", k, 3, scaled_rows(k - 3), before, group_no(o, k) - 3, w=GW)

                pipeline(act, gat, 3)
            ln_sqrt(3)

        @block.vector
        def _(dve):
            V = nc.vector
            n_linked = [0]

            def link(ins):
                n_linked[0] += 1
                ins.then_inc(S("dve_chain"), 1)
                dve.wait_ge(S("dve_chain"), n_linked[0])

            dve.wait_ge(S("ints_in"), 16)
            dve.wait_ge(S("presets"), 1)
            src_i, dst_i, t16_i, t9_i = (ints_sb[0:TROW, a * 512:(a + 1) * 512] for a in range(4))
            dst_f, src_f, rel_f, t9_f = (edge_f[0:TROW, a * 512:(a + 1) * 512] for a in range(4))
            lb_i = itmp[0:TROW, 0:4]
            V.tensor_scalar(lb_i, dst_i.rearrange("q (j f) -> q j f", j=4)[:, :, P - 1], 7, None,
                            ALU.arith_shift_right)
            V.tensor_copy(dst_f, dst_i)
            V.tensor_copy(src_f, src_i)
            V.tensor_copy(t9_f, t9_i)
            link(V.tensor_copy(rel_f, t16_i))
            link(V.scalar_tensor_tensor(out=rel_f, in0=src_f, scalar=float(NTYPE), in1=rel_f,
                                        op0=ALU.mult, op1=ALU.add))
            last_block = small[0:TROW, 8:12]
            V.tensor_copy(last_block, lb_i).then_inc(S("last_block"), 1)
            dve.wait_ge(S("prev_block"), 1)
            first, end = small[0:TROW, 12:16], small[0:TROW, 16:20]
            V.tensor_tensor(first[:, 1:4], tile_no[:, 1:4], last_block[:, 0:3], ALU.add)
            V.tensor_tensor(first[:, 0:1], tile_no[:, 0:1], bank(4, 0, 1, TROW), ALU.add)
            link(V.scalar_tensor_tensor(out=end, in0=tile_no[:, :], scalar=1.0, in1=last_block,
                                        op0=ALU.add, op1=ALU.add))
            for j in range(4):
                m = step_of_tile[0:TROW, j * STEPS:(j + 1) * STEPS]
                link(V.tensor_scalar(m, iota[0:TROW, :], first[:, j:j + 1], None, ALU.is_ge))
                i = V.scalar_tensor_tensor(out=m, in0=iota[0:TROW, :], scalar=end[:, j:j + 1], in1=m,
                                           op0=ALU.is_lt, op1=ALU.mult)
            i.then_inc(S("step_of_tile"), 1)
            dve.wait_ge(S("step_psum"), 5)
            blk, tmp, vld = sf[:, 0:STEPS], sf[:, STEPS:2 * STEPS], sf[:, 2 * STEPS:3 * STEPS]
            V.tensor_copy(tile_row[:, FRONT:FRONT + STEPS], bank(2, 0, STEPS, 1))
            V.tensor_copy(src_idx[:, 0:STEPS], bank(4, 0, STEPS))
            V.tensor_copy(rel_idx[:, 0:STEPS], bank(5, 0, STEPS))
            V.tensor_copy(type9[:, :], bank(6, 0, STEPS))
            link(V.tensor_tensor(blk, iota[:, :], bank(2, 0, STEPS), ALU.subtract))
            V.tensor_copy(block_row[:, FRONT:FRONT + STEPS], blk[0:1, :])
            first_of = blk[0:1, :].rearrange("p (g s) -> p g s", s=GS)[:, :, 0]
            V.tensor_copy(first_row[:, 8:8 + GROUPS], first_of)
            V.tensor_tensor(slot_row[:, FRONT:FRONT + STEPS].rearrange("p (g s) -> p g s", s=GS),
                            blk[0:1, :].rearrange("p (g s) -> p g s", s=GS),
                            first_of.unsqueeze(2).to_broadcast([1, GROUPS, GS]), ALU.subtract)\
                .then_inc(S("steps_ready"), 1)
            link(V.scalar_tensor_tensor(out=node_loc[:, :], in0=blk, scalar=-float(P),
                                        in1=bank(3, 0, STEPS), op0=ALU.mult, op1=ALU.add))
            V.tensor_scalar(node_loc_bf[:, :], node_loc[:, :], -1.0, float(P), ALU.max, ALU.min)
            hi_i, lo_i = itmp[:, 0:STEPS], itmp[:, STEPS:2 * STEPS]
            V.tensor_scalar(hi_i, src_idx[:, 0:STEPS], 7, None, ALU.arith_shift_right)
            V.tensor_scalar(lo_i, src_idx[:, 0:STEPS], P - 1, None, ALU.bitwise_and)
            link(V.tensor_scalar(tmp, node_loc[:, :], 0.0, None, ALU.is_ge))
            link(V.scalar_tensor_tensor(out=vld, in0=node_loc[:, :], scalar=float(P), in1=tmp,
                                        op0=ALU.is_lt, op1=ALU.mult))
            V.tensor_copy(src_hi[:, :], hi_i)
            link(V.tensor_copy(tmp, lo_i))
            V.scalar_tensor_tensor(out=bucket[:, :], in0=src_hi[:, :], scalar=float(NREL),
                                   in1=type9[:, :], op0=ALU.mult, op1=ALU.add)
            link(V.scalar_tensor_tensor(out=tmp, in0=tmp, scalar=1.0, in1=vld, op0=ALU.add, op1=ALU.mult))
            V.tensor_scalar(src_lo[:, :], tmp, -1.0, None, ALU.add)
            V.tensor_copy(sf[:, 3 * STEPS:4 * STEPS], bank(3, 0, STEPS)).then_inc(S("dst_step"), 1)

            for q, nb in enumerate(XG):
                dve.wait_ge(S("pq_psum"), q + 1)
                V.tensor_copy(xv(nA[:, q * 4 * F:(q * 4 + nb) * F]),
                              xv(bank(2 + q % 2, 0, nb * P), P)[:, :, F:2 * F]).then_inc(S("q_read"), 1)
            dve.wait_ge(S("q_read"), len(XG))
            qv = q_parts.rearrange("p (b a f) -> p b a f", a=3, f=F)
            link(V.tensor_copy(qv[:, :, 0, :], xv(nA[:, :])))
            link(V.tensor_tensor(xv(nB[:, :]), xv(nA[:, :]), qv[:, :, 0, :], ALU.subtract))
            link(V.tensor_copy(qv[:, :, 1, :], xv(nB[:, :])))
            link(V.tensor_tensor(xv(nA[:, :]), xv(nB[:, :]), qv[:, :, 1, :], ALU.subtract))
            V.tensor_copy(qv[:, :, 2, :], xv(nA[:, :])).then_inc(S("q_parts"), 1)
            dve.wait_ge(S("keys_psum"), 1)
            V.tensor_copy(scan[:, :], bank(6, 0, 512, SROW)).then_inc(S("keys_staged"), 1)
            w = EP // 32
            for h in range(2):
                dve.wait_ge(S("attr_part0"), h + 1)
                V.tensor_tensor(attr_half, attr_half, attr_split[:, 0:w], ALU.subtract).then_inc(S("attr_rest"), 1)
                dve.wait_ge(S("attr_part1"), h + 1)
                V.tensor_tensor(attr_split[:, 2 * w:3 * w], attr_half, attr_split[:, w:2 * w], ALU.subtract)\
                    .then_inc(S("attr_split"), 1)
            dve.wait_ge(S("w_in"), 16 * 7)
            wp = lambda a: w0_attr_parts[0:24, a * F:(a + 1) * F]
            w_all = w0_attr_sb[0:24, :]
            link(V.tensor_copy(wp(0), w_all))
            link(V.tensor_tensor(w_all, w_all, wp(0), ALU.subtract))
            link(V.tensor_copy(wp(1), w_all))
            V.tensor_tensor(wp(2), w_all, wp(1), ALU.subtract).then_inc(S("w0_attr_ready"), 1)
            link(V.memset(acc[:, :], 0.0))

            def hots(g, k, sumw, before=0):
                reached(dve, S(sumw), before + g - 9)
                return V.tensor_tensor(
                    hot_ring[:, k % HOTS * 512:(k % HOTS + 1) * 512].rearrange("p (s c) -> p s c", s=GS),
                    iota_bf[:, 0:P].unsqueeze(1).to_broadcast([P, GS, P]),
                    node_loc_bf[:, ds(g * GS, GS)].unsqueeze(2).to_broadcast([P, GS, P]), ALU.is_equal)

            def rest_of(layer, k, lag, value, before, g, relu=False, w=F):
                dve.wait_ge(S(f"{layer}_part0"), before + g + 1)
                if relu:
                    i = V.scalar_tensor_tensor(out=value, in0=value, scalar=0.0, in1=part(k - lag, 0, w),
                                               op0=ALU.max, op1=ALU.subtract)
                else:
                    i = V.tensor_tensor(value, value, part(k - lag, 0, w), ALU.subtract)
                i.then_inc(S(f"{layer}_rest"), 1)

            def third_part(layer, k, lag, rest, before, g, w=F):
                dve.wait_ge(S(f"{layer}_part1"), before + g + 1)
                V.tensor_tensor(part(k - lag, 2, w), rest, part(k - lag, 1, w), ALU.subtract)\
                    .then_inc(S(f"{layer}_parts"), 1)

            first_block = row_values(first_row, mybir.EngineType.DVE, BLOCKS - 1, 1, 8)

            def add_sums(layer, o, k, w, before=0):
                b, = first_block(o, k, 6)
                if not live(o, k, 6):
                    return
                g, kk = group_no(o, k) - 6, k - 6
                dve.wait_ge(S(f"{layer}_summed"), before + g + 1)
                reached(dve, S(f"{layer}_added"), before + g)
                a = acc[:, ds(b * w, GS * w)]
                V.tensor_tensor(a, a, bank(4 + kk % 2, 0, GS * w), ALU.add).then_inc(S(f"{layer}_added"), 1)

            def l0(o, k):
                if live(o, k, 0):
                    g = group_no(o, k)
                    hots(g, k, "l0_summed")
                    reached(dve, S("l0_counted"), g - 1)
                    V.tensor_tensor(
                        src_hot[:, k % 2 * 512:k % 2 * 512 + 512].rearrange("p (s c) -> p s c", s=GS),
                        iota_bf[:, 0:P].unsqueeze(1).to_broadcast([P, GS, P]),
                        src_lo[:, ds(g * GS, GS)].unsqueeze(2).to_broadcast([P, GS, P]), ALU.is_equal)
                    V.tensor_tensor(
                        bucket_hot[:, k % 2 * GS * 226:(k % 2 + 1) * GS * 226].rearrange("p (s c) -> p s c", s=GS),
                        iota_bf[:, :].unsqueeze(1).to_broadcast([P, GS, 226]),
                        bucket[:, ds(g * GS, GS)].unsqueeze(2).to_broadcast([P, GS, 226]), ALU.is_equal)\
                        .then_inc(S("l0_hots"), 1)
                if live(o, k, 3):
                    kk = (k - 3) % 5
                    rest_of("l0", k, 3, xv(nB[:, kk * 256:kk * 256 + 256]), 0, group_no(o, k) - 3, relu=True)
                if live(o, k, 2):
                    g, kk = group_no(o, k) - 2, k - 2
                    dve.wait_ge(S(f"rows_in{kk % RING}"), rows_in_count(0, o, kk))
                    dve.wait_ge(S("l0_expanded"), g + 1)
                    reached(dve, S("l0_parts"), g - 4)
                    V.tensor_tensor(xv(nB[:, kk % 5 * 256:kk % 5 * 256 + 256]), rows_in_slot(kk),
                                    xv(bank(2 + kk % 2, 0, 256)), ALU.add).then_inc(S("l0_pre"), 1)
                    reached(dve, S("l0_summed"), g - 4)
                    V.tensor_tensor(part(kk, 0)[:, :, F + 1:ACC0],
                                    lane[:, 0:NREL].unsqueeze(1).to_broadcast([P, GS, NREL]),
                                    type9[:, ds(g * GS, GS)].unsqueeze(2).to_broadcast([P, GS, NREL]),
                                    ALU.is_equal)
                if live(o, k, 4):
                    kk = (k - 4) % 5
                    third_part("l0", k, 4, xv(nB[:, kk * 256:kk * 256 + 256]), 0, group_no(o, k) - 4)
                add_sums("l0", o, k, ACC0)

            pipeline(dve, l0, 6)
            dve.wait_ge(S("l0_added"), GROUPS)
            dve.wait_ge(S("src_counts"), 1)
            cv = xv(counts[:, :], 2 * NREL)
            av = xv(acc[:, 0:BLOCKS * ACC0], ACC0)
            V.tensor_copy(cv[:, :, 0:NREL], xv(bank(6, 0, BLOCKS * NREL), NREL))
            link(V.tensor_copy(cv[:, :, NREL:], av[:, :, F + 1:]))
            link(V.tensor_reduce(col(10), cv, axis=AX.X, op=ALU.add))
            link(V.tensor_scalar(col(10), col(10), 1.0, None, ALU.max))
            V.reciprocal(col(11), col(10))
            link(V.tensor_copy(col(12), av[:, :, F]))
            V.tensor_scalar(col(13), col(12), 0.0, None, ALU.is_gt).then_inc(S("degree"), 1)
            dve.wait_ge(S("degree_psum"), 1)
            link(V.tensor_copy(col(14), bank(7, 32, 32 + BLOCKS)))
            link(V.tensor_tensor_scan(col(15), ones[:, 0:BLOCKS],
                                      col(14), 0.0, ALU.mult, ALU.add))
            link(V.tensor_tensor(col(15), col(15), col(14), ALU.subtract))
            link(V.tensor_tensor(col(15), col(15), node_base[:, :], ALU.add))
            link(V.tensor_tensor(col(15), col(15), bank(7, 0, BLOCKS), ALU.add))
            link(V.tensor_scalar(col(15), col(15), -float(STEPS * P), None, ALU.add))
            link(V.tensor_tensor(col(15), col(15), col(13), ALU.mult))
            V.tensor_scalar(end_idx[:, :], col(15), float(STEPS * P), None, ALU.add)

            dve.wait_ge(S("prev_key"), 16)
            link(V.tensor_tensor(seg_start[:, :], scan[:, :], seg_start[:, :], ALU.not_equal))
            link(V.tensor_reduce(tail[:, 0:1], seg_start[:, :], axis=AX.X, op=ALU.max))
            link(V.tensor_scalar(tail[:, 1:2], tail[:, 0:1], -BIG, None, ALU.mult))
            V.tensor_scalar(seg_start[:, :], seg_start[:, :], -BIG, None, ALU.mult)\
                .then_inc(S("row_start_in"), 1)
            dve.wait_ge(S("row_start_psum"), 1)
            link(V.tensor_copy(row_start[:, :], bank(7, 64, 64 + SROW, 1)))

            def layer_norm(n):
                link(V.tensor_reduce(col(0), xv(nA[:, :]), axis=AX.X, op=ALU.add))
                link(V.tensor_scalar(col(0), col(0), 1.0 / F, None, ALU.mult))
                link(V.tensor_tensor(xv(nA[:, :]), xv(nA[:, :]),
                                     col(0).unsqueeze(2).to_broadcast([P, BLOCKS, F]), ALU.subtract))
                link(V.tensor_tensor(nB[:, :], nA[:, :], nA[:, :], ALU.mult))
                V.tensor_reduce(col(1), xv(nB[:, :]), axis=AX.X, op=ALU.add).then_inc(S("ln_var"), 1)
                dve.wait_ge(S("ln_std"), n + 1)
                link(V.reciprocal(col(3), col(2)))
                V.tensor_tensor(xv(X[:, :]), xv(nA[:, :]),
                                col(3).unsqueeze(2).to_broadcast([P, BLOCKS, F]), ALU.mult)\
                    .then_inc(S("ln_done"), 1)

            for q in range(4):
                nb = min(8, BLOCKS - 8 * q)
                dve.wait_ge(S("out0_psum"), q + 1)
                i = V.tensor_tensor(nA[:, q * 512:q * 512 + nb * F], X[:, q * 512:q * 512 + nb * F],
                                    bank(2 + q % 2, 0, nb * F), ALU.add)
                i.then_inc(S("out0_added"), 1)
            dve.wait_ge(S("out0_added"), 4)
            layer_norm(0)

            for b in range(BLOCKS):
                dve.wait_ge(S("rel1_psum"), b + 1)
                z = relprod[:, b % 2 * 1152:(b % 2 + 1) * 1152].rearrange("p (r f) -> p r f", f=F)
                lo = (b % 2) * 3
                V.tensor_tensor(z, PS[:, lo * 512:lo * 512 + 1152].rearrange("p (r f) -> p r f", f=F),
                                cv[:, b, :].unsqueeze(2).to_broadcast([P, 2 * NREL, F]), ALU.mult)\
                    .then_inc(S("rel1_read"), 1)
                dve.wait_ge(S("rel1_read"), b + 1)
                V.tensor_reduce(nA[:, b * F:(b + 1) * F], z.rearrange("p r f -> p f r"),
                                axis=AX.X, op=ALU.add).then_inc(S("rel1_sum"), 1)
            dve.wait_ge(S("rel1_sum"), BLOCKS)
            link(V.tensor_tensor(xv(nA[:, :]), xv(nA[:, :]),
                                 col(11).unsqueeze(2).to_broadcast([P, BLOCKS, F]), ALU.mult))
            link(V.tensor_tensor(nA[:, :], nA[:, :], X[:, :], ALU.add))
            layer_norm(1)

            for b in range(BLOCKS):
                dve.wait_ge(S("rel_psum"), b + 1)
                if b >= 2:
                    dve.wait_ge(S(f"l2_table{b % 2}"), 16 * (b // 2))
                V.tensor_copy(rel_stage[:, (b % 2) * 1024:(b % 2) * 1024 + 512],
                              bank(2 + (b % 2) * 2)).then_inc(S("rel_staged_v"), 1)
            dve.wait_ge(S("rel_staged_v"), BLOCKS)
            V.memset(acc[:, :], 0.0).then_inc(S("arena_free"), 1)
            dve.wait_ge(S("arena_free"), 1)

            def l2(o, k):
                if live(o, k, 0):
                    g = group_no(o, k)
                    hots(g, k, "l2_summed")
                    reached(dve, S("l2_srcT_psum"), g - 1)
                    V.tensor_tensor(
                        hot_T[:, k % 2 * 512:k % 2 * 512 + 512].rearrange("p (s c) -> p s c", s=GS),
                        iota_bf[:, 0:P].unsqueeze(1).to_broadcast([P, GS, P]),
                        src_lo[:, ds(g * GS, GS)].unsqueeze(2).to_broadcast([P, GS, P]), ALU.is_equal)\
                        .then_inc(S("l2_hots"), 1)
                if live(o, k, 3):
                    rest_of("l2", k, 3, rows_in_slot(k - 3), 0, group_no(o, k) - 3)
                if live(o, k, 4):
                    third_part("l2", k, 4, rows_in_slot(k - 4), 0, group_no(o, k) - 4)
                add_sums("l2", o, k, F)

            pipeline(dve, l2, 6)
            dve.wait_ge(S("l2_added"), GROUPS)
            link(V.tensor_tensor(nA[:, :], X[:, :], acc[:, 0:BLOCKS * F], ALU.add))
            layer_norm(2)

            def split3(dst, value, rest):
                link(V.tensor_copy(dst(0), value))
                link(V.tensor_tensor(rest, value, dst(0), ALU.subtract))
                link(V.tensor_copy(dst(1), rest))
                link(V.tensor_tensor(rest, rest, dst(1), ALU.subtract))
                return V.tensor_copy(dst(2), rest)

            for n in range(3):
                dve.wait_ge(S("gat_h"), (n + 1) * len(XG))
                hv = xv(node_h[:, :], F + 2)
                V.tensor_copy(col(4), hv[:, :, F])
                link(V.tensor_copy(col(5), hv[:, :, F + 1]))
                split3(lambda a: as_parts[:, a * BLOCKS:(a + 1) * BLOCKS], col(4), col(6))\
                    .then_inc(S("gat_as_parts"), 1)
                link(V.memset(acc[:, :], 0.0))

                def pick(o, before=n * BATCHES):
                    for half in range(2):
                        batch = 2 * o + half
                        reached(dve, S("gat_picked"), before + batch - 1)
                        pv = picked[:, half * 500:half * 500 + 500].rearrange("p (s c) -> p s c", c=BLOCKS)
                        V.tensor_tensor(pv, lane[:, 0:BLOCKS].unsqueeze(1).to_broadcast([P, BATCH, BLOCKS]),
                                        src_hi[:, ds(batch * BATCH, BATCH)].unsqueeze(2)
                                        .to_broadcast([P, BATCH, BLOCKS]), ALU.is_equal).then_inc(S("gat_p1"), 1)
                        dve.wait_ge(S("gat_as_psum"), before + batch + 1)
                        dve.wait_ge(S("gat_p1"), 2 * (before + batch) + 1)
                        V.tensor_tensor(pv, pv, bank(4 + half, 0, 500).rearrange("p (s c) -> p s c", c=BLOCKS),
                                        ALU.mult).then_inc(S("gat_p1"), 1)
                        dve.wait_ge(S("gat_p1"), 2 * (before + batch) + 2)
                        V.tensor_reduce(as_edge[:, ds(batch * BATCH, BATCH)], pv, axis=AX.X, op=ALU.add)\
                            .then_inc(S("gat_picked"), 1)

                pick(0)
                with dve.Fori(1, BATCHES // 2) as o:
                    pick(o)
                dve.wait_ge(S("gat_asT_psum"), n + 1)
                V.tensor_tensor_scan(scan[:, :], seg_start[:, :], bank(6, 0, 512, SROW), -BIG,
                                     ALU.add, ALU.max).then_inc(S("gat_scan1"), 1)
                dve.wait_ge(S("gat_tail_psum"), n + 1)
                V.tensor_tensor_scan(carry[:, 1:SROW + 1], row_start[:, :], bank(7, 0, SROW, 1), -BIG,
                                     ALU.add, ALU.max).then_inc(S("gat_carry"), 1)
                dve.wait_ge(S("gat_carry_psum"), n + 1)
                link(V.tensor_copy(carry_col[:, :], bank(7, 128, 129, SROW)))
                V.tensor_tensor_scan(scan[:, :], seg_start[:, :], bank(6, 0, 512, SROW), carry_col[:, 0:1],
                                     ALU.add, ALU.max).then_inc(S("gat_scanned"), 1)
                dve.wait_ge(S("seg_node_in"), 16 * BLOCKS * (n + 1))
                link(V.tensor_tensor(col(6), seg_node[:, :], col(4), ALU.max))
                link(V.tensor_tensor(col(6), col(6), col(5), ALU.add))
                link(V.scalar_tensor_tensor(out=col(6), in0=col(6), scalar=0.2, in1=col(6),
                                            op0=ALU.mult, op1=ALU.max))
                link(V.tensor_tensor(col(7), col(4), col(5), ALU.add))
                link(V.scalar_tensor_tensor(out=col(7), in0=col(7), scalar=0.2, in1=col(7),
                                            op0=ALU.mult, op1=ALU.max))
                V.tensor_tensor(col(7), col(7), col(6), ALU.subtract).then_inc(S("gat_self_e"), 1)
                mv = adm_parts[:, :].rearrange("p (b a c) -> p b a c", a=3, c=2)
                link(split3(lambda a: mv[:, :, a, 0], col(5), col(9)))
                split3(lambda a: mv[:, :, a, 1], col(6), col(9)).then_inc(S("gat_adm_parts"), 1)

                def gat(o, k, before=n * GROUPS):
                    if live(o, k, 0):
                        g = group_no(o, k)
                        hots(g, k, "gat_summed", before).then_inc(S("gat_hots"), 1)
                    if live(o, k, 2):
                        g, kk = group_no(o, k) - 2, k - 2
                        dve.wait_ge(S("gat_expanded"), before + g + 1)
                        reached(dve, S("gat_weight"), before + g - 1)
                        z = wtmp[:, kk % 2 * GS:kk % 2 * GS + GS]
                        ev = bank(2 + kk % 2, 0, 2 * GS).rearrange("p (s c) -> p s c", c=2)
                        V.tensor_tensor(z, as_edge[:, ds(g * GS, GS)], ev[:, :, 0], ALU.add)\
                            .then_inc(S("gat_z"), 1)
                        dve.wait_ge(S("gat_z"), 2 * (before + g) + 1)
                        V.scalar_tensor_tensor(out=z, in0=z, scalar=0.2, in1=z, op0=ALU.mult, op1=ALU.max)\
                            .then_inc(S("gat_z"), 1)
                        dve.wait_ge(S("gat_z"), 2 * (before + g) + 2)
                        V.tensor_tensor(wtmp[:, 16 + kk % 2 * GS:16 + kk % 2 * GS + GS], z, ev[:, :, 1],
                                        ALU.subtract).then_inc(S("gat_logit"), 1)
                    if live(o, k, 3):
                        rest_of("gat", k, 3, scaled_rows(k - 3), before, group_no(o, k) - 3, w=GW)
                    if live(o, k, 4):
                        third_part("gat", k, 4, scaled_rows(k - 4), before, group_no(o, k) - 4, w=GW)
                    add_sums("gat", o, k, GW, before)

                pipeline(dve, gat, 6)
                dve.wait_ge(S("gat_added"), (n + 1) * GROUPS)
                dve.wait_ge(S("gat_self_w"), n + 1)
                sv = acc[:, 0:BLOCKS * GW].rearrange("p (b f) -> p b f", f=GW)
                wide = lambda c: col(c).unsqueeze(2).to_broadcast([P, BLOCKS, F])
                link(V.tensor_tensor(xv(nB[:, :]), hv[:, :, 0:F], wide(8), ALU.mult))
                link(V.tensor_tensor(xv(nB[:, :]), xv(nB[:, :]), sv[:, :, 0:F], ALU.add))
                link(V.tensor_tensor(col(9), sv[:, :, F], col(8), ALU.add))
                link(V.tensor_scalar(col(9), col(9), 1e-16, None, ALU.add))
                link(V.reciprocal(col(7), col(9)))
                link(V.tensor_tensor(xv(nB[:, :]), xv(nB[:, :]), wide(7), ALU.mult))
                dve.wait_ge(S("b3_in"), 16 * (n + 1))
                i = V.tensor_tensor(xv(nB[:, :]), xv(nB[:, :]),
                                    b3_sb[:, :].unsqueeze(1).to_broadcast([P, BLOCKS, F]), ALU.add)
                link(i)
                if n < 2:
                    V.tensor_scalar(nA[:, :], nB[:, :], 0.0, None, ALU.max).then_inc(S("gat_done"), 1)
                else:
                    link(V.tensor_tensor(nA[:, :], X[:, :], nB[:, :], ALU.add))
            layer_norm(3)

        @block.tensor
        def _(pe):
            T = nc.tensor

            def transpose_X(time, src_tile):
                for q, nb in enumerate(XG):
                    if q >= 2:
                        pe.wait_ge(S("xT"), time * len(XG) + q - 1)
                    for s in range(nb):
                        b = 4 * q + s
                        i = T.transpose(bank(q % 2, s * P, (s + 1) * P, F), src_tile[:, b * F:(b + 1) * F],
                                        ident[:, :])
                    i.then_inc(S("xT_psum"), 1)

            pe.wait_ge(S("consts"), 1)
            pe.wait_ge(S("last_block"), 1)
            T.matmul(bank(4, 0, 1, TROW), next_row, small[0:TROW, 11:12], start=True, stop=True)\
                .then_inc(S("prev_block"), 1)
            pe.wait_ge(S("x_in"), 16)
            transpose_X(0, X)
            pe.wait_ge(S("step_of_tile"), 1)
            for j in range(4):
                i = T.matmul(bank(2, 0, STEPS), tile_no[:, j:j + 1].to_broadcast([TROW, P]),
                             step_of_tile[0:TROW, j * STEPS:(j + 1) * STEPS], start=j == 0, stop=j == 3)
            i.then_inc(S("step_psum"), 1)
            for a in range(4):
                for j in range(4):
                    i = T.matmul(bank(3 + a, 0, STEPS), edge_f[0:TROW, a * 512 + j * P:a * 512 + (j + 1) * P],
                                 step_of_tile[0:TROW, j * STEPS:(j + 1) * STEPS], start=j == 0, stop=j == 3)
                i.then_inc(S("step_psum"), 1)
            pe.wait_ge(S("w_in"), 16 * 7)
            pe.wait_ge(S("dst_step"), 1)
            for j in range(4):
                i = T.transpose(bank(6, j * P, (j + 1) * P, SROW),
                                sf[:, 3 * STEPS:4 * STEPS].rearrange("p (q j) -> p j q", j=4)[:, j, :],
                                ident[:, :])
            i.then_inc(S("keys_psum"), 1)
            for q, nb in enumerate(XG):
                pe.wait_ge(S("xT"), q + 1)
                if q >= 2:
                    pe.wait_ge(S("p_staged"), q - 1)
                    pe.wait_ge(S("q_read"), q - 1)
                for s in range(nb):
                    b = 4 * q + s
                    i = T.matmul(bank(2 + q % 2, s * P, (s + 1) * P), XT[:, b * P:(b + 1) * P],
                                 w0_pq_sb[0:F + 1, :], start=True, stop=True)
                i.then_inc(S("pq_psum"), 1)

            def sums(layer, o, k, w, values_w, before=0):
                slots = slot_of(o, k, 5)
                if not live(o, k, 5):
                    return
                g, kk = group_no(o, k) - 5, k - 5
                pe.wait_ge(S(f"{layer}_parts"), before + g + 1)
                reached(pe, S(f"{layer}_added"), before + g - 1)
                b = 4 + kk % 2
                for s in range(GS):
                    h = (kk % HOTS * GS + s) * P
                    if s == 0:
                        T.matmul(bank(b, 0, GS * w), hot_ring[:, h:h + P], zero_bf[:, 0:GS * w], start=True,
                                 stop=False, skip_group_check=True)
                    for a in range(3):
                        n_cols = w if a == 0 else values_w
                        i = T.matmul(PS[:, ds(slots[s] * w + b * 512, n_cols)], hot_ring[:, h:h + P],
                                     part(kk, a, n_cols)[:, s, :], start=False,
                                     stop=s == GS - 1 and a == 2, skip_group_check=True)
                i.then_inc(S(f"{layer}_summed"), 1)

            def transpose_hots(layer, k, g, before=0):
                reached(pe, S(f"{layer}_hotT"), before + g - 1)
                for s in range(GS):
                    h = (k % HOTS * GS + s) * P
                    i = T.transpose(bank(k % 2).bitcast(bf16)[:, s * P:(s + 1) * P], hot_ring[:, h:h + P],
                                    ident_bf[:, :])
                i.then_inc(S(f"{layer}_hotT_psum"), 1)

            slot_of = row_values(slot_row, mybir.EngineType.PE, GS - 1)
            block_of = row_values(block_row, mybir.EngineType.PE, BLOCKS - 1)

            pe.wait_ge(S("q_parts"), 1)
            pe.wait_ge(S("steps_ready"), 1)
            pe.wait_ge(S("keys_staged"), 1)
            pe.wait_ge(S("w0_attr_ready"), 1)
            pe.wait_ge(S("count_column"), 1)
            T.matmul(bank(6, 0, 226), ident_bf[:, :], zero_bf[:, 0:226], start=True, stop=False,
                     skip_group_check=True)

            def l0(o, k):
                bs = block_of(o, k, 1)
                sums("l0", o, k, ACC0, F)
                if live(o, k, 1):
                    g, kk = group_no(o, k) - 1, k - 1
                    pe.wait_ge(S("l0_hotT"), g + 1)
                    reached(pe, S("l0_pre"), g - 1)
                    pe.wait_ge(S(f"attr_in{kk % 5}"), 64 * (4 * o + kk // 5 - 1))
                    for s in range(GS):
                        ps = bank(2 + kk % 2, s * F, (s + 1) * F)
                        e = (kk % 5 * GS + s) * P
                        for a in range(3):
                            T.matmul(ps, attr_ring[0:24, e:e + P], w0_attr_parts[0:24, a * F:(a + 1) * F],
                                     start=a == 0, stop=False)
                        for a in range(3):
                            i = T.matmul(ps, hot_T[:, (kk % 2 * GS + s) * P:(kk % 2 * GS + s + 1) * P],
                                         q_parts[:, ds(bs[s] * (3 * F) + a * F, F)], start=False, stop=a == 2)
                    i.then_inc(S("l0_expanded"), 1)
                if live(o, k, 0):
                    g = group_no(o, k)
                    pe.wait_ge(S("l0_hots"), g + 1)
                    transpose_hots("l0", k, g)
                    for s in range(GS):
                        i = T.matmul(bank(6, 0, 226), src_hot[:, (k % 2 * GS + s) * P:(k % 2 * GS + s + 1) * P],
                                     bucket_hot[:, (k % 2 * GS + s) * 226:(k % 2 * GS + s + 1) * 226],
                                     start=False, stop=False, skip_group_check=True)
                    i.then_inc(S("l0_counted"), 1)

            pipeline(pe, l0, 5)
            T.matmul(bank(6, 0, 226), ident_bf[:, :], zero_bf[:, 0:226], start=False, stop=True,
                     skip_group_check=True).then_inc(S("src_counts"), 1)
            pe.wait_ge(S("degree"), 1)
            T.matmul(bank(7, 0, BLOCKS), upper[:, :], col(12), start=True, stop=True)
            T.matmul(bank(7, 32, 32 + BLOCKS), ones[:, :], col(12), start=True, stop=True)\
                .then_inc(S("degree_psum"), 1)
            pe.wait_ge(S("row_start_in"), 1)
            T.transpose(bank(7, 64, 64 + SROW, 1), tail[:, 1:2], ident[0:SROW, 0:SROW])\
                .then_inc(S("row_start_psum"), 1)
            for q, nb in enumerate(XG):
                if q >= 2:
                    pe.wait_ge(S("sum_T"), q - 1)
                for s in range(nb):
                    b = 4 * q + s
                    i = T.transpose(bank(q % 2, s * P, (s + 1) * P, F + 1),
                                    acc[:, b * ACC0:b * ACC0 + F + 1], ident[:, :])
                i.then_inc(S("sum_T_psum"), 1)
            for q in range(4):
                nb = min(8, BLOCKS - 8 * q)
                pe.wait_ge(S("sum_T"), min(len(XG), 2 * q + 2))
                if q >= 2:
                    pe.wait_ge(S("out0_added"), q - 1)
                for s in range(nb):
                    b = 8 * q + s
                    i = T.matmul(bank(2 + q % 2, s * F, (s + 1) * F), XT[:, b * P:(b + 1) * P],
                                 w0_out_sb[0:F + 1, :], start=True, stop=True)
                i.then_inc(S("out0_psum"), 1)

            pe.wait_ge(S("ln_done"), 1)
            transpose_X(1, X)
            pe.wait_ge(S("xT"), 2 * len(XG))
            pe.wait_ge(S("row_of_ones"), 2)
            for b in range(BLOCKS):
                if b >= 2:
                    pe.wait_ge(S("rel1_read"), b - 1)
                lo = (b % 2) * 3
                for a in range(0, 2 * NREL * F, 512):
                    w = min(512, 2 * NREL * F - a)
                    i = T.matmul(PS[:, lo * 512 + a:lo * 512 + a + w], XT[:, b * P:(b + 1) * P],
                                 w1_sb[0:F + 1, a:a + w], start=True, stop=True)
                i.then_inc(S("rel1_psum"), 1)

            pe.wait_ge(S("ln_done"), 2)
            transpose_X(2, X)
            pe.wait_ge(S("xT"), 3 * len(XG))
            for b in range(BLOCKS):
                if b >= 2:
                    pe.wait_ge(S("rel_staged_v"), b - 1)
                    pe.wait_ge(S("rel_staged_a"), b - 1)
                for a in range(2):
                    i = T.matmul(bank(2 + (b % 2) * 2 + a), XT[0:F, b * P:(b + 1) * P],
                                 w2_sb[0:F, a * 512:(a + 1) * 512], start=True, stop=True)
                i.then_inc(S("rel_psum"), 1)
            pe.wait_ge(S("arena_free"), 1)

            def l2(o, k):
                sums("l2", o, k, F, F)
                if live(o, k, 0):
                    g = group_no(o, k)
                    pe.wait_ge(S("l2_hots"), g + 1)
                    reached(pe, S("l2_srcT"), g - 1)
                    for s in range(GS):
                        i = T.transpose(bank(k % 2).bitcast(bf16)[:, s * P:(s + 1) * P],
                                        hot_T[:, (k % 2 * GS + s) * P:(k % 2 * GS + s + 1) * P], ident_bf[:, :])
                    i.then_inc(S("l2_srcT_psum"), 1)

            pipeline(pe, l2, 5)
            pe.wait_ge(S("l2_srcT"), GROUPS)

            for n in range(3):
                pe.wait_ge(S("w3_in"), 48 * (n + 1))
                pe.wait_ge(S("ln_done") if n == 0 else S("gat_done"), 3 if n == 0 else n)
                T.matmul(bank(7, 0, 2, F), w3T_sb[:, :], a3_sb[:, :], start=True, stop=True)\
                    .then_inc(S("gat_wa_psum"), 1)
                transpose_X(3 + n, X if n == 0 else nA)
                pe.wait_ge(S("gat_wa"), n + 1)
                for q, nb in enumerate(XG):
                    pe.wait_ge(S("xT"), (3 + n) * len(XG) + q + 1)
                    if q >= 2:
                        pe.wait_ge(S("gat_h"), n * len(XG) + q - 1)
                    for s in range(nb):
                        b = 4 * q + s
                        i = T.matmul(bank(2 + q % 2, s * (F + 2), (s + 1) * (F + 2)),
                                     XT[0:F, b * P:(b + 1) * P], w3_sb[:, :], start=True, stop=True)
                    i.then_inc(S("gat_h_psum"), 1)
                pe.wait_ge(S("gat_h_psum"), (n + 1) * len(XG))
                pe.sem_inc(S("weights_free"), 1)
                pe.wait_ge(S("gat_as_parts"), n + 1)

                def look_up(o, before=n * BATCHES):
                    for half in range(2):
                        batch = 2 * o + half
                        reached(pe, S("gat_picked"), before + batch - 1)
                        for s in range(BATCH):
                            for a in range(3):
                                i = T.matmul(bank(4 + half, s * BLOCKS, (s + 1) * BLOCKS),
                                             src_hot_T[:, ds((batch * BATCH + s) * P, P)],
                                             as_parts[:, a * BLOCKS:(a + 1) * BLOCKS], start=a == 0, stop=a == 2)
                        i.then_inc(S("gat_as_psum"), 1)

                look_up(0)
                with pe.Fori(1, BATCHES // 2) as o:
                    look_up(o)
                pe.wait_ge(S("gat_picked"), (n + 1) * BATCHES)
                for j in range(4):
                    i = T.transpose(bank(6, j * P, (j + 1) * P, SROW),
                                    as_edge[:, :].rearrange("p (q j) -> p j q", j=4)[:, j, :], ident[:, :])
                i.then_inc(S("gat_asT_psum"), 1)
                pe.wait_ge(S("gat_scan1"), n + 1)
                T.transpose(bank(7, 0, SROW, 1), scan[:, 511:512], ident[0:SROW, 0:SROW])\
                    .then_inc(S("gat_tail_psum"), 1)
                pe.wait_ge(S("gat_carry"), n + 1)
                T.matmul(bank(7, 128, 129, SROW), carry[0:1, 0:SROW], ones[0:1, 0:1], start=True, stop=True)\
                    .then_inc(S("gat_carry_psum"), 1)
                pe.wait_ge(S("gat_adm_parts"), n + 1)

                def gat(o, k, before=n * GROUPS):
                    bs = block_of(o, k, 1)
                    sums("gat", o, k, GW, GW, before)
                    if live(o, k, 1):
                        g, kk = group_no(o, k) - 1, k - 1
                        pe.wait_ge(S("gat_hotT"), before + g + 1)
                        reached(pe, S("gat_logit"), before + g - 1)
                        for s in range(GS):
                            for a in range(3):
                                i = T.matmul(bank(2 + kk % 2, 2 * s, 2 * s + 2),
                                             hot_T[:, (kk % 2 * GS + s) * P:(kk % 2 * GS + s + 1) * P],
                                             adm_parts[:, ds(bs[s] * 6 + 2 * a, 2)], start=a == 0, stop=a == 2)
                        i.then_inc(S("gat_expanded"), 1)
                    if live(o, k, 0):
                        g = group_no(o, k)
                        pe.wait_ge(S("gat_hots"), before + g + 1)
                        transpose_hots("gat", k, g, before)

                pipeline(pe, gat, 5)


_INS = ["x", "ints", "attr_t", "w0_pq", "w0_attr", "w0_out", "w1", "w2", "w3", "w3_t", "a3", "b3"]


def laid_out(inputs):
    import numpy as np
    f = lambda n: np.asarray(inputs[n])
    f32, i32 = np.float32, np.int32
    padded = lambda a, v: np.concatenate([a, np.full(EP - E, v, i32)])
    return {
        "x": np.concatenate([f("x"), np.zeros((NP_ - N, F), f32)]),
        "ints": np.stack([padded(f("src"), NP_ - 1), padded(f("dst"), NP_ - 1),
                          padded(f("edge_type_16"), 0), padded(f("edge_type_9"), 0)]),
        "attr_t": np.ascontiguousarray(np.concatenate([f("edge_attr_8"), np.zeros((EP - E, 8), f32)]).T),
        "w0_pq": np.concatenate([
            np.concatenate([f("L0_gnn_W1")[0:F], f("L0_gnn_W1")[F:2 * F]], axis=1),
            np.concatenate([np.zeros(F, f32), f("L0_gnn_b1")])[None]]),
        "w0_attr": np.ascontiguousarray(f("L0_gnn_W1")[2 * F:]),
        "w0_out": np.concatenate([f("L0_gnn_W2"), f("L0_gnn_b2")[None]]),
        "w1": np.concatenate([f("L1_gnn_weights").transpose(0, 2, 1, 3).reshape(3, F, 2 * NREL * F),
                              f("L1_gnn_biases").reshape(3, 1, 2 * NREL * F)], axis=1),
        "w2": np.ascontiguousarray(f("L2_gnn_weight").transpose(1, 0, 2).reshape(F, NTYPE * F)),
        "w3": np.stack([f(f"L3_gnn_W{n}") for n in (1, 2, 3)]),
        "w3_t": np.ascontiguousarray(np.stack([f(f"L3_gnn_W{n}").T for n in (1, 2, 3)])),
        "a3": np.ascontiguousarray(np.stack([np.stack([f(f"L3_gnn_a{n}s"), f(f"L3_gnn_a{n}d")], axis=1)
                                             for n in (1, 2, 3)])),
        "b3": np.stack([f(f"L3_gnn_b{n}")[None] for n in (1, 2, 3)]),
    }


def kernel(**inputs):
    import concourse.bacc as bacc
    from concourse.bass_utils import run_bass_kernel_spmd

    nc = bacc.Bacc("TRN2", target_bir_lowering=False, num_devices=1)
    arrays = laid_out(inputs)
    args = [nc.dram_tensor(f"in_{n}", arrays[n].shape, mybir.dt.from_np(arrays[n].dtype),
                           kind="ExternalInput").ap() for n in _INS]
    out = nc.dram_tensor("out", (N, F), mybir.dt.float32, kind="ExternalOutput").ap()
    gnn_kernel(nc, *args, out)
    r = run_bass_kernel_spmd(nc, [{f"in_{n}": arrays[n] for n in _INS}], core_ids=[0])
    return r.results[0]["out"]
```

```python
import concourse.bass as bass
from concourse import mybir
from contextlib import ExitStack

N, F, E, NREL, NTYPE = 3125, 64, 53125, 9, 16
P = 128
BLOCKS = -(-N // P)
NP_ = BLOCKS * P
TILES = -(-E // P)
EP = TILES * P
STEPS = TILES + BLOCKS - 1
TROW = TILES // 4
SROW = STEPS // 4
GS = 4
GROUPS = STEPS // GS
RING = 20
START = RING - GROUPS % RING
OUTER = (START + GROUPS) // RING
HOTS = 10
OWN_ROWS = 11
BATCH = 5 * GS
BATCHES = STEPS // BATCH
SPAN = 5 * GS
FRONT = 8 * GS
ACC0 = F + 1 + NREL
GW = F + 1
BUCKETS = BLOCKS * NREL + 1
BIG = 1e30
EPS = 1e-5


def gnn_kernel(nc, x, ints, prev_dst, attr_t, w0_pq, w0_attr, w0_out, w1, b1, w2, w3, w3_t, a3, b3, out):
    fp32, bf16, i32 = mybir.dt.float32, mybir.dt.bfloat16, mybir.dt.int32
    ALU, ACT, AX = mybir.AluOpType, mybir.ActivationFunctionType, mybir.AxisListType
    ds = bass.ds

    src_rows = nc.dram_tensor("src_rows", [NP_, F], fp32).ap()
    rel_rows = nc.dram_tensor("rel_rows", [NP_ * NTYPE, F], fp32).ap()
    gat_rows = [nc.dram_tensor(f"gat_rows{n}", [NP_, F], fp32).ap() for n in range(3)]
    keys = nc.dram_tensor("keys", [STEPS * P + 1, 1], fp32).ap()
    attr_parts = nc.dram_tensor("attr_parts", [3 * 8, EP], bf16).ap()
    sorted_edges = nc.dram_tensor("sorted_edges", [EP, 12], fp32).ap()
    sorted_ints = nc.dram_tensor("sorted_ints", [4, EP], i32).ap()
    sorted_attr = nc.dram_tensor("sorted_attr", [8, EP], fp32).ap()
    seg_max = nc.dram_tensor("seg_max", [STEPS * P + 1, 1], fp32).ap()

    ctx = ExitStack()
    with ctx:
        def sb(name, shape, dt=fp32):
            return ctx.enter_context(nc.sbuf_tensor(name, shape, dt))

        sems = {}

        def S(name):
            if name not in sems:
                sems[name] = ctx.enter_context(nc.semaphore(name))
            return sems[name]

        arena = sb("arena", [P, STEPS * P // 2])
        src_hot_T = arena[:, :].bitcast(bf16)
        at = [0]

        def carve(cols):
            a = arena[:, at[0]:at[0] + cols]
            at[0] += cols
            assert at[0] <= STEPS * P // 2
            return a

        ints_sb = carve(4 * 512).bitcast(i32)
        edge_bf = carve(6 * 512 // 2).bitcast(bf16)
        step_of_tile = carve(4 * STEPS // 2).bitcast(bf16)
        itmp = carve(2 * 512).bitcast(i32)
        q_parts = carve(BLOCKS * 3 * F // 2).bitcast(bf16)
        attr_ring = carve(5 * GS * P // 2).bitcast(bf16)
        w1_sb = carve(2 * NREL * F)
        w2_sb = carve(NTYPE * F)
        work = carve(2 * 2 * NREL * F + 2 * NTYPE * F)
        relprod = work[:, 0:4 * NREL * F]
        bias_work = work[:, 4 * NREL * F:]
        attr_half = work[:, 0:EP // 32]
        attr_split = work[:, EP // 32:EP // 32 * 5 // 2].bitcast(bf16)
        src_hot = carve(2 * GS * P // 2).bitcast(bf16)
        bucket_hot = carve(2 * GS * BUCKETS // 2).bitcast(bf16)
        w0_pq_sb = carve(2 * F)
        w0_attr_sb = carve(F)
        w0_attr_parts = carve(3 * F // 2).bitcast(bf16)
        w0_out_sb = carve(F)
        b1_sb = carve(F)[0:2 * NREL, :]
        sf = carve(4 * STEPS)
        type9 = carve(STEPS)
        bucket = carve(STEPS)
        tile_row = carve(FRONT + STEPS + SPAN)[0:1, :].bitcast(i32)
        counts = carve(BLOCKS * 2 * NREL)
        upper = carve(P)
        next_row = carve(TROW)[0:TROW, :]
        iota = carve(STEPS)

        lane = sb("lane", [P, P])
        zero_bf = sb("zero_bf", [P, GS * ACC0], bf16)
        iota_bf = sb("iota_bf", [P, BUCKETS], bf16)
        ident = sb("ident", [P, P])
        ident_bf = sb("ident_bf", [P, P], bf16)
        ones = sb("ones", [P, P])
        tile_no = sb("tile_no", [TROW, 4])
        tile_no_bf = sb("tile_no_bf", [TROW, 8], bf16)
        node_base = sb("node_base", [P, BLOCKS])
        small = sb("small", [P, 64])
        node_loc = sb("node_loc", [P, STEPS])
        src_lo = sb("src_lo", [P, STEPS], bf16)
        src_hi = sb("src_hi", [P, STEPS])
        src_idx = sb("src_idx", [P, STEPS + RING * GS], i32)
        rel_idx = sb("rel_idx", [P, STEPS + RING * GS], i32)
        slot_row = sb("slot_row", [1, FRONT + STEPS + SPAN], i32)
        first_row = sb("first_row", [1, 8 + GROUPS + 8], i32)
        block_row = sb("block_row", [1, FRONT + STEPS + SPAN], i32)
        seg_start = sb("seg_start", [SROW, 512])
        row_start = sb("row_start", [1, SROW])
        end_idx = sb("end_idx", [P, BLOCKS], i32)
        X = sb("X", [P, BLOCKS * F])
        xt_area = sb("xt_area", [P, NP_])
        XT = xt_area[0:F + 1, :]
        parts = xt_area[:, :].bitcast(bf16)
        acc = sb("acc", [P, (BLOCKS + GS - 1) * ACC0])
        node_h = sb("node_h", [P, BLOCKS * (F + 2)])
        nA = sb("nA", [P, BLOCKS * F])
        nB = sb("nB", [P, BLOCKS * F])
        picked = nB[:, 0:2 * BATCH * BLOCKS]
        c25 = sb("c25", [P, 16 * BLOCKS])
        idx_ring = sb("idx_ring", [P, RING * GS], i32)
        rows_ring = sb("rows_ring", [P, OWN_ROWS * GS * F])
        hot_ring = sb("hot_ring", [P, HOTS * GS * P], bf16)
        hot_T = sb("hot_T", [P, 2 * GS * P], bf16)
        as_edge = sb("as_edge", [P, STEPS])
        logits = sb("logits", [P, 4 * GS])
        scan = sb("scan", [SROW, 512])
        carry = sb("carry", [1, SROW + 1])
        carry_col = sb("carry_col", [SROW, 1])
        tail = sb("tail", [SROW, 2])
        seg_node = sb("seg_node", [P, BLOCKS])
        as_parts = sb("as_parts", [P, 3 * BLOCKS], bf16)
        adm_parts = sb("adm_parts", [P, BLOCKS * 6], bf16)
        w3_sb = sb("w3_sb", [F, F + 2])
        w3T_sb = sb("w3T_sb", [F, F])
        a3_sb = sb("a3_sb", [F, 2])
        b3_sb = sb("b3_sb", [P, F])

        node_loc_bf = sb("node_loc_bf", [P, STEPS], bf16)
        PS = ctx.enter_context(nc.psum_tensor("PS", [P, 8 * 512], fp32))

        def bank(n, a=0, b=512, p=P):
            return PS[0:p, n * 512 + a:n * 512 + b]

        def part(k, a, w=ACC0):
            v = parts[:, k % 5 * GS * 3 * ACC0:(k % 5 + 1) * GS * 3 * ACC0]
            return v.rearrange("p (s a f) -> p s a f", s=GS, a=3)[:, :, a, 0:w]

        PARTS = 5 * GS * 3 * ACC0 // 2

        def row_slot(k):
            n = (k - START) % RING
            for area, first, count in ((rows_ring[:, :], 0, OWN_ROWS), (nA[:, :], OWN_ROWS, 6),
                                       (xt_area[:, PARTS:], OWN_ROWS + 6, 3)):
                if n < first + count:
                    return area[:, (n - first) * GS * F:(n - first + 1) * GS * F]

        def rows_in_slot(k):
            return row_slot(k).rearrange("p (s f) -> p s f", f=F)

        sort_at = [0]

        def sort_area(cols, p=P):
            sort_at[0] += cols
            assert sort_at[0] <= OWN_ROWS * GS * F
            return rows_ring[0:p, sort_at[0] - cols:sort_at[0]]

        prev_sb = sort_area(512, TROW).bitcast(i32)
        disorder = sort_area(512, TROW)
        record = sort_area(12)
        lo_hi_i = sort_area(2).bitcast(i32)
        lo_hi = sort_area(2)
        dst_col = sort_area(1)
        lo_hot = sort_area(P)
        lo_hot_T = sort_area(P)
        hi_hot = sort_area(BLOCKS)
        place = sort_area(BLOCKS)
        held_place = sort_area(BLOCKS)
        same_before = sort_area(P)
        below = sort_area(P)
        rank = sort_area(4)
        position = sort_area(1).bitcast(i32)
        unsorted_i = sort_area(1, 1).bitcast(i32)

        def in_disorder(engine):
            return nc.values_load_multi_w_load_instructions(
                unsorted_i, engines=[engine], min_val=0, max_val=1,
                skip_runtime_bounds_check_because="a minimum with one")[1][0]

        def group_no(o, k):
            return o * RING + k - START

        def rows_in_count(layer, o, k):
            late = k % RING >= START
            return 64 * (layer * (OUTER if late else OUTER - 1) + o + k // RING + late)

        def messages(k):
            return nB[:, k % 5 * GS * F:(k % 5 + 1) * GS * F].rearrange("p (s f) -> p s f", f=F)

        def scaled_rows(k):
            v = nB[:, k % 5 * GS * GW:(k % 5 + 1) * GS * GW]
            return v.rearrange("p (s f) -> p s f", f=GW)

        def products(b):
            return relprod[:, b % 2 * 2 * NREL * F:(b % 2 + 1) * 2 * NREL * F]

        TABLE_SLOTS = 4

        def rel_stage(b, a, z):
            return work[:, b % TABLE_SLOTS * NTYPE * F + a:b % TABLE_SLOTS * NTYPE * F + z]

        def wait_table(eng):
            for slot in range(TABLE_SLOTS):
                eng.wait_ge(S(f"l2_table{slot}"), 16 * -(-(BLOCKS - slot) // TABLE_SLOTS))

        def wait_rel_slot(eng, b):
            if b >= TABLE_SLOTS:
                eng.wait_ge(S(f"l2_table{b % TABLE_SLOTS}"), 16 * (b // TABLE_SLOTS))

        def xv(t, w=F):
            return t.rearrange("p (b f) -> p b f", f=w)

        def col(n, k=1):
            return c25[:, n * BLOCKS:(n + k) * BLOCKS]

        ORDER = {"l0": 0, "l2": GROUPS, "gat": 2 * GROUPS}
        XG = [min(4, BLOCKS - 4 * q) for q in range(-(-BLOCKS // 4))]

        def pipeline(eng, iteration, lag):
            for k in range(START, RING):
                iteration(0, k)
            with eng.Fori(1, OUTER) as o:
                for k in range(RING):
                    iteration(o, k)
            for k in range(lag):
                iteration(OUTER, k)

        def live(o, k, lag):
            return not isinstance(o, int) or 0 <= group_no(o, k) - lag < GROUPS

        def row_values(row, engine, most, per=GS, front=FRONT):
            held = {}

            def values(o, k, lag):
                if k % 5 == 0:
                    held["now"] = nc.values_load_multi_w_load_instructions(
                        row[0:1, ds((group_no(o, k) - lag) * per + front, 5 * per)], engines=[engine],
                        min_val=0, max_val=most,
                        skip_runtime_bounds_check_because="tile and block numbers by construction")[1]
                return held["now"][k % 5 * per:(k % 5 + 1) * per]
            return values

        def reached(eng, sem, value):
            if not isinstance(value, int) or value > 0:
                eng.wait_ge(sem, value)

        def attr_rests(eng, h):
            w = EP // 32
            eng.wait_ge(S("attr_part0"), h + 1)
            eng.tensor_tensor(attr_half, attr_half, attr_split[:, 0:w], ALU.subtract).then_inc(S("attr_rest"), 1)
            eng.wait_ge(S("attr_part1"), h + 1)
            eng.tensor_tensor(attr_split[:, 2 * w:3 * w], attr_half, attr_split[:, w:2 * w], ALU.subtract)\
                .then_inc(S("attr_split"), 1)

        block = ctx.enter_context(nc.Block())

        @block.sync
        def _(sp):
            sp.dma_start(ints_sb[0:TROW, :].rearrange("q (a f) -> q a f", a=4),
                         ints.rearrange("a (q f) -> q a f", q=TROW)).then_inc(S("ints_in"), 16)
            sp.dma_start(prev_sb, prev_dst.rearrange("a (q f) -> (a q) f", q=TROW)).then_inc(S("ints_in"), 16)
            halves = lambda a: a.rearrange("a (q f) -> (a q) f", q=16).rearrange("p (h f) -> p h f", h=2)
            scratch = attr_parts.rearrange("(a r) (q f) -> (r q) a f", a=3, q=16)
            sp.dma_start(xv(X[:, :]), x.rearrange("(b p) f -> p b f", p=P)).then_inc(S("x_in"), 16)
            for dst, s in ((w0_pq_sb[0:F + 1, :], w0_pq), (w0_attr_sb[0:8, :], w0_attr),
                           (w0_attr_sb[8:16, :], w0_attr), (w0_attr_sb[16:24, :], w0_attr),
                           (w0_out_sb[0:F + 1, :], w0_out), (w1_sb[0:F, :], w1), (b1_sb, b1),
                           (w2_sb[0:F, :], w2)):
                sp.dma_start(dst, s).then_inc(S("w_in"), 16)
            sp.wait_ge(S("order_known"), 1)
            unsorted = in_disorder(mybir.EngineType.SP)
            with sp.If(unsorted > 0):
                with sp.Fori(1, TILES + 1) as t:
                    sp.wait_ge(S("sort_free"), t)
                    sp.sem_inc(S("carrier"), 1)
                    sp.dma_start(record[:, 1:2].bitcast(i32),
                                 ints[1:2, ds((t - 1) * P, P)].rearrange("a p -> p a"),
                                 allow_slow_non_contiguous=True)\
                        .then_inc(S("sort_in"), 16)
                with sp.Fori(1, TILES + 1) as t:
                    sp.wait_ge(S("sort_free"), t + TILES)
                    sp.sem_inc(S("carrier"), 1)
                    sp.dma_start(record[:, 0:4].bitcast(i32),
                                 ints[:, ds((t - 1) * P, P)].rearrange("a p -> p a"),
                                 allow_slow_non_contiguous=True).then_inc(S("sort_in"), 16)
                    sp.dma_start(record[:, 4:12],
                                 attr_t[:, ds((t - 1) * P, P)].rearrange("a p -> p a"),
                                 allow_slow_non_contiguous=True).then_inc(S("sort_in"), 16)
                    sp.wait_ge(S("sort_scattered"), t * 16)
                    sp.sem_inc(S("carrier"), 1)
                with sp.Fori(0, TILES) as t:
                    tile = ds(t * P, P)
                    sp.dma_start(sorted_ints[:, tile],
                                 sorted_edges[tile, 0:4].bitcast(i32).rearrange("p a -> a p"),
                                 allow_slow_non_contiguous=True)\
                        .then_inc(S("sort_split"), 16)
                    sp.dma_start(sorted_attr[:, tile], sorted_edges[tile, 4:12].rearrange("p a -> a p"),
                                 allow_slow_non_contiguous=True)\
                        .then_inc(S("sort_split"), 16)
                sp.wait_ge(S("sort_split"), 32 * TILES)
                sp.dma_start(ints_sb[0:TROW, :].rearrange("q (a f) -> q a f", a=4),
                             sorted_ints.rearrange("a (q f) -> q a f", q=TROW)).then_inc(S("sorted_in"), 16)
                sp.dma_start(attr_half, halves(sorted_attr)[:, 0, :]).then_inc(S("attr_half_in"), 16)
            with sp.Else():
                sp.dma_start(attr_half, halves(attr_t)[:, 0, :]).then_inc(S("attr_half_in"), 16)
            w = EP // 32

            def attr_parts_out(h):
                sp.wait_ge(S("attr_split"), h + 1)
                sp.dma_start(scratch[:, :, h * w:(h + 1) * w],
                             attr_split.rearrange("p (a f) -> p a f", a=3)).then_inc(S("attr_out"), 16)

            attr_parts_out(0)
            sp.wait_ge(S("attr_out"), 16)
            with sp.If(unsorted > 0):
                sp.dma_start(attr_half, halves(sorted_attr)[:, 1, :]).then_inc(S("attr_half_in"), 16)
            with sp.Else():
                sp.dma_start(attr_half, halves(attr_t)[:, 1, :]).then_inc(S("attr_half_in"), 16)
            for q, nb in enumerate(XG):
                sp.wait_ge(S("p_staged"), q + 1)
                sp.dma_start(src_rows.rearrange("(b p) f -> p b f", p=P)[:, 4 * q:4 * q + nb, :],
                             xv(node_h[:, 0:BLOCKS * F])[:, 4 * q:4 * q + nb, :]).then_inc(S("l0_table"), 16)
            attr_parts_out(1)
            sp.wait_ge(S("keys_staged"), 1)
            sp.dma_start(keys[0:1, :], small[0:1, 0:1]).then_inc(S("keys_out"), 16)
            sp.dma_start(keys[1:STEPS * P + 1, :].rearrange("(q f) o -> q (f o)", q=SROW),
                         scan[:, :]).then_inc(S("keys_out"), 16)
            sp.dma_start(seg_max[STEPS * P:STEPS * P + 1, :], small[0:1, 1:2]).then_inc(S("keys_out"), 16)
            sp.wait_ge(S("keys_out"), 48)
            sp.dma_start(seg_start[:, :], keys[0:STEPS * P, :].rearrange("(q f) o -> q (f o)", q=SROW))\
              .then_inc(S("prev_key"), 16)

            sp.wait_ge(S("attr_out"), 32)
            tile_of = row_values(tile_row, mybir.EngineType.SP, TILES - 1)

            def attrs(o, k):
                tiles = tile_of(o, k, 0)
                reached(sp, S("l0_expanded"), group_no(o, k) - 4)
                for s in range(GS):
                    sp.dma_start(attr_ring[0:24, (k % 5 * GS + s) * P:(k % 5 * GS + s + 1) * P],
                                 attr_parts[:, ds(tiles[s] * P, P)]).then_inc(S(f"attr_in{k % 5}"), 16)

            sp.wait_ge(S("steps_ready"), 1)
            pipeline(sp, attrs, 0)

            for b in range(BLOCKS):
                sp.wait_ge(S("rel_staged_v"), b + 1)
                sp.wait_ge(S("rel_staged_a"), b + 1)
                sp.dma_start(rel_rows.rearrange("(n r) f -> n (r f)", r=NTYPE)[b * P:(b + 1) * P, :],
                             rel_stage(b, 0, NTYPE * F)).then_inc(S(f"l2_table{b % TABLE_SLOTS}"), 16)

            for n in range(3):
                if n:
                    sp.wait_ge(S("weights_free"), n)
                sp.dma_start(w3_sb[:, 0:F], w3[n]).then_inc(S("w3_in"), 16)
                sp.dma_start(w3T_sb[:, :], w3_t[n]).then_inc(S("w3_in"), 16)
                sp.dma_start(a3_sb[:, :], a3[n]).then_inc(S("w3_in"), 16)
                if n:
                    sp.wait_ge(S("gat_done"), n * len(XG))
                sp.dma_start(b3_sb[:, :], b3[n].to_broadcast([P, F]))\
                  .then_inc(S("b3_in"), 16)
                for q, nb in enumerate(XG):
                    sp.wait_ge(S("gat_h"), n * len(XG) + q + 1)
                    sp.dma_start(gat_rows[n].rearrange("(b p) f -> p b f", p=P)[:, 4 * q:4 * q + nb, :],
                                 xv(node_h[:, :], F + 2)[:, 4 * q:4 * q + nb, 0:F]).then_inc(S("gat_table"), 16)
                sp.wait_ge(S("gat_scanned"), n + 1)
                sp.dma_start(seg_max[0:STEPS * P, :].rearrange("(q f) o -> q (f o)", q=SROW),
                             scan[:, :]).then_inc(S("seg_max_out"), 16)
            for q, nb in enumerate(XG):
                sp.wait_ge(S("ln_done"), 3 * len(XG) + q + 1)
                full = min(4 * q + nb, N // P) - 4 * q
                if full:
                    sp.dma_start(out[4 * q * P:(4 * q + full) * P, :].rearrange("(b p) f -> p b f", p=P),
                                 xv(X[:, 4 * q * F:(4 * q + full) * F])).then_inc(S("out_done"), 16)
                if full < nb:
                    sp.dma_start(out[N // P * P:N, :], X[0:N % P, N // P * F:BLOCKS * F])\
                        .then_inc(S("out_done"), 16)
            assert (N // P) % 4 == 0 and N % P
            sp.wait_ge(S("out_done"), 16 * len(XG))

        @block.gpsimd
        def _(pool):
            pool.iota(iota, [[1, STEPS]], base=0, channel_multiplier=0,
                      allow_small_or_imprecise_dtypes=True)
            pool.iota(lane[:, :], [[1, P]], base=0, channel_multiplier=0,
                      allow_small_or_imprecise_dtypes=True)
            pool.iota(iota_bf[:, :], [[1, BUCKETS]], base=0, channel_multiplier=0,
                      allow_small_or_imprecise_dtypes=True)
            pool.iota(tile_no[:, :], [[1, 4]], base=0, channel_multiplier=4,
                      allow_small_or_imprecise_dtypes=True)
            pool.iota(tile_no_bf[:, 0:4], [[0, 4]], base=0, channel_multiplier=4,
                      allow_small_or_imprecise_dtypes=True)
            pool.iota(tile_no_bf[:, 4:8], [[1, 4]], base=0, channel_multiplier=0,
                      allow_small_or_imprecise_dtypes=True)
            pool.iota(node_base[:, :], [[P, BLOCKS]], base=-1, channel_multiplier=0,
                      allow_small_or_imprecise_dtypes=True)
            pool.memset(ident[:, :], 0.0)
            pool.memset(ident_bf[:, :], 0.0)
            pool.memset(next_row, 0.0)
            pool.memset(ones[:, :], 1.0)
            pool.memset(upper[:, :], 1.0).then_inc(S("filled"), 1)
            pool.wait_ge(S("filled"), 1)
            for m in (ident, ident_bf):
                pool.affine_select(out=m[:, :], in_=m[:, :], compare_op=ALU.not_equal, fill=1.0,
                                   base=0, pattern=[[-1, P]], channel_multiplier=1)
            pool.affine_select(out=next_row, in_=next_row, compare_op=ALU.not_equal,
                               fill=1.0, base=1, pattern=[[-1, TROW]], channel_multiplier=1)
            pool.affine_select(out=upper[:, :], in_=upper[:, :], compare_op=ALU.is_ge, fill=0.0,
                               base=0, pattern=[[1, P]], channel_multiplier=-1).then_inc(S("consts"), 1)
            pool.wait_ge(S("consts"), 1)
            pool.memset(xt_area[F:F + 1, :], 1.0).then_inc(S("row_of_ones"), 1)
            pool.wait_ge(S("row_of_ones"), 1)
            pool.memset(zero_bf[:, :], 0.0)
            pool.memset(src_idx[:, STEPS:], 0)
            pool.memset(rel_idx[:, STEPS:], 0)
            for row in (block_row, tile_row, slot_row):
                pool.memset(row[:, 0:FRONT], 0)
                pool.memset(row[:, FRONT + STEPS:], 0)
            pool.memset(first_row[:, 0:8], 0)
            pool.memset(first_row[:, 8 + GROUPS:], 0)
            pool.memset(small[:, 0:1], -1.0)
            pool.memset(small[:, 1:2], -BIG)
            pool.memset(small[:, 2:3], EPS)
            pool.memset(carry[:, :], -BIG).then_inc(S("presets"), 1)

            def gathers(li, table, freed, before=0, between=None):

                def group(o, k):
                    if not isinstance(o, int) or group_no(o, k) >= RING:
                        reached(pool, S(freed), before + group_no(o, k) - RING + 1)
                        pool.sem_inc(S("carrier"), 1)
                        pool.wait_ge(S("idx_staged"), li * (GROUPS + 1) + 2 + group_no(o, k) - RING)
                        pool.sem_inc(S("carrier"), 1)
                    for s in range(GS):
                        c = k * GS + s
                        pool.indirect_dma_start(
                            row_slot(k)[:, s * F:(s + 1) * F], None, table,
                            bass.IndirectOffsetOnAxis(ap=idx_ring[:, c:c + 1], axis=0))\
                            .then_inc(S(f"rows_in{k}"), 16)

                pool.wait_ge(S("idx_staged"), li * (GROUPS + 1) + 1)
                for n in range(RING):
                    if li == 0 and n == OWN_ROWS:
                        pool.wait_ge(S("q_parts"), 1)
                    if n == RING - 3 and between:
                        between()
                    group((n + START) // RING, (n + START) % RING)
                return group

            def rest(group):
                for k in range(START, RING):
                    group(1, k)
                with pool.Fori(2, OUTER) as o:
                    for k in range(RING):
                        group(o, k)

            pool.wait_ge(S("order_known"), 1)
            with pool.If(in_disorder(mybir.EngineType.Pool) > 0):
                with pool.Fori(1, TILES + 1) as t:
                    pool.wait_ge(S("sort_placed"), t)
                    pool.sem_inc(S("carrier"), 1)
                    pool.indirect_dma_start(
                        sorted_edges, bass.IndirectOffsetOnAxis(ap=position, axis=0), record, None)\
                        .then_inc(S("sort_scattered"), 16)
            attr_rests(pool, 0)
            pool.wait_ge(S("presets"), 1)
            pool.wait_ge(S("steps_ready"), 1)
            pool.wait_ge(S("l0_table"), 16 * len(XG))
            pool.wait_ge(S("pq_psum"), len(XG))
            for k in range(5):
                pool.memset(part(k, 0)[:, :, F:F + 1], 1.0)
            pool.memset(small[:, 3:4], 0.0).then_inc(S("count_column"), 1)
            rest(gathers(0, src_rows, "l0_pre"))
            for b in range(BLOCKS):
                pool.wait_ge(S("rel1_read"), b + 1)
                z = products(b)
                pool.tensor_tensor(z[:, 0:NREL * F], z[:, 0:NREL * F], z[:, NREL * F:], ALU.add)\
                    .then_inc(S("rel1_folded"), 1)
            wait_table(pool)
            rest(gathers(1, rel_rows, "parts", GROUPS))
            for n in range(3):
                pool.wait_ge(S("gat_table"), 16 * len(XG) * (n + 1))

                def maxima(n=n):
                    pool.wait_ge(S("seg_max_out"), 16 * (n + 1))
                    for b in range(BLOCKS):
                        pool.indirect_dma_start(
                            seg_node[:, b:b + 1], None, seg_max,
                            bass.IndirectOffsetOnAxis(ap=end_idx[:, b:b + 1], axis=0))\
                            .then_inc(S("seg_node_in"), 16)

                rest(gathers(2 + n, gat_rows[n], "gat_scaled", n * GROUPS, maxima))

        @block.scalar
        def _(act):
            A = nc.scalar

            def copy_XT(time, func=ACT.Copy):
                for q, nb in enumerate(XG):
                    act.wait_ge(S("xT_psum"), time * len(XG) + q + 1)
                    A.activation(XT[0:F, q * 512:q * 512 + nb * P], bank(q % 2, 0, nb * P, F), func)\
                        .then_inc(S("xT"), 1)

            def ln_sqrt(n):
                act.wait_ge(S("ln_var"), n + 1)
                A.activation(col(2), col(1), ACT.Sqrt, bias=small[:, 2:3], scale=1.0 / F)\
                    .then_inc(S("ln_std"), 1)

            def first_indices(idx):
                A.activation(idx_ring[:, START * GS:], idx[:, 0:(RING - START) * GS], ACT.Copy)
                A.activation(idx_ring[:, 0:START * GS], idx[:, (RING - START) * GS:RING * GS], ACT.Copy)\
                    .then_inc(S("idx_staged"), 1)

            def next_indices(idx, o, k, lag, li):
                g, kk = group_no(o, k) - lag, (k - lag) % RING
                act.wait_ge(S(f"rows_in{kk}"), rows_in_count(li, o, k - lag))
                A.activation(idx_ring[:, kk * GS:(kk + 1) * GS], idx[:, ds((g + RING) * GS, GS)], ACT.Copy)\
                    .then_inc(S("idx_staged"), 1)

            act.wait_ge(S("ordered"), 1)
            for a, field in ((0, 1), (1, 0), (2, 2), (3, 3)):
                i = A.activation(edge_bf[0:TROW, a * 512:(a + 1) * 512],
                                 ints_sb[0:TROW, field * 512:(field + 1) * 512], ACT.Copy)
            i.then_inc(S("rounded"), 1)
            w = EP // 32

            def attr_parts_of(h):
                act.wait_ge(S("attr_half_in"), 16 * (h + 1))
                if h:
                    act.wait_ge(S("attr_out"), 16)
                A.activation(attr_split[:, 0:w], attr_half, ACT.Copy).then_inc(S("attr_part0"), 1)
                act.wait_ge(S("attr_rest"), h + 1)
                A.activation(attr_split[:, w:2 * w], attr_half, ACT.Copy).then_inc(S("attr_part1"), 1)

            attr_parts_of(0)
            act.wait_ge(S("presets"), 1)
            copy_XT(0)
            for q, nb in enumerate(XG):
                act.wait_ge(S("pq_psum"), q + 1)
                A.activation(xv(node_h[:, q * 4 * F:(q * 4 + nb) * F]),
                             xv(bank(q % 2, 0, nb * P), P)[:, :, 0:F], ACT.Copy)\
                    .then_inc(S("p_staged"), 1)
                A.activation(xv(nA[:, q * 4 * F:(q * 4 + nb) * F]),
                             xv(bank(q % 2, 0, nb * P), P)[:, :, F:2 * F], ACT.Copy)\
                    .then_inc(S("q_read"), 1)

            def first_part(layer, k, lag, value, before, g, func=ACT.Copy, w=F):
                reached(act, S("summed"), ORDER[layer] + before + g - 4)
                A.activation(part(k - lag, 0, w), value, func).then_inc(S("part0"), 1)

            def second_part(layer, k, lag, rest, before, g, w=F):
                act.wait_ge(S("rest"), ORDER[layer] + before + g + 1)
                A.activation(part(k - lag, 1, w), rest, ACT.Copy).then_inc(S("part1"), 1)

            act.wait_ge(S("steps_ready"), 1)
            first_indices(src_idx)
            attr_parts_of(1)


            def l0(o, k):
                if live(o, k, 0):
                    g = group_no(o, k)
                    act.wait_ge(S("l0_hotT_psum"), g + 1)
                    reached(act, S("l0_expanded"), g - 1)
                    A.activation(hot_T[:, k % 2 * 512:k % 2 * 512 + 512],
                                 bank(k % 2).bitcast(bf16)[:, 0:512], ACT.Copy).then_inc(S("l0_hotT"), 1)
                if live(o, k, 2):
                    g = group_no(o, k) - 2
                    act.wait_ge(S("l0_pre"), g + 1)
                    first_part("l0", k, 2, messages(k - 2), 0, g, ACT.Relu)
                    next_indices(src_idx, o, k, 2, 0)
                if live(o, k, 3):
                    second_part("l0", k, 3, messages(k - 3), 0, group_no(o, k) - 3)

            pipeline(act, l0, 3)
            for q, nb in enumerate(XG):
                act.wait_ge(S("sum_T_psum"), q + 1)
                A.activation(XT[0:F + 1, q * 512:q * 512 + nb * P], bank(q % 2, 0, nb * P, F + 1), ACT.Copy)\
                    .then_inc(S("sum_T"), 1)
            ln_sqrt(0)
            copy_XT(1)
            for q, nb in enumerate(XG):
                act.wait_ge(S("counts_T_psum"), q + 1)
                A.activation(bias_work[0:2 * NREL, 0:nb * P], bank(6, 0, nb * P, 2 * NREL), ACT.Copy)\
                    .then_inc(S("counts_T"), 1)
                act.wait_ge(S("count_bias_psum"), q + 1)
                A.activation(node_h[:, q * 4 * F:(q * 4 + nb) * F], bank(7, 0, nb * F), ACT.Copy)\
                    .then_inc(S("count_bias"), 1)
            ln_sqrt(1)
            copy_XT(2)
            for b in range(BLOCKS):
                act.wait_ge(S("rel_psum"), b + 1)
                wait_rel_slot(act, b)
                A.activation(rel_stage(b, 512, 1024),
                             bank(2 + (b % 2) * 2 + 1), ACT.Copy).then_inc(S("rel_staged_a"), 1)

            first_indices(rel_idx)

            def l2(o, k):
                if live(o, k, 0):
                    g = group_no(o, k)
                    if isinstance(o, int) and o == 0 and k == 0:
                        wait_table(act)
                        act.wait_ge(S("arena_free"), 1)
                    act.wait_ge(S("l2_srcT_psum"), g + 1)
                    A.activation(src_hot_T[:, ds(g * GS * P, GS * P)],
                                 bank(k % 2).bitcast(bf16)[:, 0:GS * P], ACT.Copy)\
                        .then_inc(S("l2_srcT"), 1)
                if live(o, k, 2):
                    next_indices(rel_idx, o, k, 2, 1)
                    first_part("l2", k, 2, rows_in_slot(k - 2), 0, group_no(o, k) - 2)
                if live(o, k, 3):
                    second_part("l2", k, 3, rows_in_slot(k - 3), 0, group_no(o, k) - 3)

            pipeline(act, l2, 3)
            ln_sqrt(2)

            for n in range(3):
                copy_XT(3 + n, ACT.Relu if n else ACT.Copy)
                act.wait_ge(S("gat_wa_psum"), n + 1)
                A.activation(w3_sb[:, F:F + 2], bank(7, 0, 2, F), ACT.Copy).then_inc(S("gat_wa"), 1)
                for q, nb in enumerate(XG):
                    act.wait_ge(S("gat_h_psum"), n * len(XG) + q + 1)
                    A.activation(xv(node_h[:, q * 4 * (F + 2):(q * 4 + nb) * (F + 2)], F + 2),
                                 xv(bank(2 + q % 2, 0, nb * (F + 2)), F + 2), ACT.Copy)\
                        .then_inc(S("gat_h"), 1)
                first_indices(src_idx)
                act.wait_ge(S("gat_self_e"), n + 1)
                A.activation(col(8), col(7), ACT.Exp).then_inc(S("gat_self_w"), 1)

                def gat(o, k, n=n, before=n * GROUPS):
                    if live(o, k, 0):
                        g = group_no(o, k)
                        act.wait_ge(S("gat_hotT_psum"), before + g + 1)
                        reached(act, S("gat_expanded"), before + g - 1)
                        A.activation(hot_T[:, k % 2 * 512:k % 2 * 512 + 512],
                                     bank(k % 2).bitcast(bf16)[:, 0:512], ACT.Copy).then_inc(S("gat_hotT"), 1)
                    if live(o, k, 2):
                        g, kk = group_no(o, k) - 2, k - 2
                        act.wait_ge(S("gat_logit"), before + g + 1)
                        reached(act, S("parts"), 2 * GROUPS + before + g - 4)
                        w = scaled_rows(kk)[:, :, F]
                        A.activation(w, logits[:, (2 + kk % 2) * GS:(3 + kk % 2) * GS], ACT.Exp)\
                            .then_inc(S("gat_weight"), 1)
                        act.wait_ge(S("gat_weight"), before + g + 1)
                        act.wait_ge(S(f"rows_in{kk % RING}"), rows_in_count(2 + n, o, kk))
                        for s in range(GS):
                            i = A.activation(scaled_rows(kk)[:, s, 0:F], rows_in_slot(kk)[:, s, :],
                                             ACT.Copy, scale=w[:, s:s + 1])
                        i.then_inc(S("gat_scaled"), 1)
                        next_indices(src_idx, o, k, 2, 2 + n)
                        act.wait_ge(S("gat_scaled"), before + g + 1)
                        first_part("gat", k, 2, scaled_rows(kk), before, g, w=GW)
                    if live(o, k, 3):
                        second_part("gat", k, 3, scaled_rows(k - 3), before, group_no(o, k) - 3, w=GW)

                pipeline(act, gat, 3)
            ln_sqrt(3)

        @block.vector
        def _(dve):
            V = nc.vector
            n_linked = [0]

            def link(ins):
                n_linked[0] += 1
                ins.then_inc(S("dve_chain"), 1)
                dve.wait_ge(S("dve_chain"), n_linked[0])

            dve.wait_ge(S("ints_in"), 32)
            dve.wait_ge(S("presets"), 1)
            src_i, dst_i, t16_i, t9_i = (ints_sb[0:TROW, a * 512:(a + 1) * 512] for a in range(4))
            dst_hi, src_hi_bf, _, _, dst_rest, src_rest = (edge_bf[0:TROW, a * 512:(a + 1) * 512]
                                                           for a in range(6))
            link(V.tensor_tensor(disorder, dst_i, prev_sb, ALU.is_lt))
            V.tensor_reduce(small[0:TROW, 4:5], disorder, axis=AX.X, op=ALU.add).then_inc(S("order_counted"), 1)
            dve.wait_ge(S("order_psum"), 1)
            V.tensor_scalar(unsorted_i, bank(7, 0, 1, 1), 1.0, None, ALU.min).then_inc(S("order_known"), 1)
            dve.wait_ge(S("order_known"), 1)
            with dve.If(in_disorder(mybir.EngineType.DVE) > 0):
                n_sort = [0]

                def sort_link(ins, first, per, t):
                    n_sort[0] += 1
                    ins.then_inc(S("sort_chain"), 1)
                    dve.wait_ge(S("sort_chain"), (t - 1) * per + (first + n_sort[0]))

                def edge_hots(sort_wait):
                    V.tensor_scalar(lo_hi_i[:, 0:1], record[:, 1:2].bitcast(i32), P - 1, None, ALU.bitwise_and)
                    sort_wait(V.tensor_scalar(lo_hi_i[:, 1:2], record[:, 1:2].bitcast(i32), 7, None,
                                              ALU.arith_shift_right))
                    V.tensor_copy(dst_col, record[:, 1:2].bitcast(i32))
                    sort_wait(V.tensor_copy(lo_hi, lo_hi_i))
                    V.tensor_scalar(lo_hot, lane[:, :], lo_hi[:, 0:1], None, ALU.is_equal)
                    V.tensor_scalar(hi_hot, lane[:, 0:BLOCKS], lo_hi[:, 1:2], None, ALU.is_equal)\
                        .then_inc(S("sort_hots"), 1)

                V.memset(place, 0.0)
                V.tensor_scalar(below, upper[:, :], -1.0, 1.0, ALU.mult, ALU.add).then_inc(S("sort_free"), 1)
                with dve.Fori(1, TILES + 1) as t:
                    n_sort[0] = 0
                    dve.wait_ge(S("sort_in"), t * 16)
                    edge_hots(lambda i: sort_link(i, 0, 2, t))
                    dve.wait_ge(S("sort_looked"), t)
                    dve.wait_ge(S("sort_free"), t)
                    V.tensor_tensor(place, place, bank(7, 0, BLOCKS), ALU.add).then_inc(S("sort_free"), 1)
                dve.wait_ge(S("sort_T"), 1)
                dve.wait_ge(S("sort_free"), TILES + 1)
                totals, before = same_before[:, 0:BLOCKS], same_before[:, 32:32 + BLOCKS]
                n_base = [0]

                def base(ins):
                    n_base[0] += 1
                    ins.then_inc(S("sort_base_chain"), 1)
                    dve.wait_ge(S("sort_base_chain"), n_base[0])

                base(V.tensor_tensor(place, bank(7, 32, 32 + BLOCKS), place, ALU.subtract))
                base(V.tensor_copy(totals, bank(7, 64, 64 + BLOCKS)))
                base(V.tensor_tensor_scan(before, ones[:, 0:BLOCKS], totals, 0.0, ALU.mult, ALU.add))
                base(V.tensor_tensor(before, before, totals, ALU.subtract))
                base(V.tensor_tensor(place, place, before, ALU.add))
                with dve.Fori(1, TILES + 1) as t:
                    n_sort[0] = 0
                    chain = lambda i: sort_link(i, 2 * TILES, 8, t)
                    dve.wait_ge(S("sort_in"), t * 32 + 16 * TILES)
                    edge_hots(chain)
                    dve.wait_ge(S("sort_T"), t + 1)
                    V.tensor_copy(held_place, place)
                    V.tensor_copy(lo_hot_T, bank(4, 0, P)).then_inc(S("sort_T_read"), 1)
                    chain(V.scalar_tensor_tensor(out=same_before, in0=bank(4, P, 2 * P), scalar=dst_col,
                                                 in1=below, op0=ALU.is_equal, op1=ALU.mult))
                    chain(V.tensor_reduce(rank[:, 0:1], same_before, axis=AX.X, op=ALU.add))
                    dve.wait_ge(S("sort_looked"), t + TILES)
                    chain(V.tensor_tensor(hi_hot, hi_hot, bank(6, 0, BLOCKS), ALU.mult))
                    chain(V.tensor_reduce(rank[:, 1:2], hi_hot, axis=AX.X, op=ALU.add))
                    chain(V.tensor_tensor(rank[:, 2:3], rank[:, 0:1], rank[:, 1:2], ALU.add))
                    V.tensor_copy(position, rank[:, 2:3]).then_inc(S("sort_placed"), 1)
                    chain(V.tensor_tensor(place, place, bank(7, 0, BLOCKS), ALU.add))
                    V.tensor_copy(rank[:, 3:4], rank[:, 2:3]).then_inc(S("sort_free"), 1)
                dve.wait_ge(S("sorted_in"), 16)
            dve.sem_inc(S("ordered"), 1)
            lb_i = itmp[0:TROW, 0:4]
            link(V.tensor_scalar(lb_i, dst_i.rearrange("q (j f) -> q j f", j=4)[:, :, P - 1], 7, None,
                                 ALU.arith_shift_right))
            last_block = small[0:TROW, 8:12]
            V.tensor_copy(last_block, lb_i).then_inc(S("last_block"), 1)
            dve.wait_ge(S("rounded"), 1)
            V.tensor_tensor(dst_rest, dst_i, dst_hi, ALU.subtract)
            V.tensor_tensor(src_rest, src_i, src_hi_bf, ALU.subtract).then_inc(S("edge_parts"), 1)
            dve.wait_ge(S("prev_block"), 1)
            first, end = small[0:TROW, 12:16], small[0:TROW, 16:20]
            V.tensor_tensor(first[:, 1:4], tile_no[:, 1:4], last_block[:, 0:3], ALU.add)
            V.tensor_tensor(first[:, 0:1], tile_no[:, 0:1], bank(4, 0, 1, TROW), ALU.add)
            link(V.scalar_tensor_tensor(out=end, in0=tile_no[:, :], scalar=1.0, in1=last_block,
                                        op0=ALU.add, op1=ALU.add))
            for j in range(4):
                m = step_of_tile[0:TROW, j * STEPS:(j + 1) * STEPS]
                link(V.tensor_scalar(m, iota[0:TROW, :], first[:, j:j + 1], None, ALU.is_ge))
                i = V.scalar_tensor_tensor(out=m, in0=iota[0:TROW, :], scalar=end[:, j:j + 1], in1=m,
                                           op0=ALU.is_lt, op1=ALU.mult)
            i.then_inc(S("step_of_tile"), 1)
            dve.wait_ge(S("step_psum"), 5)
            blk, tmp, vld = sf[:, 0:STEPS], sf[:, STEPS:2 * STEPS], sf[:, 2 * STEPS:3 * STEPS]
            V.tensor_copy(tile_row[:, FRONT:FRONT + STEPS], bank(2, 0, STEPS, 1))
            V.tensor_copy(src_idx[:, 0:STEPS], bank(4, 0, STEPS))
            link(V.tensor_tensor(blk, iota[:, :], bank(2, 0, STEPS), ALU.subtract))
            V.tensor_copy(block_row[:, FRONT:FRONT + STEPS], blk[0:1, :])
            first_of = blk[0:1, :].rearrange("p (g s) -> p g s", s=GS)[:, :, 0]
            V.tensor_copy(first_row[:, 8:8 + GROUPS], first_of)
            V.tensor_tensor(slot_row[:, FRONT:FRONT + STEPS].rearrange("p (g s) -> p g s", s=GS),
                            blk[0:1, :].rearrange("p (g s) -> p g s", s=GS),
                            first_of.unsqueeze(2).to_broadcast([1, GROUPS, GS]), ALU.subtract)\
                .then_inc(S("steps_ready"), 1)
            V.tensor_copy(type9[:, :], bank(6, 0, STEPS))
            V.scalar_tensor_tensor(out=rel_idx[:, 0:STEPS], in0=src_idx[:, 0:STEPS], scalar=float(NTYPE),
                                   in1=bank(5, 0, STEPS), op0=ALU.mult, op1=ALU.add)
            link(V.scalar_tensor_tensor(out=node_loc[:, :], in0=blk, scalar=-float(P),
                                        in1=bank(3, 0, STEPS), op0=ALU.mult, op1=ALU.add))
            V.tensor_scalar(node_loc_bf[:, :], node_loc[:, :], -1.0, float(P), ALU.max, ALU.min)
            hi_i, lo_i = itmp[:, 0:STEPS], itmp[:, STEPS:2 * STEPS]
            V.tensor_scalar(hi_i, src_idx[:, 0:STEPS], 7, None, ALU.arith_shift_right)
            V.tensor_scalar(lo_i, src_idx[:, 0:STEPS], P - 1, None, ALU.bitwise_and)
            link(V.tensor_scalar(tmp, node_loc[:, :], 0.0, None, ALU.is_ge))
            link(V.scalar_tensor_tensor(out=vld, in0=node_loc[:, :], scalar=float(P), in1=tmp,
                                        op0=ALU.is_lt, op1=ALU.mult))
            V.tensor_copy(src_hi[:, :], hi_i)
            link(V.tensor_copy(tmp, lo_i))
            V.scalar_tensor_tensor(out=bucket[:, :], in0=src_hi[:, :], scalar=float(NREL),
                                   in1=type9[:, :], op0=ALU.mult, op1=ALU.add)
            link(V.scalar_tensor_tensor(out=tmp, in0=tmp, scalar=1.0, in1=vld, op0=ALU.add, op1=ALU.mult))
            V.tensor_scalar(src_lo[:, :], tmp, -1.0, None, ALU.add)
            V.tensor_copy(sf[:, 3 * STEPS:4 * STEPS], bank(3, 0, STEPS)).then_inc(S("dst_step"), 1)

            dve.wait_ge(S("q_read"), len(XG))
            qv = q_parts.rearrange("p (b a f) -> p b a f", a=3, f=F)
            link(V.tensor_copy(qv[:, :, 0, :], xv(nA[:, :])))
            link(V.tensor_tensor(xv(nB[:, :]), xv(nA[:, :]), qv[:, :, 0, :], ALU.subtract))
            link(V.tensor_copy(qv[:, :, 1, :], xv(nB[:, :])))
            link(V.tensor_tensor(xv(nA[:, :]), xv(nB[:, :]), qv[:, :, 1, :], ALU.subtract))
            V.tensor_copy(qv[:, :, 2, :], xv(nA[:, :])).then_inc(S("q_parts"), 1)
            dve.wait_ge(S("keys_psum"), 1)
            V.tensor_copy(scan[:, :], bank(6, 0, 512, SROW)).then_inc(S("keys_staged"), 1)
            attr_rests(dve, 1)
            dve.wait_ge(S("w_in"), 16 * 8)
            wp = lambda a: w0_attr_parts[0:24, a * F:(a + 1) * F]
            w_all = w0_attr_sb[0:24, :]
            link(V.tensor_copy(wp(0), w_all))
            link(V.tensor_tensor(w_all, w_all, wp(0), ALU.subtract))
            link(V.tensor_copy(wp(1), w_all))
            V.tensor_tensor(wp(2), w_all, wp(1), ALU.subtract).then_inc(S("w0_attr_ready"), 1)
            link(V.memset(acc[:, :], 0.0))

            def hots(layer, g, k, before=0):
                reached(dve, S("summed"), ORDER[layer] + before + g - 9)
                return V.tensor_tensor(
                    hot_ring[:, k % HOTS * 512:(k % HOTS + 1) * 512].rearrange("p (s c) -> p s c", s=GS),
                    iota_bf[:, 0:P].unsqueeze(1).to_broadcast([P, GS, P]),
                    node_loc_bf[:, ds(g * GS, GS)].unsqueeze(2).to_broadcast([P, GS, P]), ALU.is_equal)

            def rest_of(layer, k, lag, value, before, g, relu=False, w=F):
                dve.wait_ge(S("part0"), ORDER[layer] + before + g + 1)
                if relu:
                    i = V.scalar_tensor_tensor(out=value, in0=value, scalar=0.0, in1=part(k - lag, 0, w),
                                               op0=ALU.max, op1=ALU.subtract)
                else:
                    i = V.tensor_tensor(value, value, part(k - lag, 0, w), ALU.subtract)
                i.then_inc(S("rest"), 1)

            def third_part(layer, k, lag, rest, before, g, w=F):
                dve.wait_ge(S("part1"), ORDER[layer] + before + g + 1)
                V.tensor_tensor(part(k - lag, 2, w), rest, part(k - lag, 1, w), ALU.subtract)\
                    .then_inc(S("parts"), 1)

            first_block = row_values(first_row, mybir.EngineType.DVE, BLOCKS - 1, 1, 8)

            def add_sums(layer, o, k, w, before=0):
                b, = first_block(o, k, 6)
                if not live(o, k, 6):
                    return
                g, kk = group_no(o, k) - 6, k - 6
                dve.wait_ge(S("summed"), ORDER[layer] + before + g + 1)
                reached(dve, S("added"), ORDER[layer] + before + g)
                a = acc[:, ds(b * w, GS * w)]
                V.tensor_tensor(a, a, bank(4 + kk % 2, 0, GS * w), ALU.add).then_inc(S("added"), 1)

            def l0(o, k):
                if live(o, k, 0):
                    g = group_no(o, k)
                    hots("l0", g, k)
                    reached(dve, S("l0_counted"), g - 1)
                    V.tensor_tensor(
                        src_hot[:, k % 2 * 512:k % 2 * 512 + 512].rearrange("p (s c) -> p s c", s=GS),
                        iota_bf[:, 0:P].unsqueeze(1).to_broadcast([P, GS, P]),
                        src_lo[:, ds(g * GS, GS)].unsqueeze(2).to_broadcast([P, GS, P]), ALU.is_equal)
                    for s in range(GS):
                        at = (k % 2 * GS + s) * BUCKETS
                        i = V.tensor_scalar(bucket_hot[:, at:at + BUCKETS], iota_bf[:, :],
                                            bucket[:, ds(g * GS + s, 1)], None, ALU.is_equal)
                    i.then_inc(S("l0_hots"), 1)
                if live(o, k, 3):
                    rest_of("l0", k, 3, messages(k - 3), 0, group_no(o, k) - 3, relu=True)
                if live(o, k, 2):
                    g, kk = group_no(o, k) - 2, k - 2
                    dve.wait_ge(S(f"rows_in{kk % RING}"), rows_in_count(0, o, kk))
                    dve.wait_ge(S("l0_expanded"), g + 1)
                    reached(dve, S("parts"), g - 4)
                    V.tensor_tensor(messages(kk), rows_in_slot(kk),
                                    xv(bank(2 + kk % 2, 0, 256)), ALU.add).then_inc(S("l0_pre"), 1)
                    reached(dve, S("summed"), g - 4)
                    V.tensor_tensor(part(kk, 0)[:, :, F + 1:ACC0],
                                    lane[:, 0:NREL].unsqueeze(1).to_broadcast([P, GS, NREL]),
                                    type9[:, ds(g * GS, GS)].unsqueeze(2).to_broadcast([P, GS, NREL]),
                                    ALU.is_equal)
                if live(o, k, 4):
                    third_part("l0", k, 4, messages(k - 4), 0, group_no(o, k) - 4)
                add_sums("l0", o, k, ACC0)

            pipeline(dve, l0, 6)
            dve.wait_ge(S("added"), GROUPS)
            dve.wait_ge(S("src_counts"), 1)
            cv = xv(counts[:, :], 2 * NREL)
            av = xv(acc[:, 0:BLOCKS * ACC0], ACC0)
            V.tensor_copy(cv[:, :, 0:NREL], xv(bank(6, 0, BLOCKS * NREL), NREL))
            V.tensor_copy(cv[:, :, NREL:], av[:, :, F + 1:]).then_inc(S("rel_counts"), 1)
            dve.wait_ge(S("rel_counts"), 1)
            link(V.tensor_reduce(col(10), cv, axis=AX.X, op=ALU.add))
            link(V.tensor_scalar(col(10), col(10), 1.0, None, ALU.max))
            V.reciprocal(col(11), col(10))
            link(V.tensor_copy(col(12), av[:, :, F]))
            def layer_norm(n):
                link(V.tensor_reduce(col(0), xv(nA[:, :]), axis=AX.X, op=ALU.add))
                link(V.tensor_scalar(col(0), col(0), 1.0 / F, None, ALU.mult))
                link(V.tensor_tensor(xv(nA[:, :]), xv(nA[:, :]),
                                     col(0).unsqueeze(2).to_broadcast([P, BLOCKS, F]), ALU.subtract))
                link(V.tensor_tensor(nB[:, :], nA[:, :], nA[:, :], ALU.mult))
                V.tensor_reduce(col(1), xv(nB[:, :]), axis=AX.X, op=ALU.add).then_inc(S("ln_var"), 1)
                dve.wait_ge(S("ln_std"), n + 1)
                link(V.reciprocal(col(3), col(2)))
                for q, nb in enumerate(XG):
                    b = slice(4 * q, 4 * q + nb)
                    V.tensor_tensor(xv(X[:, :])[:, b, :], xv(nA[:, :])[:, b, :],
                                    col(3)[:, b].unsqueeze(2).to_broadcast([P, nb, F]), ALU.mult)\
                        .then_inc(S("ln_done"), 1)
                dve.wait_ge(S("ln_done"), (n + 1) * len(XG))

            for q in range(4):
                nb = min(8, BLOCKS - 8 * q)
                dve.wait_ge(S("out0_psum"), q + 1)
                i = V.tensor_tensor(nA[:, q * 512:q * 512 + nb * F], X[:, q * 512:q * 512 + nb * F],
                                    bank(2 + q % 2, 0, nb * F), ALU.add)
                i.then_inc(S("out0_added"), 1)
            dve.wait_ge(S("out0_added"), 4)
            layer_norm(0)

            for b in range(BLOCKS + 1):
                if b < BLOCKS:
                    dve.wait_ge(S("rel1_psum"), b + 1)
                    if b >= 2:
                        dve.wait_ge(S("rel1_sum"), b - 1)
                    z = products(b).rearrange("p (r f) -> p r f", f=F)
                    lo = (b % 2) * 3
                    V.tensor_tensor(z, PS[:, lo * 512:lo * 512 + 2 * NREL * F].rearrange("p (r f) -> p r f", f=F),
                                    cv[:, b, :].unsqueeze(2).to_broadcast([P, 2 * NREL, F]), ALU.mult)\
                        .then_inc(S("rel1_read"), 1)
                if b:
                    dve.wait_ge(S("rel1_folded"), b)
                    z = products(b - 1).rearrange("p (r f) -> p f r", f=F)
                    V.tensor_reduce(nA[:, (b - 1) * F:b * F], z[:, :, 0:NREL], axis=AX.X, op=ALU.add)\
                        .then_inc(S("rel1_sum"), 1)
            dve.wait_ge(S("rel1_sum"), BLOCKS)
            dve.wait_ge(S("count_bias"), len(XG))
            link(V.tensor_tensor(nA[:, :], nA[:, :], node_h[:, 0:BLOCKS * F], ALU.add))
            link(V.tensor_tensor(xv(nA[:, :]), xv(nA[:, :]),
                                 col(11).unsqueeze(2).to_broadcast([P, BLOCKS, F]), ALU.mult))
            link(V.tensor_tensor(nA[:, :], nA[:, :], X[:, :], ALU.add))
            layer_norm(1)

            for b in range(BLOCKS):
                dve.wait_ge(S("rel_psum"), b + 1)
                wait_rel_slot(dve, b)
                V.tensor_copy(rel_stage(b, 0, 512),
                              bank(2 + (b % 2) * 2)).then_inc(S("rel_staged_v"), 1)
            V.tensor_scalar(col(13), col(12), 0.0, None, ALU.is_gt).then_inc(S("degree"), 1)
            dve.wait_ge(S("degree_psum"), 1)
            link(V.tensor_copy(col(14), bank(7, 32, 32 + BLOCKS)))
            link(V.tensor_tensor_scan(col(15), ones[:, 0:BLOCKS],
                                      col(14), 0.0, ALU.mult, ALU.add))
            link(V.tensor_tensor(col(15), col(15), col(14), ALU.subtract))
            link(V.tensor_tensor(col(15), col(15), node_base[:, :], ALU.add))
            link(V.tensor_tensor(col(15), col(15), bank(7, 0, BLOCKS), ALU.add))
            link(V.tensor_scalar(col(15), col(15), -float(STEPS * P), None, ALU.add))
            link(V.tensor_tensor(col(15), col(15), col(13), ALU.mult))
            V.tensor_scalar(end_idx[:, :], col(15), float(STEPS * P), None, ALU.add)

            dve.wait_ge(S("prev_key"), 16)
            link(V.tensor_tensor(seg_start[:, :], scan[:, :], seg_start[:, :], ALU.not_equal))
            link(V.tensor_reduce(tail[:, 0:1], seg_start[:, :], axis=AX.X, op=ALU.max))
            link(V.tensor_scalar(tail[:, 1:2], tail[:, 0:1], -BIG, None, ALU.mult))
            V.tensor_scalar(seg_start[:, :], seg_start[:, :], -BIG, None, ALU.mult)\
                .then_inc(S("row_start_in"), 1)
            dve.wait_ge(S("row_start_psum"), 1)
            link(V.tensor_copy(row_start[:, :], bank(7, 64, 64 + SROW, 1)))

            dve.wait_ge(S("rel_staged_v"), BLOCKS)
            V.memset(acc[:, :], 0.0).then_inc(S("arena_free"), 1)
            dve.wait_ge(S("arena_free"), 1)

            def l2(o, k):
                if live(o, k, 0):
                    g = group_no(o, k)
                    hots("l2", g, k)
                    reached(dve, S("l2_srcT_psum"), g - 1)
                    V.tensor_tensor(
                        hot_T[:, k % 2 * 512:k % 2 * 512 + 512].rearrange("p (s c) -> p s c", s=GS),
                        iota_bf[:, 0:P].unsqueeze(1).to_broadcast([P, GS, P]),
                        src_lo[:, ds(g * GS, GS)].unsqueeze(2).to_broadcast([P, GS, P]), ALU.is_equal)\
                        .then_inc(S("l2_hots"), 1)
                if live(o, k, 3):
                    rest_of("l2", k, 3, rows_in_slot(k - 3), 0, group_no(o, k) - 3)
                if live(o, k, 4):
                    third_part("l2", k, 4, rows_in_slot(k - 4), 0, group_no(o, k) - 4)
                add_sums("l2", o, k, F)

            pipeline(dve, l2, 6)
            dve.wait_ge(S("added"), GROUPS + GROUPS)
            link(V.tensor_tensor(nA[:, :], X[:, :], acc[:, 0:BLOCKS * F], ALU.add))
            layer_norm(2)

            def split3(dst, value, rest):
                link(V.tensor_copy(dst(0), value))
                link(V.tensor_tensor(rest, value, dst(0), ALU.subtract))
                link(V.tensor_copy(dst(1), rest))
                link(V.tensor_tensor(rest, rest, dst(1), ALU.subtract))
                return V.tensor_copy(dst(2), rest)

            for n in range(3):
                dve.wait_ge(S("gat_h"), (n + 1) * len(XG))
                hv = xv(node_h[:, :], F + 2)
                V.tensor_copy(col(4), hv[:, :, F])
                link(V.tensor_copy(col(5), hv[:, :, F + 1]))
                split3(lambda a: as_parts[:, a * BLOCKS:(a + 1) * BLOCKS], col(4), col(6))\
                    .then_inc(S("gat_as_parts"), 1)

                def pick(o, before=n * BATCHES):
                    for half in range(2):
                        batch = 2 * o + half
                        reached(dve, S("gat_picked"), before + batch - 1)
                        pv = picked[:, half * 500:half * 500 + 500].rearrange("p (s c) -> p s c", c=BLOCKS)
                        V.tensor_tensor(pv, lane[:, 0:BLOCKS].unsqueeze(1).to_broadcast([P, BATCH, BLOCKS]),
                                        src_hi[:, ds(batch * BATCH, BATCH)].unsqueeze(2)
                                        .to_broadcast([P, BATCH, BLOCKS]), ALU.is_equal).then_inc(S("gat_p1"), 1)
                        dve.wait_ge(S("gat_as_psum"), before + batch + 1)
                        dve.wait_ge(S("gat_p1"), 2 * (before + batch) + 1)
                        V.tensor_tensor(pv, pv, bank(4 + half, 0, 500).rearrange("p (s c) -> p s c", c=BLOCKS),
                                        ALU.mult).then_inc(S("gat_p1"), 1)
                        dve.wait_ge(S("gat_p1"), 2 * (before + batch) + 2)
                        V.tensor_reduce(as_edge[:, ds(batch * BATCH, BATCH)], pv, axis=AX.X, op=ALU.add)\
                            .then_inc(S("gat_picked"), 1)

                pick(0)
                with dve.Fori(1, BATCHES // 2) as o:
                    pick(o)
                dve.wait_ge(S("gat_asT_psum"), n + 1)
                V.tensor_tensor_scan(scan[:, :], seg_start[:, :], bank(6, 0, 512, SROW), -BIG,
                                     ALU.add, ALU.max).then_inc(S("gat_scan1"), 1)
                dve.wait_ge(S("gat_tail_psum"), n + 1)
                V.tensor_tensor_scan(carry[:, 1:SROW + 1], row_start[:, :], bank(7, 0, SROW, 1), -BIG,
                                     ALU.add, ALU.max).then_inc(S("gat_carry"), 1)
                dve.wait_ge(S("gat_carry_psum"), n + 1)
                link(V.tensor_copy(carry_col[:, :], bank(7, 128, 129, SROW)))
                V.tensor_tensor_scan(scan[:, :], seg_start[:, :], bank(6, 0, 512, SROW), carry_col[:, 0:1],
                                     ALU.add, ALU.max).then_inc(S("gat_scanned"), 1)
                dve.wait_ge(S("seg_node_in"), 16 * BLOCKS * (n + 1))
                link(V.tensor_tensor(col(6), seg_node[:, :], col(4), ALU.max))
                link(V.tensor_tensor(col(6), col(6), col(5), ALU.add))
                link(V.scalar_tensor_tensor(out=col(6), in0=col(6), scalar=0.2, in1=col(6),
                                            op0=ALU.mult, op1=ALU.max))
                link(V.tensor_tensor(col(7), col(4), col(5), ALU.add))
                link(V.scalar_tensor_tensor(out=col(7), in0=col(7), scalar=0.2, in1=col(7),
                                            op0=ALU.mult, op1=ALU.max))
                V.tensor_tensor(col(7), col(7), col(6), ALU.subtract).then_inc(S("gat_self_e"), 1)
                mv = adm_parts[:, :].rearrange("p (b a c) -> p b a c", a=3, c=2)
                link(split3(lambda a: mv[:, :, a, 0], col(5), col(9)))
                split3(lambda a: mv[:, :, a, 1], col(6), col(9)).then_inc(S("gat_adm_parts"), 1)
                dve.wait_ge(S("gat_self_w"), n + 1)
                sv = acc[:, 0:BLOCKS * GW].rearrange("p (b f) -> p b f", f=GW)
                wide = lambda c: col(c).unsqueeze(2).to_broadcast([P, BLOCKS, F])
                V.memset(acc[:, BLOCKS * GW:], 0.0)
                V.tensor_copy(sv[:, :, F], col(8))
                link(V.tensor_tensor(sv[:, :, 0:F], hv[:, :, 0:F], wide(8), ALU.mult))

                def gat(o, k, before=n * GROUPS):
                    if live(o, k, 0):
                        g = group_no(o, k)
                        hots("gat", g, k, before).then_inc(S("gat_hots"), 1)
                    if live(o, k, 2):
                        g, kk = group_no(o, k) - 2, k - 2
                        dve.wait_ge(S("gat_expanded"), before + g + 1)
                        reached(dve, S("gat_weight"), before + g - 1)
                        z = logits[:, kk % 2 * GS:(kk % 2 + 1) * GS]
                        ev = bank(2 + kk % 2, 0, 2 * GS).rearrange("p (s c) -> p s c", c=2)
                        V.tensor_tensor(z, as_edge[:, ds(g * GS, GS)], ev[:, :, 0], ALU.add)\
                            .then_inc(S("gat_z"), 1)
                        dve.wait_ge(S("gat_z"), 2 * (before + g) + 1)
                        V.scalar_tensor_tensor(out=z, in0=z, scalar=0.2, in1=z, op0=ALU.mult, op1=ALU.max)\
                            .then_inc(S("gat_z"), 1)
                        dve.wait_ge(S("gat_z"), 2 * (before + g) + 2)
                        V.tensor_tensor(logits[:, (2 + kk % 2) * GS:(3 + kk % 2) * GS], z, ev[:, :, 1],
                                        ALU.subtract).then_inc(S("gat_logit"), 1)
                    if live(o, k, 3):
                        rest_of("gat", k, 3, scaled_rows(k - 3), before, group_no(o, k) - 3, w=GW)
                    if live(o, k, 4):
                        third_part("gat", k, 4, scaled_rows(k - 4), before, group_no(o, k) - 4, w=GW)
                    add_sums("gat", o, k, GW, before)

                pipeline(dve, gat, 6)
                dve.wait_ge(S("added"), 2 * GROUPS + (n + 1) * GROUPS)
                link(V.tensor_scalar(col(9), sv[:, :, F], 1e-16, None, ALU.add))
                link(V.reciprocal(col(7), col(9)))
                dve.wait_ge(S("b3_in"), 16 * (n + 1))
                for q, nb in enumerate(XG):
                    for b in range(4 * q, 4 * q + nb):
                        i = V.scalar_tensor_tensor(out=nA[:, b * F:(b + 1) * F], in0=sv[:, b, 0:F],
                                                   scalar=col(7)[:, b:b + 1], in1=b3_sb[:, :],
                                                   op0=ALU.mult, op1=ALU.add)
                    i.then_inc(S("gat_done"), 1)
                if n == 2:
                    dve.wait_ge(S("gat_done"), 3 * len(XG))
                    link(V.tensor_tensor(nA[:, :], X[:, :], nA[:, :], ALU.add))
            layer_norm(3)

        @block.tensor
        def _(pe):
            T = nc.tensor

            def transpose_X(time, src_tile, ready=None, before=0):
                for q, nb in enumerate(XG):
                    if ready:
                        pe.wait_ge(S(ready), before * len(XG) + q + 1)
                    if q >= 2:
                        pe.wait_ge(S("xT"), time * len(XG) + q - 1)
                    for s in range(nb):
                        b = 4 * q + s
                        i = T.transpose(bank(q % 2, s * P, (s + 1) * P, F), src_tile[:, b * F:(b + 1) * F],
                                        ident[:, :])
                    i.then_inc(S("xT_psum"), 1)

            pe.wait_ge(S("consts"), 1)
            pe.wait_ge(S("order_counted"), 1)
            T.matmul(bank(7, 0, 1, 1), ones[0:TROW, 0:1], small[0:TROW, 4:5], start=True, stop=True)\
                .then_inc(S("order_psum"), 1)
            pe.wait_ge(S("order_known"), 1)
            with pe.If(in_disorder(mybir.EngineType.PE) > 0):
                with pe.Fori(1, TILES + 1) as t:
                    pe.wait_ge(S("sort_hots"), t)
                    pe.wait_ge(S("sort_free"), t)
                    T.matmul(bank(7, 0, BLOCKS), lo_hot, hi_hot, start=True, stop=True)\
                        .then_inc(S("sort_looked"), 1)
                pe.wait_ge(S("sort_free"), TILES + 1)
                T.matmul(bank(7, 32, 32 + BLOCKS), upper[:, :], place, start=True, stop=True)
                T.matmul(bank(7, 64, 64 + BLOCKS), ones[:, :], place, start=True, stop=True)\
                    .then_inc(S("sort_T"), 1)
                with pe.Fori(1, TILES + 1) as t:
                    pe.wait_ge(S("sort_hots"), t + TILES)
                    pe.wait_ge(S("sort_free"), t + TILES)
                    T.transpose(bank(4, 0, P), lo_hot, ident[:, :])
                    T.transpose(bank(4, P, 2 * P), dst_col.to_broadcast([P, P]), ident[:, :])\
                        .then_inc(S("sort_T"), 1)
                    pe.wait_ge(S("sort_T_read"), t)
                    T.matmul(bank(7, 0, BLOCKS), lo_hot, hi_hot, start=True, stop=True)
                    T.matmul(bank(6, 0, BLOCKS), lo_hot_T, held_place, start=True, stop=True)\
                        .then_inc(S("sort_looked"), 1)
            pe.wait_ge(S("last_block"), 1)
            T.matmul(bank(4, 0, 1, TROW), next_row, small[0:TROW, 11:12], start=True, stop=True)\
                .then_inc(S("prev_block"), 1)
            pe.wait_ge(S("x_in"), 16)
            transpose_X(0, X)
            pe.wait_ge(S("step_of_tile"), 1)
            pe.wait_ge(S("edge_parts"), 1)
            on_steps = lambda j: step_of_tile[0:TROW, j * STEPS:(j + 1) * STEPS]
            for j in range(4):
                for a in range(2):
                    i = T.matmul(bank(2, 0, STEPS), tile_no_bf[:, a * 4 + j:a * 4 + j + 1].to_broadcast([TROW, P]),
                                 on_steps(j), start=j + a == 0, stop=j + a == 4)
            i.then_inc(S("step_psum"), 1)
            for n, fields in enumerate(((0, 4), (1, 5), (2,), (3,))):
                for j in range(4):
                    for a in fields:
                        i = T.matmul(bank(3 + n, 0, STEPS), edge_bf[0:TROW, a * 512 + j * P:a * 512 + (j + 1) * P],
                                     on_steps(j), start=j == 0 and a == fields[0],
                                     stop=j == 3 and a == fields[-1])
                i.then_inc(S("step_psum"), 1)
            pe.wait_ge(S("w_in"), 16 * 8)
            pe.wait_ge(S("xT"), len(XG))
            for q, nb in enumerate(XG):
                if q >= 2:
                    pe.wait_ge(S("q_read"), q - 1)
                for s in range(nb):
                    b = 4 * q + s
                    i = T.matmul(bank(q % 2, s * P, (s + 1) * P), XT[:, b * P:(b + 1) * P],
                                 w0_pq_sb[0:F + 1, :], start=True, stop=True)
                i.then_inc(S("pq_psum"), 1)
            pe.wait_ge(S("dst_step"), 1)
            for j in range(4):
                i = T.transpose(bank(6, j * P, (j + 1) * P, SROW),
                                sf[:, 3 * STEPS:4 * STEPS].rearrange("p (q j) -> p j q", j=4)[:, j, :],
                                ident[:, :])
            i.then_inc(S("keys_psum"), 1)

            def sums(layer, o, k, w, values_w, before=0):
                slots = slot_of(o, k, 5)
                if not live(o, k, 5):
                    return
                g, kk = group_no(o, k) - 5, k - 5
                pe.wait_ge(S("parts"), ORDER[layer] + before + g + 1)
                reached(pe, S("added"), ORDER[layer] + before + g - 1)
                b = 4 + kk % 2
                for s in range(GS):
                    h = (kk % HOTS * GS + s) * P
                    if s == 0:
                        T.matmul(bank(b, 0, GS * w), hot_ring[:, h:h + P], zero_bf[:, 0:GS * w], start=True,
                                 stop=False, skip_group_check=True)
                    for a in range(3):
                        n_cols = w if a == 0 else values_w
                        i = T.matmul(PS[:, ds(slots[s] * w + b * 512, n_cols)], hot_ring[:, h:h + P],
                                     part(kk, a, n_cols)[:, s, :], start=False,
                                     stop=s == GS - 1 and a == 2, skip_group_check=True)
                i.then_inc(S("summed"), 1)

            def transpose_hots(layer, k, g, before=0):
                reached(pe, S(f"{layer}_hotT"), before + g - 1)
                for s in range(GS):
                    h = (k % HOTS * GS + s) * P
                    i = T.transpose(bank(k % 2).bitcast(bf16)[:, s * P:(s + 1) * P], hot_ring[:, h:h + P],
                                    ident_bf[:, :])
                i.then_inc(S(f"{layer}_hotT_psum"), 1)

            slot_of = row_values(slot_row, mybir.EngineType.PE, GS - 1)
            block_of = row_values(block_row, mybir.EngineType.PE, BLOCKS - 1)

            pe.wait_ge(S("q_parts"), 1)
            pe.wait_ge(S("q_read"), len(XG))
            pe.wait_ge(S("steps_ready"), 1)
            pe.wait_ge(S("keys_staged"), 1)
            pe.wait_ge(S("w0_attr_ready"), 1)
            pe.wait_ge(S("count_column"), 1)
            T.matmul(bank(6, 0, BUCKETS), ident_bf[:, :], zero_bf[:, 0:BUCKETS], start=True, stop=False,
                     skip_group_check=True)

            def l0(o, k):
                bs = block_of(o, k, 1)
                sums("l0", o, k, ACC0, F)
                if live(o, k, 1):
                    g, kk = group_no(o, k) - 1, k - 1
                    pe.wait_ge(S("l0_hotT"), g + 1)
                    reached(pe, S("l0_pre"), g - 1)
                    pe.wait_ge(S(f"attr_in{kk % 5}"), 64 * (4 * o + kk // 5 - 1))
                    for s in range(GS):
                        ps = bank(2 + kk % 2, s * F, (s + 1) * F)
                        e = (kk % 5 * GS + s) * P
                        for a in range(3):
                            T.matmul(ps, attr_ring[0:24, e:e + P], w0_attr_parts[0:24, a * F:(a + 1) * F],
                                     start=a == 0, stop=False)
                        for a in range(3):
                            i = T.matmul(ps, hot_T[:, (kk % 2 * GS + s) * P:(kk % 2 * GS + s + 1) * P],
                                         q_parts[:, ds(bs[s] * (3 * F) + a * F, F)], start=False, stop=a == 2)
                    i.then_inc(S("l0_expanded"), 1)
                if live(o, k, 0):
                    g = group_no(o, k)
                    pe.wait_ge(S("l0_hots"), g + 1)
                    transpose_hots("l0", k, g)
                    for s in range(GS):
                        i = T.matmul(bank(6, 0, BUCKETS),
                                     src_hot[:, (k % 2 * GS + s) * P:(k % 2 * GS + s + 1) * P],
                                     bucket_hot[:, (k % 2 * GS + s) * BUCKETS:(k % 2 * GS + s + 1) * BUCKETS],
                                     start=False, stop=False, skip_group_check=True)
                    i.then_inc(S("l0_counted"), 1)

            pipeline(pe, l0, 5)
            T.matmul(bank(6, 0, BUCKETS), ident_bf[:, :], zero_bf[:, 0:BUCKETS], start=False, stop=True,
                     skip_group_check=True).then_inc(S("src_counts"), 1)
            pe.wait_ge(S("added"), GROUPS)
            for q, nb in enumerate(XG):
                if q >= 2:
                    pe.wait_ge(S("sum_T"), q - 1)
                for s in range(nb):
                    b = 4 * q + s
                    i = T.transpose(bank(q % 2, s * P, (s + 1) * P, F + 1),
                                    acc[:, b * ACC0:b * ACC0 + F + 1], ident[:, :])
                i.then_inc(S("sum_T_psum"), 1)
            for q in range(4):
                nb = min(8, BLOCKS - 8 * q)
                pe.wait_ge(S("sum_T"), min(len(XG), 2 * q + 2))
                if q >= 2:
                    pe.wait_ge(S("out0_added"), q - 1)
                for s in range(nb):
                    b = 8 * q + s
                    i = T.matmul(bank(2 + q % 2, s * F, (s + 1) * F), XT[:, b * P:(b + 1) * P],
                                 w0_out_sb[0:F + 1, :], start=True, stop=True)
                i.then_inc(S("out0_psum"), 1)

            pe.wait_ge(S("rel_counts"), 1)

            def transpose_counts(q):
                if q:
                    pe.wait_ge(S("counts_T"), q)
                for s in range(XG[q]):
                    i = T.transpose(bank(6, s * P, (s + 1) * P, 2 * NREL),
                                    counts[:, (4 * q + s) * 2 * NREL:(4 * q + s + 1) * 2 * NREL], ident[:, :])
                i.then_inc(S("counts_T_psum"), 1)

            def counts_times_biases(q):
                pe.wait_ge(S("counts_T"), q + 1)
                if q:
                    pe.wait_ge(S("count_bias"), q)
                for s in range(XG[q]):
                    i = T.matmul(bank(7, s * F, (s + 1) * F), bias_work[0:2 * NREL, s * P:(s + 1) * P],
                                 b1_sb, start=True, stop=True)
                i.then_inc(S("count_bias_psum"), 1)

            transpose_X(1, X, "ln_done", 0)
            pe.wait_ge(S("xT"), 2 * len(XG))
            for b in range(BLOCKS):
                if b >= 2:
                    pe.wait_ge(S("rel1_read"), b - 1)
                lo = (b % 2) * 3
                for a in range(0, 2 * NREL * F, 512):
                    w = min(512, 2 * NREL * F - a)
                    i = T.matmul(PS[:, lo * 512 + a:lo * 512 + a + w], XT[0:F, b * P:(b + 1) * P],
                                 w1_sb[0:F, a:a + w], start=True, stop=True)
                i.then_inc(S("rel1_psum"), 1)
                if b % 3 == 0 and b // 3 < len(XG):
                    transpose_counts(b // 3)
                elif b % 3 == 1 and b // 3 < len(XG):
                    counts_times_biases(b // 3)

            transpose_X(2, X, "ln_done", 1)
            pe.wait_ge(S("xT"), 3 * len(XG))
            for b in range(BLOCKS):
                if b >= 2:
                    pe.wait_ge(S("rel_staged_v"), b - 1)
                    pe.wait_ge(S("rel_staged_a"), b - 1)
                for a in range(2):
                    i = T.matmul(bank(2 + (b % 2) * 2 + a), XT[0:F, b * P:(b + 1) * P],
                                 w2_sb[0:F, a * 512:(a + 1) * 512], start=True, stop=True)
                i.then_inc(S("rel_psum"), 1)
            pe.wait_ge(S("degree"), 1)
            T.matmul(bank(7, 0, BLOCKS), upper[:, :], col(12), start=True, stop=True)
            T.matmul(bank(7, 32, 32 + BLOCKS), ones[:, :], col(12), start=True, stop=True)\
                .then_inc(S("degree_psum"), 1)
            pe.wait_ge(S("row_start_in"), 1)
            T.transpose(bank(7, 64, 64 + SROW, 1), tail[:, 1:2], ident[0:SROW, 0:SROW])\
                .then_inc(S("row_start_psum"), 1)
            pe.wait_ge(S("arena_free"), 1)

            def l2(o, k):
                sums("l2", o, k, F, F)
                if live(o, k, 0):
                    g = group_no(o, k)
                    pe.wait_ge(S("l2_hots"), g + 1)
                    reached(pe, S("l2_srcT"), g - 1)
                    for s in range(GS):
                        i = T.transpose(bank(k % 2).bitcast(bf16)[:, s * P:(s + 1) * P],
                                        hot_T[:, (k % 2 * GS + s) * P:(k % 2 * GS + s + 1) * P], ident_bf[:, :])
                    i.then_inc(S("l2_srcT_psum"), 1)

            pipeline(pe, l2, 5)
            pe.wait_ge(S("l2_srcT"), GROUPS)

            for n in range(3):
                pe.wait_ge(S("w3_in"), 48 * (n + 1))
                T.matmul(bank(7, 0, 2, F), w3T_sb[:, :], a3_sb[:, :], start=True, stop=True)\
                    .then_inc(S("gat_wa_psum"), 1)
                if n == 0:
                    transpose_X(3, X, "ln_done", 2)
                else:
                    transpose_X(3 + n, nA, "gat_done", n - 1)
                pe.wait_ge(S("gat_wa"), n + 1)
                for q, nb in enumerate(XG):
                    pe.wait_ge(S("xT"), (3 + n) * len(XG) + q + 1)
                    if q >= 2:
                        pe.wait_ge(S("gat_h"), n * len(XG) + q - 1)
                    for s in range(nb):
                        b = 4 * q + s
                        i = T.matmul(bank(2 + q % 2, s * (F + 2), (s + 1) * (F + 2)),
                                     XT[0:F, b * P:(b + 1) * P], w3_sb[:, :], start=True, stop=True)
                    i.then_inc(S("gat_h_psum"), 1)
                pe.wait_ge(S("gat_h_psum"), (n + 1) * len(XG))
                pe.sem_inc(S("weights_free"), 1)
                pe.wait_ge(S("gat_as_parts"), n + 1)

                def look_up(o, before=n * BATCHES):
                    for half in range(2):
                        batch = 2 * o + half
                        reached(pe, S("gat_picked"), before + batch - 1)
                        for s in range(BATCH):
                            for a in range(3):
                                i = T.matmul(bank(4 + half, s * BLOCKS, (s + 1) * BLOCKS),
                                             src_hot_T[:, ds((batch * BATCH + s) * P, P)],
                                             as_parts[:, a * BLOCKS:(a + 1) * BLOCKS], start=a == 0, stop=a == 2)
                        i.then_inc(S("gat_as_psum"), 1)

                look_up(0)
                with pe.Fori(1, BATCHES // 2) as o:
                    look_up(o)
                pe.wait_ge(S("gat_picked"), (n + 1) * BATCHES)
                for j in range(4):
                    i = T.transpose(bank(6, j * P, (j + 1) * P, SROW),
                                    as_edge[:, :].rearrange("p (q j) -> p j q", j=4)[:, j, :], ident[:, :])
                i.then_inc(S("gat_asT_psum"), 1)
                pe.wait_ge(S("gat_scan1"), n + 1)
                T.transpose(bank(7, 0, SROW, 1), scan[:, 511:512], ident[0:SROW, 0:SROW])\
                    .then_inc(S("gat_tail_psum"), 1)
                pe.wait_ge(S("gat_carry"), n + 1)
                T.matmul(bank(7, 128, 129, SROW), carry[0:1, 0:SROW], ones[0:1, 0:1], start=True, stop=True)\
                    .then_inc(S("gat_carry_psum"), 1)
                pe.wait_ge(S("gat_adm_parts"), n + 1)

                def gat(o, k, before=n * GROUPS):
                    bs = block_of(o, k, 1)
                    sums("gat", o, k, GW, GW, before)
                    if live(o, k, 1):
                        g, kk = group_no(o, k) - 1, k - 1
                        pe.wait_ge(S("gat_hotT"), before + g + 1)
                        reached(pe, S("gat_logit"), before + g - 1)
                        for s in range(GS):
                            for a in range(3):
                                i = T.matmul(bank(2 + kk % 2, 2 * s, 2 * s + 2),
                                             hot_T[:, (kk % 2 * GS + s) * P:(kk % 2 * GS + s + 1) * P],
                                             adm_parts[:, ds(bs[s] * 6 + 2 * a, 2)], start=a == 0, stop=a == 2)
                        i.then_inc(S("gat_expanded"), 1)
                    if live(o, k, 0):
                        g = group_no(o, k)
                        pe.wait_ge(S("gat_hots"), before + g + 1)
                        transpose_hots("gat", k, g, before)

                pipeline(pe, gat, 5)


_INS = ["x", "ints", "prev_dst", "attr_t", "w0_pq", "w0_attr", "w0_out", "w1", "b1", "w2", "w3", "w3_t",
        "a3", "b3"]


def laid_out(inputs):
    import numpy as np
    f = lambda n: np.asarray(inputs[n])
    f32, i32 = np.float32, np.int32
    padded = lambda a, v: np.concatenate([a, np.full(EP - E, v, i32)])
    return {
        "x": np.concatenate([f("x"), np.zeros((NP_ - N, F), f32)]),
        "ints": np.stack([padded(f("src"), NP_ - 1), padded(f("dst"), NP_ - 1),
                          padded(f("edge_type_16"), 0), padded(f("edge_type_9"), 0)]),
        "prev_dst": np.concatenate([f("dst")[:1], padded(f("dst"), NP_ - 1)[:-1]])[None],
        "attr_t": np.ascontiguousarray(np.concatenate([f("edge_attr_8"), np.zeros((EP - E, 8), f32)]).T),
        "w0_pq": np.concatenate([
            np.concatenate([f("L0_gnn_W1")[0:F], f("L0_gnn_W1")[F:2 * F]], axis=1),
            np.concatenate([np.zeros(F, f32), f("L0_gnn_b1")])[None]]),
        "w0_attr": np.ascontiguousarray(f("L0_gnn_W1")[2 * F:]),
        "w0_out": np.concatenate([f("L0_gnn_W2"), f("L0_gnn_b2")[None]]),
        "w1": np.ascontiguousarray(f("L1_gnn_weights")[-1].transpose(1, 0, 2).reshape(F, 2 * NREL * F)),
        "b1": np.ascontiguousarray(f("L1_gnn_biases")[-1]),
        "w2": np.ascontiguousarray(f("L2_gnn_weight").transpose(1, 0, 2).reshape(F, NTYPE * F)),
        "w3": np.stack([f(f"L3_gnn_W{n}") for n in (1, 2, 3)]),
        "w3_t": np.ascontiguousarray(np.stack([f(f"L3_gnn_W{n}").T for n in (1, 2, 3)])),
        "a3": np.ascontiguousarray(np.stack([np.stack([f(f"L3_gnn_a{n}s"), f(f"L3_gnn_a{n}d")], axis=1)
                                             for n in (1, 2, 3)])),
        "b3": np.stack([f(f"L3_gnn_b{n}")[None] for n in (1, 2, 3)]),
    }


def kernel(**inputs):
    import concourse.bacc as bacc
    from concourse.bass_utils import run_bass_kernel_spmd

    nc = bacc.Bacc("TRN2", target_bir_lowering=False, num_devices=1)
    arrays = laid_out(inputs)
    args = [nc.dram_tensor(f"in_{n}", arrays[n].shape, mybir.dt.from_np(arrays[n].dtype),
                           kind="ExternalInput").ap() for n in _INS]
    out = nc.dram_tensor("out", (N, F), mybir.dt.float32, kind="ExternalOutput").ap()
    gnn_kernel(nc, *args, out)
    r = run_bass_kernel_spmd(nc, [{f"in_{n}": arrays[n] for n in _INS}], core_ids=[0])
    return r.results[0]["out"]
```
